# Optimizing a Trainium2 kernel written in Bass

```python
import numpy as np
import jax
import jax.numpy as jnp

def _softmax(x, axis=-1):
    return jax.nn.softmax(x, axis=axis)

def _gelu(x):
    return jax.nn.gelu(x, approximate=True)

def _silu(x):
    return jax.nn.silu(x)

def _sigmoid(x):
    return jax.nn.sigmoid(x)

def _layernorm(x, axis=-1, eps=1e-05):
    m = jnp.mean(x, axis=axis, keepdims=True)
    v = jnp.var(x, axis=axis, keepdims=True)
    return (x - m) / jnp.sqrt(v + eps)

def _scatter_add(tgt, idx, src, axis=0):
    return tgt.at[idx].add(src)

def _segment_sum(src, seg, n):
    return jax.ops.segment_sum(src, seg, n)
kernel_name = 'mk_perceiver_d2_seqx_r2_daa42f'

def setup_inputs(seed: int=0):
    np.random.seed(seed)
    _w = jnp.asarray

    def _rec_inputs():
        import jax
        import jax.numpy as jnp
        _rk = jax.random.key(seed)
        x = 0.002226 + 0.9996 * jax.random.normal(jax.random.fold_in(_rk, 1), (8, 64, 512), jnp.float32)
        _lenS = 64 - jax.random.randint(jax.random.fold_in(_rk, 7), (8,), 0, max(1, 64 // 4) + 1, jnp.int32)
        _lenS2 = 512 - jax.random.randint(jax.random.fold_in(_rk, 8), (8,), 0, max(1, 512 // 4) + 1, jnp.int32)
        _ctx_1024P = jax.random.normal(jax.random.fold_in(_rk, 11), (8, 16, 512), jnp.float32)
        _ctx_1024c = jax.random.dirichlet(jax.random.fold_in(_rk, 511), 0.3 * jnp.ones((16,), jnp.float32), (8, 512))
        _ctx_1024t = jnp.einsum('bsk,bkd->bsd', _ctx_1024c, _ctx_1024P)
        _ctx_1024t = _ctx_1024t * jax.lax.rsqrt(jnp.mean(jnp.square(_ctx_1024t)) + 1e-12) * 0.953939
        ctx_1024 = -7.10856e-05 + 0.999911 * (_ctx_1024t + 0.3 * jax.random.normal(jax.random.fold_in(_rk, 611), (8, 512, 512), jnp.float32))
        return (x, ctx_1024)
    x, ctx_1024 = _rec_inputs()

    def _L0_xattn_setup():
        import jax, jax.numpy as jnp
        import numpy as np
        DIM = 512
        HEAD_DIM = 64
        NUM_HEADS = 8
        INNER = HEAD_DIM * NUM_HEADS
        ROT_DIM = HEAD_DIM
        ROPE_BASE = 10000.0
        EPS = 1e-05

        def layer_norm(x, g, b):
            mu = jnp.mean(x, axis=-1, keepdims=True)
            var = jnp.var(x, axis=-1, keepdims=True)
            return (x - mu) * jax.lax.rsqrt(var + EPS) * g + b

        def rope_rotate_k(k):
            n = k.shape[1]
            half = ROT_DIM // 2
            inv_freq = 1.0 / ROPE_BASE ** (jnp.arange(0, ROT_DIM, 2, dtype=jnp.float32) / ROT_DIM)
            theta = jnp.arange(n, dtype=jnp.float32)[:, None] * inv_freq[None, :]
            angles = jnp.concatenate([theta, theta], axis=-1)
            cos = jnp.cos(angles)[None, :, None, :].astype(k.dtype)
            sin = jnp.sin(angles)[None, :, None, :].astype(k.dtype)
            k_rope, k_pass = (k[..., :ROT_DIM], k[..., ROT_DIM:])
            neg_half = jnp.concatenate([-k_rope[..., half:], k_rope[..., :half]], axis=-1)
            k_rope = k_rope * cos + neg_half * sin
            return jnp.concatenate([k_rope, k_pass], axis=-1)
        key = jax.random.key(seed)
        ks = jax.random.split(key, 5)
        b, n, m = (8, 4096, 64)
        s = 1.0 / np.sqrt(DIM)
        return {'x': jax.random.normal(ks[0], (b, n, DIM), jnp.float32), 'latents': jax.random.normal(ks[1], (b, m, DIM), jnp.float32), 'gamma_x': jnp.ones((DIM,), jnp.float32), 'beta_x': jnp.zeros((DIM,), jnp.float32), 'gamma_l': jnp.ones((DIM,), jnp.float32), 'beta_l': jnp.zeros((DIM,), jnp.float32), 'Wq': jax.random.normal(ks[2], (DIM, INNER), jnp.float32) * s, 'Wkv': jax.random.normal(ks[3], (DIM, 2 * INNER), jnp.float32) * s, 'Wo': jax.random.normal(ks[4], (INNER, DIM), jnp.float32) * (1.0 / np.sqrt(INNER))}
    _L0_xattn_all = _L0_xattn_setup()
    _L0_xattn_in = {k: v for k, v in _L0_xattn_all.items() if k in ('gamma_x', 'beta_x', 'gamma_l', 'beta_l', 'Wq', 'Wkv', 'Wo')}
    del _L0_xattn_all

    def _L0_attn_setup():
        import jax, jax.numpy as jnp
        import numpy as np
        B, T, D_MODEL = (2, 256, 512)
        D_INNER, D_HEAD, D_CONV = (1024, 64, 4)
        N_HEADS, D_STATE = (32, 32)
        DT_MIN, DT_MAX, K_MAX, EPS = (0.0001, 0.1, 0.5, 1e-08)

        def _forward(x, W_in, dw_weight, dw_bias, W_bc, W_out, skip, A_log, dt_bias):
            Bsz, Tlen, D = x.shape
            DI, K = dw_weight.shape
            H, N = A_log.shape
            DH = DI // H
            proj = jnp.einsum('btd,od->bto', x, W_in)
            gate = proj[..., :DI]
            value_raw = proj[..., DI:2 * DI]
            params = proj[..., 2 * DI:].reshape(Bsz, Tlen, H, 2)
            xp = jnp.pad(value_raw, ((0, 0), (K - 1, 0), (0, 0)))
            conv = dw_bias + sum((xp[:, k:k + Tlen, :] * dw_weight[:, k] for k in range(K)))
            value = jax.nn.silu(conv)
            dt = jnp.clip(jax.nn.softplus(params[..., 0] + dt_bias), DT_MIN, DT_MAX)
            kd = K_MAX * jax.nn.sigmoid(params[..., 1])
            A = jnp.exp(A_log)
            bc = jnp.einsum('bti,oi->bto', value, W_bc).reshape(Bsz, Tlen, H, 4, N)
            bc = bc / (jnp.sqrt(jnp.sum(bc * bc, axis=-1, keepdims=True)) + EPS)
            Bz, Bx, Cz, Cx = (bc[..., 0, :], bc[..., 1, :], bc[..., 2, :], bc[..., 3, :])
            u = value.reshape(Bsz, Tlen, H, DH)

            def step(carry, inp):
                z, s = carry
                u_t, dt_t, k_t, Bz_t, Bx_t, Cz_t, Cx_t = inp
                dtE = dt_t[:, :, None, None]
                S = 1.0 / (1.0 + dt_t[..., None] * k_t[..., None] + (dt_t * dt_t)[..., None] * A)
                z = S[..., None] * (z - dtE * A[None, :, :, None] * s + dtE * (Bz_t[..., None] * u_t[:, :, None, :]))
                s = s + dtE * z + dtE * (Bx_t[..., None] * u_t[:, :, None, :])
                y = jnp.einsum('bhn,bhnd->bhd', Cz_t, z) + jnp.einsum('bhn,bhnd->bhd', Cx_t, s)
                return ((z, s), y)
            tm = lambda a: jnp.moveaxis(a, 1, 0)
            init = (jnp.zeros((Bsz, H, N, DH), x.dtype), jnp.zeros((Bsz, H, N, DH), x.dtype))
            _, ys = jax.lax.scan(step, init, (tm(u), tm(dt), tm(kd), tm(Bz), tm(Bx), tm(Cz), tm(Cx)))
            y = jnp.moveaxis(ys, 0, 1).reshape(Bsz, Tlen, DI)
            y = (y + skip * value) * jax.nn.silu(gate)
            return jnp.einsum('bti,oi->bto', y, W_out)
        key = jax.random.key(seed)
        ks = jax.random.split(key, 8)
        n = lambda k, sh, s=1.0: jax.random.normal(k, sh, jnp.float32) * s
        return {'x': n(ks[0], (B, T, D_MODEL)), 'W_in': n(ks[1], (2 * D_INNER + N_HEADS * 2, D_MODEL), D_MODEL ** (-0.5)), 'dw_weight': n(ks[2], (D_INNER, D_CONV), D_CONV ** (-0.5)), 'dw_bias': n(ks[3], (D_INNER,), 0.1), 'W_bc': n(ks[4], (N_HEADS * 4 * D_STATE, D_INNER), D_INNER ** (-0.5)), 'W_out': n(ks[5], (D_MODEL, D_INNER), D_INNER ** (-0.5)), 'skip': jnp.ones((D_INNER,), jnp.float32), 'A_log': n(ks[6], (N_HEADS, D_STATE), 0.5), 'dt_bias': n(ks[7], (N_HEADS,), 0.5)}
    _L0_attn_all = _L0_attn_setup()
    _L0_attn_in = {k: v for k, v in _L0_attn_all.items() if k in ('W_in', 'dw_weight', 'dw_bias', 'W_bc', 'W_out', 'skip', 'A_log', 'dt_bias')}
    del _L0_attn_all

    def _L0_ffn_setup():
        import jax, jax.numpy as jnp
        import numpy as np
        B, S, D_MODEL, D_HIDDEN = (4, 1024, 512, 2048)

        def act_quant(x):
            scale = 127.0 / jnp.clip(jnp.max(jnp.abs(x), axis=-1, keepdims=True), 1e-05)
            return jnp.clip(jnp.round(x * scale), -128, 127) / scale

        def weight_quant(w):
            scale = 1.0 / jnp.clip(jnp.mean(jnp.abs(w)), 1e-05)
            return jnp.clip(jnp.round(w * scale), -1, 1) / scale

        def bit_linear(x, w):
            xq = x + jax.lax.stop_gradient(act_quant(x) - x)
            wq = w + jax.lax.stop_gradient(weight_quant(w) - w)
            return jnp.einsum('bsd,hd->bsh', xq, wq)

        def depthwise_conv1d(x_bcl, w, b):
            y = jax.lax.conv_general_dilated(x_bcl, w, window_strides=(1,), padding=[(1, 1)], dimension_numbers=('NCH', 'OIH', 'NCH'), feature_group_count=x_bcl.shape[1])
            return y + b[None, :, None]
        key = jax.random.key(seed)
        ks = jax.random.split(key, 5)
        lim1 = 1.0 / np.sqrt(D_MODEL)
        lim2 = 1.0 / np.sqrt(D_HIDDEN)
        limc = 1.0 / np.sqrt(3.0)
        return {'x': jax.random.normal(ks[0], (B, S, D_MODEL), dtype=jnp.float32), 'w1': jax.random.uniform(ks[1], (D_HIDDEN, D_MODEL), jnp.float32, -lim1, lim1), 'conv_w': jax.random.uniform(ks[2], (D_HIDDEN, 1, 3), jnp.float32, -limc, limc), 'conv_b': jax.random.uniform(ks[3], (D_HIDDEN,), jnp.float32, -limc, limc), 'w2': jax.random.uniform(ks[4], (D_MODEL, D_HIDDEN), jnp.float32, -lim2, lim2)}
    _L0_ffn_all = _L0_ffn_setup()
    _L0_ffn_in = {k: v for k, v in _L0_ffn_all.items() if k in ('w1', 'conv_w', 'conv_b', 'w2')}
    del _L0_ffn_all

    def _L1_xattn_setup():
        import jax, jax.numpy as jnp
        import numpy as np
        HIDDEN = 512
        NUM_HEADS = 16
        HEAD_DIM = HIDDEN // NUM_HEADS
        key = jax.random.key(seed)
        k1, k2, k3, k4, k5, k6 = jax.random.split(key, 6)
        B, SQ, SKV = (4, 512, 1024)
        s = HIDDEN ** (-0.5)
        return {'xq': jax.random.normal(k1, (B, SQ, HIDDEN), jnp.float32), 'xkv': jax.random.normal(k2, (B, SKV, HIDDEN), jnp.float32), 'Wq': jax.random.normal(k3, (HIDDEN, HIDDEN), jnp.float32) * s, 'Wkv': jax.random.normal(k4, (2 * HIDDEN, HIDDEN), jnp.float32) * s, 'Wout': jax.random.normal(k5, (HIDDEN, HIDDEN), jnp.float32) * s, 'bout': jax.random.normal(k6, (HIDDEN,), jnp.float32) * 0.01}
    _L1_xattn_all = _L1_xattn_setup()
    _L1_xattn_in = {k: v for k, v in _L1_xattn_all.items() if k in ('Wq', 'Wkv', 'Wout', 'bout')}
    del _L1_xattn_all

    def _L1_attn_setup():
        import jax, jax.numpy as jnp
        import numpy as np
        EMBED_DIM = 512
        NUM_HEADS = 16
        HEAD_DIM = EMBED_DIM // NUM_HEADS
        KERNEL_SIZE = 64
        B, L = (2, 1024)
        key = jax.random.key(seed)
        ks = jax.random.split(key, 6)
        x = jax.random.normal(ks[0], (B, L, EMBED_DIM), dtype=jnp.float32)
        qkv_w = jax.random.normal(ks[1], (EMBED_DIM, 3 * EMBED_DIM), dtype=jnp.float32) / np.sqrt(EMBED_DIM)
        qkv_b = jnp.zeros((3 * EMBED_DIM,), dtype=jnp.float32)
        out_w = jax.random.normal(ks[2], (EMBED_DIM, EMBED_DIM), dtype=jnp.float32) / np.sqrt(EMBED_DIM)
        out_b = jnp.zeros((EMBED_DIM,), dtype=jnp.float32)
        proj = jax.random.normal(ks[3], (NUM_HEADS, HEAD_DIM, KERNEL_SIZE), dtype=jnp.float32) / np.sqrt(HEAD_DIM)
        return {'x': x, 'qkv_w': qkv_w, 'qkv_b': qkv_b, 'out_w': out_w, 'out_b': out_b, 'proj': proj}
    _L1_attn_all = _L1_attn_setup()
    _L1_attn_in = {k: v for k, v in _L1_attn_all.items() if k in ('qkv_w', 'qkv_b', 'out_w', 'out_b', 'proj')}
    del _L1_attn_all

    def _L1_ffn_setup():
        import jax, jax.numpy as jnp
        import numpy as np
        ALPHA = 1.702
        LIMIT = 9.0
        TOP_K = 2

        def swiglu(x):
            g, v = (x[..., 0::2], x[..., 1::2])
            g = jnp.clip(g, None, LIMIT)
            v = jnp.clip(v, -LIMIT, LIMIT)
            return g * jax.nn.sigmoid(ALPHA * g) * (v + 1)
        key = jax.random.key(seed)
        ks = jax.random.split(key, 6)
        B, L, D = (2, 1024, 512)
        E, F = (8, 1024)
        s_gate = 1.0 / np.sqrt(D)
        s1 = 1.0 / np.sqrt(D)
        s2 = 1.0 / np.sqrt(F)
        return {'x': jax.random.normal(ks[0], (B, L, D), dtype=jnp.float32), 'gate_w': jax.random.normal(ks[1], (D, E), dtype=jnp.float32) * s_gate, 'dense_1_w': jax.random.normal(ks[2], (E, 2 * F, D), dtype=jnp.float32) * s1, 'dense_1_b': jnp.zeros((E, 2 * F), dtype=jnp.float32), 'dense_2_w': jax.random.normal(ks[3], (E, D, F), dtype=jnp.float32) * s2, 'dense_2_b': jnp.zeros((E, D), dtype=jnp.float32)}
    _L1_ffn_all = _L1_ffn_setup()
    _L1_ffn_in = {k: v for k, v in _L1_ffn_all.items() if k in ('gate_w', 'dense_1_w', 'dense_1_b', 'dense_2_w', 'dense_2_b')}
    del _L1_ffn_all
    return {'x': x, 'ctx_1024': ctx_1024, 'L0_xattn_gamma_x': _L0_xattn_in['gamma_x'], 'L0_xattn_beta_x': _L0_xattn_in['beta_x'], 'L0_xattn_gamma_l': _L0_xattn_in['gamma_l'], 'L0_xattn_beta_l': _L0_xattn_in['beta_l'], 'L0_xattn_Wq': _L0_xattn_in['Wq'], 'L0_xattn_Wkv': _L0_xattn_in['Wkv'], 'L0_xattn_Wo': _L0_xattn_in['Wo'], 'L0_attn_W_in': _L0_attn_in['W_in'], 'L0_attn_dw_weight': _L0_attn_in['dw_weight'], 'L0_attn_dw_bias': _L0_attn_in['dw_bias'], 'L0_attn_W_bc': _L0_attn_in['W_bc'], 'L0_attn_W_out': _L0_attn_in['W_out'], 'L0_attn_skip': _L0_attn_in['skip'], 'L0_attn_A_log': _L0_attn_in['A_log'], 'L0_attn_dt_bias': _L0_attn_in['dt_bias'], 'L0_ffn_w1': _L0_ffn_in['w1'], 'L0_ffn_conv_w': _L0_ffn_in['conv_w'], 'L0_ffn_conv_b': _L0_ffn_in['conv_b'], 'L0_ffn_w2': _L0_ffn_in['w2'], 'L1_xattn_Wq': _L1_xattn_in['Wq'], 'L1_xattn_Wkv': _L1_xattn_in['Wkv'], 'L1_xattn_Wout': _L1_xattn_in['Wout'], 'L1_xattn_bout': _L1_xattn_in['bout'], 'L1_attn_qkv_w': _L1_attn_in['qkv_w'], 'L1_attn_qkv_b': _L1_attn_in['qkv_b'], 'L1_attn_out_w': _L1_attn_in['out_w'], 'L1_attn_out_b': _L1_attn_in['out_b'], 'L1_attn_proj': _L1_attn_in['proj'], 'L1_ffn_gate_w': _L1_ffn_in['gate_w'], 'L1_ffn_dense_1_w': _L1_ffn_in['dense_1_w'], 'L1_ffn_dense_1_b': _L1_ffn_in['dense_1_b'], 'L1_ffn_dense_2_w': _L1_ffn_in['dense_2_w'], 'L1_ffn_dense_2_b': _L1_ffn_in['dense_2_b']}

def reference(x, ctx_1024, L0_xattn_gamma_x, L0_xattn_beta_x, L0_xattn_gamma_l, L0_xattn_beta_l, L0_xattn_Wq, L0_xattn_Wkv, L0_xattn_Wo, L0_attn_W_in, L0_attn_dw_weight, L0_attn_dw_bias, L0_attn_W_bc, L0_attn_W_out, L0_attn_skip, L0_attn_A_log, L0_attn_dt_bias, L0_ffn_w1, L0_ffn_conv_w, L0_ffn_conv_b, L0_ffn_w2, L1_xattn_Wq, L1_xattn_Wkv, L1_xattn_Wout, L1_xattn_bout, L1_attn_qkv_w, L1_attn_qkv_b, L1_attn_out_w, L1_attn_out_b, L1_attn_proj, L1_ffn_gate_w, L1_ffn_dense_1_w, L1_ffn_dense_1_b, L1_ffn_dense_2_w, L1_ffn_dense_2_b):
    import jax
    import jax.numpy as jnp

    def _L0_xattn_ref(x, latents, gamma_x, beta_x, gamma_l, beta_l, Wq, Wkv, Wo):
        import jax, jax.numpy as jnp
        import numpy as np
        DIM = 512
        HEAD_DIM = 64
        NUM_HEADS = 8
        INNER = HEAD_DIM * NUM_HEADS
        ROT_DIM = HEAD_DIM
        ROPE_BASE = 10000.0
        EPS = 1e-05

        def layer_norm(x, g, b):
            mu = jnp.mean(x, axis=-1, keepdims=True)
            var = jnp.var(x, axis=-1, keepdims=True)
            return (x - mu) * jax.lax.rsqrt(var + EPS) * g + b

        def rope_rotate_k(k):
            n = k.shape[1]
            half = ROT_DIM // 2
            inv_freq = 1.0 / ROPE_BASE ** (jnp.arange(0, ROT_DIM, 2, dtype=jnp.float32) / ROT_DIM)
            theta = jnp.arange(n, dtype=jnp.float32)[:, None] * inv_freq[None, :]
            angles = jnp.concatenate([theta, theta], axis=-1)
            cos = jnp.cos(angles)[None, :, None, :].astype(k.dtype)
            sin = jnp.sin(angles)[None, :, None, :].astype(k.dtype)
            k_rope, k_pass = (k[..., :ROT_DIM], k[..., ROT_DIM:])
            neg_half = jnp.concatenate([-k_rope[..., half:], k_rope[..., :half]], axis=-1)
            k_rope = k_rope * cos + neg_half * sin
            return jnp.concatenate([k_rope, k_pass], axis=-1)
        b, n, _ = x.shape
        m = latents.shape[1]
        h, d = (NUM_HEADS, HEAD_DIM)
        scale = d ** (-0.5)
        xn = layer_norm(x, gamma_x, beta_x)
        ln = layer_norm(latents, gamma_l, beta_l)
        q = (ln @ Wq).reshape(b, m, h, d)
        kv_x = xn @ Wkv
        k_x, v_x = (kv_x[..., :INNER], kv_x[..., INNER:])
        kv_l = ln @ Wkv
        k_l, v_l = (kv_l[..., :INNER], kv_l[..., INNER:])
        k_x = k_x.reshape(b, n, h, d)
        v_x = v_x.reshape(b, n, h, d)
        k_x = rope_rotate_k(k_x)
        q = jnp.transpose(q, (0, 2, 1, 3)) * scale
        k_x = jnp.transpose(k_x, (0, 2, 1, 3))
        v_x = jnp.transpose(v_x, (0, 2, 1, 3))
        k_l = jnp.transpose(k_l.reshape(b, m, h, d), (0, 2, 1, 3))
        v_l = jnp.transpose(v_l.reshape(b, m, h, d), (0, 2, 1, 3))
        k = jnp.concatenate([k_x, k_l], axis=2)
        v = jnp.concatenate([v_x, v_l], axis=2)
        sim = jnp.einsum('bhid,bhjd->bhij', q, k)
        attn = jax.nn.softmax(sim, axis=-1)
        out = jnp.einsum('bhij,bhjd->bhid', attn, v)
        out = jnp.transpose(out, (0, 2, 1, 3)).reshape(b, m, INNER)
        return out @ Wo

    def _L0_attn_ref(x, W_in, dw_weight, dw_bias, W_bc, W_out, skip, A_log, dt_bias):
        import jax, jax.numpy as jnp
        import numpy as np
        B, T, D_MODEL = (2, 256, 512)
        D_INNER, D_HEAD, D_CONV = (1024, 64, 4)
        N_HEADS, D_STATE = (32, 32)
        DT_MIN, DT_MAX, K_MAX, EPS = (0.0001, 0.1, 0.5, 1e-08)

        def _forward(x, W_in, dw_weight, dw_bias, W_bc, W_out, skip, A_log, dt_bias):
            Bsz, Tlen, D = x.shape
            DI, K = dw_weight.shape
            H, N = A_log.shape
            DH = DI // H
            proj = jnp.einsum('btd,od->bto', x, W_in)
            gate = proj[..., :DI]
            value_raw = proj[..., DI:2 * DI]
            params = proj[..., 2 * DI:].reshape(Bsz, Tlen, H, 2)
            xp = jnp.pad(value_raw, ((0, 0), (K - 1, 0), (0, 0)))
            conv = dw_bias + sum((xp[:, k:k + Tlen, :] * dw_weight[:, k] for k in range(K)))
            value = jax.nn.silu(conv)
            dt = jnp.clip(jax.nn.softplus(params[..., 0] + dt_bias), DT_MIN, DT_MAX)
            kd = K_MAX * jax.nn.sigmoid(params[..., 1])
            A = jnp.exp(A_log)
            bc = jnp.einsum('bti,oi->bto', value, W_bc).reshape(Bsz, Tlen, H, 4, N)
            bc = bc / (jnp.sqrt(jnp.sum(bc * bc, axis=-1, keepdims=True)) + EPS)
            Bz, Bx, Cz, Cx = (bc[..., 0, :], bc[..., 1, :], bc[..., 2, :], bc[..., 3, :])
            u = value.reshape(Bsz, Tlen, H, DH)

            def step(carry, inp):
                z, s = carry
                u_t, dt_t, k_t, Bz_t, Bx_t, Cz_t, Cx_t = inp
                dtE = dt_t[:, :, None, None]
                S = 1.0 / (1.0 + dt_t[..., None] * k_t[..., None] + (dt_t * dt_t)[..., None] * A)
                z = S[..., None] * (z - dtE * A[None, :, :, None] * s + dtE * (Bz_t[..., None] * u_t[:, :, None, :]))
                s = s + dtE * z + dtE * (Bx_t[..., None] * u_t[:, :, None, :])
                y = jnp.einsum('bhn,bhnd->bhd', Cz_t, z) + jnp.einsum('bhn,bhnd->bhd', Cx_t, s)
                return ((z, s), y)
            tm = lambda a: jnp.moveaxis(a, 1, 0)
            init = (jnp.zeros((Bsz, H, N, DH), x.dtype), jnp.zeros((Bsz, H, N, DH), x.dtype))
            _, ys = jax.lax.scan(step, init, (tm(u), tm(dt), tm(kd), tm(Bz), tm(Bx), tm(Cz), tm(Cx)))
            y = jnp.moveaxis(ys, 0, 1).reshape(Bsz, Tlen, DI)
            y = (y + skip * value) * jax.nn.silu(gate)
            return jnp.einsum('bti,oi->bto', y, W_out)
        return _forward(x, W_in, dw_weight, dw_bias, W_bc, W_out, skip, A_log, dt_bias)

    def _L0_ffn_ref(x, w1, conv_w, conv_b, w2):
        import jax, jax.numpy as jnp
        import numpy as np
        B, S, D_MODEL, D_HIDDEN = (4, 1024, 512, 2048)

        def act_quant(x):
            scale = 127.0 / jnp.clip(jnp.max(jnp.abs(x), axis=-1, keepdims=True), 1e-05)
            return jnp.clip(jnp.round(x * scale), -128, 127) / scale

        def weight_quant(w):
            scale = 1.0 / jnp.clip(jnp.mean(jnp.abs(w)), 1e-05)
            return jnp.clip(jnp.round(w * scale), -1, 1) / scale

        def bit_linear(x, w):
            xq = x + jax.lax.stop_gradient(act_quant(x) - x)
            wq = w + jax.lax.stop_gradient(weight_quant(w) - w)
            return jnp.einsum('bsd,hd->bsh', xq, wq)

        def depthwise_conv1d(x_bcl, w, b):
            y = jax.lax.conv_general_dilated(x_bcl, w, window_strides=(1,), padding=[(1, 1)], dimension_numbers=('NCH', 'OIH', 'NCH'), feature_group_count=x_bcl.shape[1])
            return y + b[None, :, None]
        h = bit_linear(x, w1)
        h = depthwise_conv1d(h.transpose(0, 2, 1), conv_w, conv_b)
        h = h.transpose(0, 2, 1)
        h = jax.nn.silu(h)
        return bit_linear(h, w2)

    def _L1_xattn_ref(xq, xkv, Wq, Wkv, Wout, bout):
        import jax, jax.numpy as jnp
        import numpy as np
        HIDDEN = 512
        NUM_HEADS = 16
        HEAD_DIM = HIDDEN // NUM_HEADS
        B, SQ, H = xq.shape
        SKV = xkv.shape[1]
        scale = HEAD_DIM ** (-0.5)
        q = (xq @ Wq.T).reshape(B, SQ, NUM_HEADS, HEAD_DIM)
        kv = (xkv @ Wkv.T).reshape(B, SKV, 2, NUM_HEADS, HEAD_DIM)
        k, v = (kv[:, :, 0], kv[:, :, 1])
        att = jax.nn.softmax(jnp.einsum('bxhd,byhd->bhxy', q, k) * scale, axis=-1)
        x = jnp.einsum('bhxy,byhd->bxhd', att, v).reshape(B, SQ, H)
        return x @ Wout.T + bout

    def _L1_attn_ref(x, qkv_w, qkv_b, out_w, out_b, proj):
        import jax, jax.numpy as jnp
        import numpy as np
        EMBED_DIM = 512
        NUM_HEADS = 16
        HEAD_DIM = EMBED_DIM // NUM_HEADS
        KERNEL_SIZE = 64
        B, L = (2, 1024)
        Bn, Ln, E = x.shape
        H, D, M = proj.shape
        qkv = x @ qkv_w + qkv_b
        q, k, v = jnp.split(qkv, 3, axis=-1)
        q = q.reshape(Bn, Ln, H, D).transpose(0, 2, 1, 3)
        k = k.reshape(Bn, Ln, H, D).transpose(0, 2, 1, 3)
        v = v.reshape(Bn, Ln, H, D).transpose(0, 2, 1, 3)
        q_prime = jax.nn.relu(jnp.einsum('bhld,hdm->bhlm', q, proj))
        k_prime = jax.nn.relu(jnp.einsum('bhld,hdm->bhlm', k, proj))
        kv_prod = jnp.einsum('bhlm,bhld->bhlmd', k_prime, v)
        kv_cumsum = jnp.cumsum(kv_prod, axis=2)
        context = jnp.einsum('bhlm,bhlmd->bhld', q_prime, kv_cumsum)
        k_cumsum = jnp.cumsum(k_prime, axis=2)
        norm = jnp.einsum('bhlm,bhlm->bhl', q_prime, k_cumsum)
        out = context / (norm[..., None] + 1e-06)
        out = out.transpose(0, 2, 1, 3).reshape(Bn, Ln, E)
        return out @ out_w + out_b

    def _L1_ffn_ref(x, gate_w, dense_1_w, dense_1_b, dense_2_w, dense_2_b):
        import jax, jax.numpy as jnp
        import numpy as np
        ALPHA = 1.702
        LIMIT = 9.0
        TOP_K = 2

        def swiglu(x):
            g, v = (x[..., 0::2], x[..., 1::2])
            g = jnp.clip(g, None, LIMIT)
            v = jnp.clip(v, -LIMIT, LIMIT)
            return g * jax.nn.sigmoid(ALPHA * g) * (v + 1)
        B, L, D = x.shape
        xf = x.reshape(B * L, D)
        gate = xf @ gate_w
        weights, sel = jax.lax.top_k(gate, k=TOP_K)
        weights = jax.nn.softmax(weights, axis=-1)
        h = jnp.einsum('ecd,td->tec', dense_1_w, xf) + dense_1_b[None]
        h = swiglu(h)
        y = jnp.einsum('edf,tef->ted', dense_2_w, h) + dense_2_b[None]
        y_sel = jnp.take_along_axis(y, sel[:, :, None], axis=1)
        out = jnp.einsum('tkd,tk->td', y_sel, weights)
        return out.reshape(B, L, D)
    x = x + _L0_xattn_ref(ctx_1024, _layernorm(x, axis=-1), L0_xattn_gamma_x, L0_xattn_beta_x, L0_xattn_gamma_l, L0_xattn_beta_l, L0_xattn_Wq, L0_xattn_Wkv, L0_xattn_Wo)
    x = x + _L0_attn_ref(_layernorm(x, axis=-1), L0_attn_W_in, L0_attn_dw_weight, L0_attn_dw_bias, L0_attn_W_bc, L0_attn_W_out, L0_attn_skip, L0_attn_A_log, L0_attn_dt_bias)
    x = x + _L0_ffn_ref(_layernorm(x, axis=-1), L0_ffn_w1, L0_ffn_conv_w, L0_ffn_conv_b, L0_ffn_w2)
    x = x + _L1_xattn_ref(_layernorm(x, axis=-1), ctx_1024, L1_xattn_Wq, L1_xattn_Wkv, L1_xattn_Wout, L1_xattn_bout)
    x = x + _L1_attn_ref(_layernorm(x, axis=-1), L1_attn_qkv_w, L1_attn_qkv_b, L1_attn_out_w, L1_attn_out_b, L1_attn_proj)
    x = x + _L1_ffn_ref(_layernorm(x, axis=-1), L1_ffn_gate_w, L1_ffn_dense_1_w, L1_ffn_dense_1_b, L1_ffn_dense_2_w, L1_ffn_dense_2_b)
    return x

_drawn_inputs = setup_inputs


def setup_inputs(seed=0):
    import zlib

    import numpy as np

    out = dict(_drawn_inputs(seed))
    spreads = {'L0_xattn_gamma_x': (1.0, 0.2),
     'L0_xattn_beta_x': (0.0, 0.1),
     'L0_xattn_gamma_l': (1.0, 0.2),
     'L0_xattn_beta_l': (0.0, 0.1),
     'L0_attn_skip': (1.0, 0.2),
     'L1_attn_qkv_b': (0.0, 0.1),
     'L1_attn_out_b': (0.0, 0.1),
     'L1_ffn_dense_1_b': (0.0, 0.1),
     'L1_ffn_dense_2_b': (0.0, 0.1)}
    factors = {'L0_attn_dt_bias': 8.0}
    for name, (base, spread) in spreads.items():
        noise = np.random.default_rng([zlib.crc32(name.encode()), seed]).standard_normal(out[name].shape)
        drawn = base * np.exp(spread * noise) if base else spread * noise
        out[name] = jnp.asarray(drawn.astype(out[name].dtype))
    for name, factor in factors.items():
        out[name] = (out[name] * factor).astype(out[name].dtype)
    return out
```

```python
from contextlib import ExitStack

import concourse.bass as bass
from concourse import mybir
import numpy as np

P = 128
T = 512
D = 512
B = 8
L = 64
KEYS = 512
KC = D // P
TT = T // P
EPS = 1e-5
MAGIC = 12582912.0

F32 = mybir.dt.float32
F32R = mybir.dt.float32r
BF16 = mybir.dt.bfloat16
ALU = mybir.AluOpType
ACT = mybir.ActivationFunctionType
AX = mybir.AxisListType

STAGE_BLOCKS = {"latent_attention": 4, "oscillator": 22, "bit_ffn": 0, "context_attention": 4,
                "linear_attention": 4, "experts": 48}
RING_UNITS = 8


class Steps:

    def __init__(self, eng, sem):
        self.eng, self.sem, self.base, self.n = eng, sem, 0, 0

    def mark(self, ins):
        ins.then_inc(self.sem, 1)
        self.n += 1

    def wait(self):
        self.eng.wait_ge(self.sem, self.base + self.n)

    def done(self, ins):
        self.mark(ins)
        self.wait()

    def enter(self, i, per_trip):
        self.before, self.per_trip = self.base + self.n, per_trip
        self.base, self.n = self.before + i * per_trip, 0

    def leave(self, trips):
        assert self.n == self.per_trip, f"{self.n} steps a trip"
        self.base, self.n = self.before + trips * self.per_trip, 0


def product(pe, out, lhs, rhs, start, stop):
    (lh, ll), (rh, rl) = lhs, rhs
    pe.matmul(out, lh, rh, start=start, stop=False)
    pe.matmul(out, lh, rl, start=False, stop=False)
    return pe.matmul(out, ll, rh, start=False, stop=stop)


def f32(ap):
    return ap.bitcast(F32)


def row_stats(dve, steps, rows, stats, mean_var, var_eps):
    for t in range(TT):
        steps.mark(dve.bn_stats(stats[:, t, :], rows[:, t, :]))
    steps.wait()
    mean, half_gap = mean_var[:, :, 0], mean_var[:, :, 1]
    steps.mark(dve.tensor_tensor(mean, stats[:, :, 1], stats[:, :, 4], ALU.add))
    steps.mark(dve.tensor_tensor(half_gap, stats[:, :, 1], stats[:, :, 4], ALU.subtract))
    steps.mark(dve.tensor_tensor(var_eps, stats[:, :, 2], stats[:, :, 5], ALU.add))
    steps.wait()
    steps.mark(dve.tensor_scalar(mean, mean, 0.5, None, ALU.mult))
    steps.mark(dve.tensor_tensor(half_gap, half_gap, half_gap, ALU.mult))
    steps.mark(dve.tensor_scalar(var_eps, var_eps, 1.0 / D, EPS, ALU.mult, ALU.add))
    steps.wait()
    return dve.scalar_tensor_tensor(var_eps, half_gap, 0.25, var_eps, ALU.mult, ALU.add)


def guess_rstd(act, steps, var_eps, rstd):
    steps.done(act.activation(rstd, var_eps, ACT.Ln))
    return act.activation(rstd, rstd, ACT.Exp, scale=-0.5)


def refine_rstd(dve, steps, var_eps, rstd, tmp):
    steps.done(dve.tensor_tensor(tmp, rstd, rstd, ALU.mult))
    steps.done(dve.tensor_tensor(tmp, tmp, var_eps, ALU.mult))
    steps.done(dve.tensor_scalar(tmp, tmp, -0.5, 1.5, ALU.mult, ALU.add))
    steps.done(dve.tensor_tensor(rstd, rstd, tmp, ALU.mult))


def normalize_rows(dve, out, rows, mean_var, rstd):
    for t in range(TT):
        last = dve.tensor_scalar(out[:, t, :], rows[:, t, :], mean_var[:, t, 0:1], rstd[:, t:t + 1],
                                 ALU.subtract, ALU.mult)
    return last


class NormalizedColumns:

    def __init__(self, m, k, rows, small, high, low, bank):
        self.m, self.k, self.rows, self.high, self.low, self.bank = m, k, rows, high, low, bank
        self.stats = small[:, 0:24].rearrange("p (t n) -> p t n", n=6)
        self.mv = small[:, 24:32].rearrange("p (t n) -> p t n", n=2)
        self.ve, self.rstd, self.tmp = small[:, 32:36], small[:, 36:40], small[:, 40:44]
        (self.stats_ready, self.uses), (self.guessed, _), (self.rows_ready, _) = (
            m.shared("norm_" + n, 1) for n in ("stats", "guess", "rows"))
        (self.turned, self.chunks), (self.high_ready, _), (self.split, _) = (
            m.shared("norm_" + n, KC) for n in ("turned", "high", "split"))

    def wait_rows(self, eng):
        eng.wait_ge(self.rows_ready, self.uses + 1)

    def wait_split(self, eng, chunks):
        eng.wait_ge(self.split, self.chunks + chunks)

    def vector_rows(self, dve, steps):
        dve.wait_ge(self.m.x_loaded, 16)
        if self.k:
            dve.wait_ge(self.m.x_ready, TT * self.k)
        row_stats(dve, steps, self.m.x, self.stats, self.mv, self.ve).then_inc(self.stats_ready, 1)
        dve.wait_ge(self.guessed, self.uses + 1)
        refine_rstd(dve, steps, self.ve, self.rstd, self.tmp)
        normalize_rows(dve, self.rows, self.m.x, self.mv, self.rstd).then_inc(self.rows_ready, 1)

    def vector_low(self, dve):
        for c in range(KC):
            dve.wait_ge(self.high_ready, self.chunks + c + 1)
            dve.tensor_tensor(self.low[:, c, :], self.m.ps[:, self.bank + c, :], f32(self.high[:, c, :]), ALU.subtract)\
               .then_inc(self.split, 1)

    def scalar_guess(self, act, steps):
        act.wait_ge(self.stats_ready, self.uses + 1)
        guess_rstd(act, steps, self.ve, self.rstd).then_inc(self.guessed, 1)

    def scalar_high(self, act):
        for c in range(KC):
            act.wait_ge(self.turned, self.chunks + c + 1)
            act.copy(self.high[:, c, :], self.m.ps[:, self.bank + c, :]).then_inc(self.high_ready, 1)

    def tensor(self, pe):
        pe.wait_ge(self.m.consts, 16)
        self.wait_rows(pe)
        for c in range(KC):
            for t in range(TT):
                last = pe.transpose(self.m.ps[:, self.bank + c, t * P:(t + 1) * P], self.rows[:, t, c * P:(c + 1) * P],
                                    self.m.ident[:, :])
            last.then_inc(self.turned, 1)


def latent_attention(nc, m, first_unit, k):
    SCALE = 64 ** -0.5
    PAIRS = 4
    NK = KEYS + L
    with ExitStack() as mem:
        sb = lambda name, shape, dt=F32: mem.enter_context(nc.sbuf_tensor("la_" + name, shape, dt))
        ctx = sb("ctx", [P, 2, TT, D])
        xh, xl = sb("xh", [P, 2, KC, T], F32R), sb("xl", [P, 2, KC, T], F32R)
        y = sb("y", [P, 2, T])
        q = sb("q", [P, KC, B, L])
        q_pairs = sb("q_pairs", [P, 2, KC, 2, 2, L])
        kl = sb("kl", [P, KC, B, L])
        kl_batch = sb("kl_batch", [P, 2, KC, L])
        vl = sb("vl", [L, B, D])
        vl_batch = sb("vl_batch", [L, D])
        kt = sb("kt", [P, 2, KC, KEYS])
        v = sb("v", [P, 2, TT, D])
        cos, sin = sb("cos", [P, KEYS]), sb("sin", [P, KEYS])
        by_sin = sb("by_sin", [P, 2, KEYS])
        p = sb("p", [P, 2, NK])
        pt = sb("pt", [P, TT + 1, P])
        o = sb("o", [P, PAIRS, T])
        small = sb("small", [P, 72])
    gx, bx, gl, bl = (small[:, KC * n:KC * n + KC] for n in range(4))
    stats, mv = small[:, 16:40].rearrange("p (t n) -> p t n", n=6), small[:, 40:48].rearrange("p (t n) -> p t n", n=2)
    ve, rstd, tmp = small[:, 48:52], small[:, 52:56], small[:, 56:60]
    nmax, rsum, rinv = small[:, 60:62], small[:, 62:64], small[:, 64:66]
    oh, ol = xh[:, 0], xl[:, 0]
    x = m.x
    s = lambda name: m.sem("la_" + name)
    consts, loaded = m.shared("stage_consts", 6 * 16)
    x_loaded = m.x_loaded
    (ctx_loaded0, _), (ctx_loaded1, _) = (m.shared(f"ctx_loaded{n}", 16 * B // 2) for n in range(2))
    ctx_loaded = (ctx_loaded0, ctx_loaded1)
    ctx_stats, ctx_guess, rows_ready = s("ctx_stats"), s("ctx_guess"), s("rows_ready")
    lat_stats, lat_guess, lat_rows = s("lat_stats"), s("lat_guess"), s("lat_rows")
    q_zero, staged = s("q_zero"), s("staged")
    lat_done, lat_out = s("lat_done"), s("lat_out")
    xt_done, y_ready, x_split = s("xt_done"), s("y_ready"), s("x_split")
    (lin_done, _), (v_ready, _) = m.shared("lin_done", 8 * B), m.shared("v_ready", 4 * B)
    rotated = s("rotated")
    (scores, _), (nmax_ready, _), (exp_done, _), (p_ready, _), (pt_done, _), (pt_ready, _), (pv_done, _), (o_ready, _) = (
        m.shared(n, PAIRS * B) for n in ("scores", "nmax_ready", "exp_done", "p_ready", "pt_done", "pt_ready", "pv_done", "o_ready"))
    (o_high, halves), (o_split, _) = m.shared("out_high", 4), m.shared("out_split", 4)
    out_done, outs = m.shared("out_done", TT - 1)
    XT, LIN, SC, PTB = 0, 1, 5, 7
    ps = m.ps
    sc_all = ps[:, SC:SC + 2, :].rearrange("p a n -> p (a n)")[:, 0:NK]
    pt5 = ps[0:L, SC + 1, 128:256]
    pv = ps[:, SC + 1, 256:384]
    CHUNK = [0, 2, 1, 3]

    def lhs(h, n, c):
        return h[:, n % RING_UNITS, c * P:(c + 1) * P]

    def tensor(pe):
        def transposes(b, par, c):
            for t in range(TT):
                last = pe.transpose(ps[:, XT, t * P:(t + 1) * P], ctx[:, par, t, c * P:(c + 1) * P], m.ident[:, :])
            last.then_inc(xt_done, 1)

        pe.wait_ge(m.consts, 16)
        pe.wait_ge(lat_rows, 1)
        for c in range(KC):
            if c:
                pe.wait_ge(y_ready, c)
            transposes(0, 1, c)
        for j in range(2):
            for n in range(KC):
                u = first_unit + 4 * j + n
                pe.wait_ge(m.unit_ready, u + 1)
                pe.wait_ge(x_split, KC)
                if j:
                    pe.wait_ge(lat_out, n + 1)
                for c in range(KC):
                    last = product(pe, ps[:, LIN + n, :], (lhs(m.wh, u, c), lhs(m.wl, u, c)),
                                   (xh[:, 1, c, :], xl[:, 1, c, :]), c == 0, c == KC - 1)
                last.then_inc(lat_done if j else m.unit_done, 1)
        for t in range(TT):
            pe.wait_ge(lat_out, KC + t + 1)
            for c in range(KC):
                u = first_unit + 8 + c
                pe.wait_ge(m.unit_ready, u + 1)
                last = product(pe, ps[:, LIN + t, :],
                               (xh[:, 1, c, t * P:(t + 1) * P], xl[:, 1, c, t * P:(t + 1) * P]),
                               (m.wh[:, u % RING_UNITS, :], m.wl[:, u % RING_UNITS, :]), c == 0, c == KC - 1)
            last.then_inc(lat_done, 1)

        def context_transposes(b, par, c):
            if c == 0:
                pe.wait_ge(rows_ready, b + 1)
            pe.wait_ge(y_ready, KC * (b + 1) + c)
            transposes(b, par, c)

        def linear(b, par, l, chunks=range(KC)):
            if l == 0:
                pe.wait_ge(x_split, KC * (b + 2))
            bank = ps[:, LIN + l % 4, :]
            if l < 4 and chunks[0] == 0 and not (isinstance(b, int) and b == 0):
                pe.wait_ge(v_ready, 4 * b + (l - 3))
            elif l >= 4 and chunks[0] == 0:
                pe.wait_ge(rotated, 2 * b + (1 if l < 6 else 2))
            for c in chunks:
                x_c = (xh[:, par, c, :], xl[:, par, c, :])
                if l < 4:
                    u = first_unit + 4 + CHUNK[l]
                    last = product(pe, bank, (lhs(m.wh, u, c), lhs(m.wl, u, c)), x_c, c == 0, c == KC - 1)
                else:
                    u = first_unit + 8 + c
                    t = slice((l - 4) * P, (l - 3) * P)
                    last = product(pe, bank, (x_c[0][:, t], x_c[1][:, t]),
                                   (m.wh[:, u % RING_UNITS, :], m.wl[:, u % RING_UNITS, :]), c == 0, c == KC - 1)
            if chunks[-1] == KC - 1:
                last.then_inc(lin_done, 1)

        def attention_scores(b, par, hp):
            if hp == 0:
                pe.wait_ge(rotated, 2 * b + 2)
                pe.wait_ge(staged, b + 1)
            pe.wait_ge(exp_done, 4 * b + hp)
            pe.wait_ge(o_ready, 4 * b + hp)
            for half in range(2):
                c = hp // 2 + 2 * half
                pe.matmul(sc_all[:, 0:KEYS], q_pairs[:, par, c, hp % 2, :, :].rearrange("p e l -> p (e l)"),
                          kt[:, par, c, :], start=half == 0, stop=half == 1)
            for half in range(2):
                c = hp // 2 + 2 * half
                last = pe.matmul(sc_all[:, KEYS:NK], q_pairs[:, par, c, hp % 2, :, :].rearrange("p e l -> p (e l)"),
                                 kl_batch[:, par, c, :], start=half == 0, stop=half == 1)
            last.then_inc(scores, 1)

        def probability_transposes(b, hp):
            pe.wait_ge(p_ready, 4 * b + hp + 1)
            pe.wait_ge(pt_ready, 4 * b + hp)
            for t in range(TT):
                pe.transpose(ps[:, PTB, t * P:(t + 1) * P], p[:, hp % 2, t * P:(t + 1) * P], m.ident[:, :])
            pe.transpose(pt5, p[:, hp % 2, KEYS:NK], m.ident[:, :]).then_inc(pt_done, 1)

        def values(b, par, hp):
            pe.wait_ge(pt_ready, 4 * b + hp + 1)
            pe.wait_ge(v_ready, 4 * b + 4)
            cols = slice(hp * P, (hp + 1) * P)
            for t in range(TT):
                pe.matmul(pv, v[:, par, t, cols], pt[:, t, :], start=t == 0, stop=False)
            pe.matmul(pv, vl_batch[:, cols], pt[0:L, TT, :],
                      start=False, stop=True).then_inc(pv_done, 1)

        def step(b, par, lin=True, att=True, nxt=True):
            for hp in range(PAIRS):
                if att:
                    attention_scores(b - 1, 1 - par, hp)
                if lin:
                    linear(b, par, 2 * hp)
                if att:
                    probability_transposes(b - 1, hp)
                if lin:
                    linear(b, par, 2 * hp + 1, range(0, 2))
                if att:
                    values(b - 1, 1 - par, hp)
                if lin:
                    linear(b, par, 2 * hp + 1, range(2, 4))
                if nxt and hp:
                    for c in ([0], [1], [2, 3])[hp - 1]:
                        context_transposes(b + 1, 1 - par, c)

        for c in range(KC):
            context_transposes(0, 0, c)
        pe.wait_ge(lat_out, 3 * KC)
        step(0, 0, att=False)
        with pe.Fori(0, 3) as i:
            step(2 * i + 1, 1)
            step(2 * i + 2, 0)
        step(7, 1, nxt=False)
        pe.wait_ge(lin_done, 8 * B)
        pe.sem_inc(m.unit_done, 8)
        step(8, 0, lin=False, nxt=False)

        pe.wait_ge(o_split, halves + PAIRS)
        for c in range(KC):
            u = first_unit + 12 + c
            pe.wait_ge(m.unit_ready, u + 1)
            for t in range(TT):
                last = product(pe, ps[:, LIN + t, :], (oh[:, c, t * P:(t + 1) * P], ol[:, c, t * P:(t + 1) * P]),
                               (m.wh[:, u % RING_UNITS, :], m.wl[:, u % RING_UNITS, :]), c == 0, c == KC - 1)
                if c == KC - 1 and t < TT - 1:
                    last.then_inc(out_done, 1)
            last.then_inc(m.unit_done, 1)

    def scalar(act):
        steps = m.act_steps
        load = lambda out, src: act.dma_start(out, src).then_inc(consts, 16)
        load(cos[:, :], m.d["rope_cos"])
        load(sin[:, :], m.d["rope_sin"])
        load(gx[:, :], m.d["gamma_x"])
        load(bx[:, :], m.d["beta_x"])
        load(gl[:, :], m.d["gamma_l"])
        load(bl[:, :], m.d["beta_l"])

        for n in range(2):
            act.wait_ge(lat_stats, n + 1)
            guess_rstd(act, steps, ve[:, :], rstd[:, :]).then_inc(lat_guess, 1)
        act.wait_ge(consts, loaded + 6 * 16)
        for c in range(KC):
            act.wait_ge(xt_done, c + 1)
            if c >= 2:
                act.wait_ge(x_split, c - 1)
            act.activation(y[:, c % 2, :], ps[:, XT, :], ACT.Identity, scale=gl[:, c:c + 1], bias=bl[:, c:c + 1])\
               .then_inc(y_ready, 1)
        act.wait_ge(ctx_stats, 1)
        guess_rstd(act, steps, ve[:, :], rstd[:, :]).then_inc(ctx_guess, 1)
        for n in range(KC):
            act.wait_ge(m.unit_done, first_unit + n + 1)
            act.activation(q[:, n, :, :].rearrange("p b l -> p (b l)"), ps[:, LIN + n, :], ACT.Copy, scale=SCALE)\
               .then_inc(lat_out, 1)
        for n in range(KC):
            act.wait_ge(lat_done, n + 1)
            act.copy(kl[:, n, :, :].rearrange("p b l -> p (b l)"), ps[:, LIN + n, :]).then_inc(lat_out, 1)
        for t in range(TT):
            act.wait_ge(lat_done, KC + t + 1)
            act.copy(vl[:, 2 * t, :], ps[0:L, LIN + t, :])
            act.copy(vl[:, 2 * t + 1, :], ps[L:P, LIN + t, :]).then_inc(lat_out, 1)

        def context_chunk(b, c):
            act.wait_ge(xt_done, KC * (b + 1) + c + 1)
            act.wait_ge(x_split, KC * (b + 1) + c - 1)
            act.activation(y[:, c % 2, :], ps[:, XT, :], ACT.Identity, scale=gx[:, c:c + 1], bias=bx[:, c:c + 1])\
               .then_inc(y_ready, 1)

        def stage(b, par):
            if isinstance(b, int) and b == 0:
                act.wait_ge(q_zero, 1)
                act.wait_ge(lat_out, 3 * KC)
            for h in range(4):
                rows = slice(32 * h, 32 * h + 32)
                act.copy(q_pairs[rows, par, :, h // 2, h % 2, :], q[rows, :, bass.ds(b, 1), :].rearrange("p c o l -> p c (o l)"))
            act.copy(kl_batch[:, par, :, :], kl[:, :, bass.ds(b, 1), :].rearrange("p c o l -> p c (o l)"))
            act.copy(vl_batch[:, :], vl[:, bass.ds(b, 1), :].rearrange("p o n -> p (o n)")).then_inc(staged, 1)

        def value_tile(b, par, t):
            act.wait_ge(lin_done, 8 * b + 5 + t)
            act.copy(v[:, par, t, :], ps[:, LIN + t, :]).then_inc(v_ready, 1)

        def exponentials(b, hp):
            act.wait_ge(nmax_ready, 4 * b + hp + 1)
            act.activation(p[:, hp % 2, :], sc_all, ACT.Exp, bias=nmax[:, hp % 2:hp % 2 + 1],
                           accum_out=rsum[:, hp % 2:hp % 2 + 1]).then_inc(exp_done, 1)

        def step(b, par, lin=True, att=True, nxt=True):
            for hp in range(PAIRS):
                if att:
                    exponentials(b - 1, hp)
                if nxt and hp == 0:
                    act.wait_ge(ctx_stats, b + 2)
                    guess_rstd(act, steps, ve[:, :], rstd[:, :]).then_inc(ctx_guess, 1)
                if lin and hp >= 2:
                    value_tile(b, par, 2 * hp - 4)
                if att:
                    act.wait_ge(pt_done, 4 * (b - 1) + hp + 1)
                    act.wait_ge(pv_done, 4 * (b - 1) + hp)
                    act.copy(pt[:, 0:TT, :].rearrange("p t n -> p (t n)"), ps[:, PTB, :])
                    act.copy(pt[0:L, TT, :], pt5).then_inc(pt_ready, 1)
                if lin and hp >= 2:
                    value_tile(b, par, 2 * hp - 3)
                if att:
                    act.wait_ge(pv_done, 4 * (b - 1) + hp + 1)
                    for e in range(2):
                        rows = slice(64 * e, 64 * e + 64)
                        last = act.copy(o[rows, hp, bass.ds((b - 1) * L, L)], pv[rows, 64 * e:64 * e + 64])
                    last.then_inc(o_ready, 1)
                if nxt and hp:
                    for c in ([0], [1], [2, 3])[hp - 1]:
                        context_chunk(b + 1, c)
            if lin:
                stage(b, par)

        for c in range(KC):
            context_chunk(0, c)
        step(0, 0, att=False)
        with act.Fori(0, 3) as i:
            steps.enter(i, 2)
            step(2 * i + 1, 1)
            step(2 * i + 2, 0)
            steps.leave(3)
        step(7, 1, nxt=False)
        step(8, 0, lin=False, nxt=False)
        act.wait_ge(o_ready, 4 * B)
        for hp in range(PAIRS):
            act.copy(oh[:, hp, :], o[:, hp, :]).then_inc(o_high, 1)

    def vector(dve):
        steps = m.dve_steps
        dve.memset(q_pairs[:, :, :, :, :, :].rearrange("p s c r e l -> p (s c r e l)"), 0.0).then_inc(q_zero, 1)
        dve.wait_ge(x_loaded, 16)
        for n in range(2):
            rows = ctx[:, 1] if n else x
            row_stats(dve, steps, rows, stats, mv, ve[:, :]).then_inc(lat_stats, 1)
            dve.wait_ge(lat_guess, n + 1)
            refine_rstd(dve, steps, ve[:, :], rstd[:, :], tmp[:, :])
            last = normalize_rows(dve, ctx[:, 1], rows, mv, rstd)
            if n:
                last.then_inc(lat_rows, 1)
            else:
                steps.done(last)

        def split(n, slot, c):
            dve.wait_ge(y_ready, n + 1)
            steps.done(dve.tensor_copy(xh[:, slot, c, :], y[:, c % 2, :]))
            dve.tensor_tensor(xl[:, slot, c, :], y[:, c % 2, :], f32(xh[:, slot, c, :]), ALU.subtract)\
               .then_inc(x_split, 1)

        def context_rows(b, par):
            dve.wait_ge(ctx_loaded[par], 8 * (b - par) + 16)
            row_stats(dve, steps, ctx[:, par], stats, mv, ve[:, :]).then_inc(ctx_stats, 1)
            dve.wait_ge(ctx_guess, b + 1)
            refine_rstd(dve, steps, ve[:, :], rstd[:, :], tmp[:, :])
            normalize_rows(dve, ctx[:, par], ctx[:, par], mv, rstd).then_inc(rows_ready, 1)

        def rotate(b, par, cc):
            dve.wait_ge(lin_done, 8 * b + 2 * cc + 2)
            if cc or not (isinstance(b, int) and b == 0):
                dve.wait_ge(rotated, 2 * b + cc)
            k1, k2 = ps[:, LIN + 2 * cc, :], ps[:, LIN + 2 * cc + 1, :]
            steps.mark(dve.tensor_tensor(kt[:, par, cc, :], k1, cos[:, :], ALU.mult))
            steps.mark(dve.tensor_tensor(by_sin[:, 0, :], k2, sin[:, :], ALU.mult))
            steps.mark(dve.tensor_tensor(kt[:, par, cc + 2, :], k2, cos[:, :], ALU.mult))
            steps.mark(dve.tensor_tensor(by_sin[:, 1, :], k1, sin[:, :], ALU.mult))
            steps.wait()
            steps.mark(dve.tensor_tensor(kt[:, par, cc, :], kt[:, par, cc, :], by_sin[:, 0, :], ALU.subtract))
            dve.tensor_tensor(kt[:, par, cc + 2, :], kt[:, par, cc + 2, :], by_sin[:, 1, :], ALU.add)\
               .then_inc(rotated, 1)

        def softmax(b, hp):
            slot = slice(hp % 2, hp % 2 + 1)
            dve.wait_ge(scores, 4 * b + hp + 1)
            dve.tensor_reduce(nmax[:, slot], sc_all, AX.X, ALU.max, negate=True).then_inc(nmax_ready, 1)
            dve.wait_ge(exp_done, 4 * b + hp + 1)
            steps.done(dve.reciprocal(rinv[:, slot], rsum[:, slot]))
            dve.tensor_scalar(p[:, hp % 2, :], p[:, hp % 2, :], rinv[:, slot], None, ALU.mult).then_inc(p_ready, 1)

        def step(b, par, lin=True, att=True, nxt=True):
            for hp in range(PAIRS):
                if att:
                    softmax(b - 1, hp)
                if nxt and hp == 0:
                    context_rows(b + 1, 1 - par)
                if lin and hp < 2:
                    rotate(b, par, hp)
                if nxt and hp:
                    for c in ([0], [1], [2, 3])[hp - 1]:
                        split(KC * (b + 2) + c, 1 - par, c)

        for c in range(KC):
            split(c, 1, c)
        context_rows(0, 0)
        dve.wait_ge(consts, loaded + 6 * 16)
        for c in range(KC):
            split(KC + c, 0, c)
        step(0, 0, att=False)
        with dve.Fori(0, 3) as i:
            steps.enter(i, 64)
            step(2 * i + 1, 1)
            step(2 * i + 2, 0)
            steps.leave(3)
        step(7, 1, nxt=False)
        step(8, 0, lin=False, nxt=False)
        for hp in range(PAIRS):
            dve.wait_ge(o_high, halves + hp + 1)
            dve.tensor_tensor(ol[:, hp, :], o[:, hp, :], f32(oh[:, hp, :]), ALU.subtract).then_inc(o_split, 1)
        for t in range(TT):
            if t < TT - 1:
                dve.wait_ge(out_done, outs + t + 1)
            else:
                dve.wait_ge(m.unit_done, first_unit + 16)
            dve.tensor_tensor(x[:, t, :], x[:, t, :], ps[:, LIN + t, :], ALU.add).then_inc(m.x_ready, 1)

    def loads(sp):
        def load_context(b, par, trip):
            sp.dma_start(ctx[:, par, :, :], m.d["ctx_rows"][bass.ds(b, 1)].rearrange("o p t n -> (o p) t n"))\
              .then_inc(ctx_loaded[par], 16)

        load_context(0, 0, 0)
        sp.wait_ge(xt_done, KC)
        load_context(1, 1, 0)
        with sp.Fori(1, B // 2) as i:
            for par in range(2):
                b = 2 * i + par
                sp.wait_ge(xt_done, KC * b)
                load_context(b, par, i)

    return tensor, scalar, vector, loads


def oscillator(nc, m, first_unit, k):
    G, DI = 8, 1024
    NM = DI // P
    CONV = 4
    with ExitStack() as mem:
        sb = lambda name, shape, dt=F32: mem.enter_context(nc.sbuf_tensor("os_" + name, shape, dt))
        vh, vl = sb("vh", [P, NM, T], F32R), sb("vl", [P, NM, T], F32R)
        qs = sb("qs", [P, 2, 2, G, B, L + 1])
        aw = sb("aw", [P, 2, G, B, L])
        small = sb("small", [P, 128])
        u3 = sb("u3", [P, 3, 2, G * B])
        with ExitStack() as early:
            sbe = lambda name, shape, dt=F32: early.enter_context(nc.sbuf_tensor("os_" + name, shape, dt))
            xh, xl = sbe("xh", [P, KC, T], F32R), sbe("xl", [P, KC, T], F32R)
            with ExitStack() as first:
                wph, wpl = (first.enter_context(nc.sbuf_tensor("os_" + n, [P, KC, P], F32R)) for n in ("wph", "wpl"))
            gate_out = sbe("gate_out", [P, 2, T])
        bc = sb("bc", [P, 4, T])
        sq = sb("sq", [P, T])
        gt = sb("gt", [P, 2, 4, P])
        ur = sb("ur", [P, TT, P])
        vg = sb("vg", [P, T])
        mask, ones = sb("mask", [P, P]), sb("ones", [P, P])
    early_at = qs[:, :, :, :, :, :].rearrange("p r c g b t -> p (r c g b t)")
    take = lambda n, at: early_at[:, at * 512:(at + n) * 512]
    rows = take(4, 0).rearrange("p (t n) -> p t n", t=TT)
    conv_y, silu_y = take(2, 4).rearrange("p (s n) -> p s n", s=2), take(2, 6).rearrange("p (s n) -> p s n", s=2)
    select = take(4, 8).rearrange("p (g n) -> p g n", g=2 * G)
    compact, e_u, e_w, e_d, e_l = (take(1, 12 + n) for n in range(5))
    dt_rows = take(2, 17).rearrange("p (s n) -> p s n", s=2)
    wp_raw = take(1, 19).rearrange("p (c n) -> p c n", c=KC)
    slot = lambda n: aw[:, 0, n, :, :].rearrange("p b t -> p (b t)")
    g0, g1, e0, e1, v1, v2, ta, tb = (slot(n) for n in range(8))
    conv_w, conv_b, skip = small[:, 44:76].rearrange("p (m j) -> p m j", j=CONV), small[:, 76:84], small[:, 84:92]
    a_log, root_a, inv_root = small[:, 92:100], small[:, 100:108], small[:, 108:116]
    dt_bias = small[:, 116:117]
    gates = nc.dram_tensor("os_gates", (P, NM, T), F32, kind="Internal").ap()
    s = lambda name: m.sem("os_" + name)
    consts, loaded = m.shared("stage_consts", 7 * 16)
    ln = NormalizedColumns(m, k, rows, small, xh, xl, 1)
    late_consts, wp_split, roots = s("late_consts"), s("wp_split"), s("roots")
    par_done, e_ready, w_ready, l_ready, k_ready, compact_ready = (
        s(n) for n in ("par_done", "e_ready", "w_ready", "l_ready", "k_ready", "compact_ready"))
    tap, conv_done, silu_done, v_split = s("tap"), s("conv_done"), s("silu_done"), s("v_split")
    sel_done, dt_copied, aw_ready = s("sel_done"), s("dt_copied"), s("aw_ready")
    gate_silu, gate_stored = s("gate_silu"), [s("gate_stored0"), s("gate_stored1")]
    squared, sums_done, rooted, bc_ready = s("squared"), s("sums_done"), s("rooted"), s("bc_ready")
    vg_ready, ur_done, ur_ready = s("vg_ready"), s("ur_done"), s("ur_ready")
    w_used, gate_loaded = s("w_used"), s("gate_loaded")
    ge_ready, head_done, gt_ready, y_done, y_ready = (s(n) for n in ("ge_ready", "head_done", "gt_ready", "y_done", "y_ready"))
    (y_high, halves), (y_split, _) = m.shared("out_high", 8), m.shared("out_split", 8)
    out_done, outs = m.shared("out_done", TT - 1)
    LIN, PAR, SEL, SUM, GB, YB = 1, 5, 6, 5, (0, 7), 6
    ps = m.ps
    value_unit, gate_unit, bc_unit, out_unit = first_unit, first_unit + 8, first_unit + 16, first_unit + 80

    def pair_of(h, n, c):
        return h[:, n % RING_UNITS, c * P:(c + 1) * P]

    def tensor(pe):
        ln.tensor(pe)
        ln.wait_split(pe, KC)
        pe.wait_ge(wp_split, 1)
        for c in range(KC):
            last = product(pe, ps[:, PAR, :], (wph[:, c, :], wpl[:, c, :]), (xh[:, c, :], xl[:, c, :]), c == 0, c == KC - 1)
        last.then_inc(par_done, 1)

        def columns(n, bank, unit):
            pe.wait_ge(m.unit_ready, unit + 1)
            for c in range(KC):
                last = product(pe, ps[:, bank, :], (pair_of(m.wh, unit, c), pair_of(m.wl, unit, c)),
                               (xh[:, c, :], xl[:, c, :]), c == 0, c == KC - 1)
            last.then_inc(m.unit_done, 1)

        for n in range(NM):
            if n >= 4:
                pe.wait_ge(conv_done, n - 3)
            columns(n, LIN + n % 4, value_unit + n)
        pe.wait_ge(compact_ready, 1)
        for g in range(G):
            pe.wait_ge(aw_ready, g)
            pe.matmul(ps[:, SEL, :], select[:, g, :], compact, start=True, stop=True)
            pe.matmul(ps[:, SEL + 1, :], select[:, G + g, :], compact, start=True, stop=True).then_inc(sel_done, 1)
        for n in range(NM):
            pe.wait_ge(conv_done, NM)
            if n >= 4:
                pe.wait_ge(gate_silu, n - 3)
            columns(n, LIN + n % 4, gate_unit + n)

        def bc_products(g, j):
            if isinstance(g, int) and g == 0:
                pe.wait_ge(v_split, NM)
                pe.wait_ge(gate_silu, 5 + j)
            else:
                pe.wait_ge(bc_ready, 4 * g + (j - 3))
            for half in range(2):
                at = 2 * j + half
                pe.wait_ge(m.unit_ready, bc_unit + 8 * g + (at + 1))
                for c in range(KC):
                    cc = KC * half + c
                    last = product(pe, ps[:, LIN + j, :], (pair_of(m.wh, bc_unit + at, c), pair_of(m.wl, bc_unit + at, c)),
                                   (vh[:, cc, :], vl[:, cc, :]), cc == 0, cc == NM - 1)
                last.then_inc(m.unit_done, 1)

        def sums(g, j):
            pe.wait_ge(squared, 4 * g + j + 1)
            pe.matmul(ps[:, SUM, :], ones[:, :], sq[:, :], start=True, stop=True).then_inc(sums_done, 1)

        def turn_values(g):
            pe.wait_ge(vg_ready, g + 1)
            if not (isinstance(g, int) and g == 0):
                pe.wait_ge(y_ready, g)
            for t in range(TT):
                last = pe.transpose(ps[:, YB, t * P:(t + 1) * P], vg[:, t * P:(t + 1) * P], m.ident[:, :])
            last.then_inc(ur_done, 1)

        def outputs(g):
            pe.wait_ge(ge_ready, g + 1)
            for half in range(2):
                pe.wait_ge(gt_ready, 4 * g + 2 * half)
                for h in range(4):
                    if h >= 2:
                        pe.wait_ge(head_done, 8 * g + 4 * half + h - 1)
                    hr = slice(32 * h, 32 * h + 32)
                    for q in range(2):
                        cols = slice((2 * half + q) * P, (2 * half + q + 1) * P)
                        at = ((h // 2) * 2 + q) * P
                        out = ps[:, GB[h % 2], at:at + P]
                        pe.matmul(out, g0[hr, cols], e0[hr, cols], start=True, stop=False)
                        last = pe.matmul(out, g1[hr, cols], e1[hr, cols], start=False, stop=True)
                    last.then_inc(head_done, 1)
                pe.wait_ge(ur_ready, g + 1)
                for h in range(4):
                    if h < 2:
                        pe.wait_ge(gt_ready, 4 * g + 2 * half + h + 1)
                    for q in range(2):
                        pr = 2 * half + q
                        last = pe.matmul(ps[32 * h:32 * h + 32, YB, pr * P:(pr + 1) * P], ur[:, pr, 32 * h:32 * h + 32],
                                         gt[:, h % 2, (h // 2) * 2 + q, :], start=True, stop=True)
                last.then_inc(y_done, 1)

        def group(g, bc=True, out=True):
            if bc:
                bc_products(g, 0)
                for j in range(1, 4):
                    bc_products(g, j)
                    sums(g, j - 1)
                sums(g, 3)
            if out:
                turn_values(g - 1)
                outputs(g - 1)

        pe.wait_ge(late_consts, 2 * 16)
        group(0, out=False)
        with pe.Fori(1, G) as g:
            group(g)
        group(G, bc=False)
        for cc in range(NM):
            u = out_unit + cc
            pe.wait_ge(m.unit_ready, u + 1)
            pe.wait_ge(y_split, halves + cc + 1)
            for t in range(TT):
                last = product(pe, ps[:, LIN + t, :], (vh[:, cc, t * P:(t + 1) * P], vl[:, cc, t * P:(t + 1) * P]),
                               (m.wh[:, u % RING_UNITS, :], m.wl[:, u % RING_UNITS, :]), cc == 0, cc == NM - 1)
                if cc == NM - 1 and t < TT - 1:
                    last.then_inc(out_done, 1)
            last.then_inc(m.unit_done, 1)

    def scalar(act):
        steps = m.act_steps
        if k:
            act.wait_ge(m.x_ready, TT * k)
        for out, src in ((conv_w, m.d["conv_w"]), (conv_b, m.d["conv_b"]), (skip, m.d["skip"]), (a_log, m.d["a_log"]),
                         (dt_bias[0:32, :], m.d["dt_bias"]), (select, m.d["select"]), (wp_raw, m.d["w_params"])):
            act.dma_start(out, src).then_inc(consts, 16)
        ln.scalar_guess(act, steps)
        act.wait_ge(consts, loaded + 7 * 16)
        steps.mark(act.activation(root_a, a_log, ACT.Exp, scale=0.5))
        act.activation(inv_root, a_log, ACT.Exp, scale=-0.5).then_inc(roots, 1)
        ln.scalar_high(act)
        act.wait_ge(par_done, 1)
        act.activation(e_u[0:32, :], ps[0:32, PAR, :], ACT.Exp, bias=dt_bias[0:32, :]).then_inc(e_ready, 1)
        act.wait_ge(w_ready, 1)
        act.activation(e_l[0:32, :], e_w[0:32, :], ACT.Ln).then_inc(l_ready, 1)
        act.activation(e_l[32:64, :], ps[32:64, PAR, :], ACT.Sigmoid).then_inc(k_ready, 1)

        def first_tap(n):
            act.wait_ge(m.unit_done, value_unit + n + 1)
            if n >= 2:
                act.wait_ge(silu_done, n - 1)
            act.activation(conv_y[:, n % 2, :], ps[:, LIN + n % 4, :], ACT.Identity, scale=conv_w[:, n, 3:4],
                           bias=conv_b[:, n:n + 1]).then_inc(tap, 1)

        for n in range(NM + 1):
            if n < NM:
                first_tap(n)
            if n:
                act.wait_ge(conv_done, n)
                if n >= 3:
                    act.wait_ge(v_split, n - 2)
                act.activation(silu_y[:, (n - 1) % 2, :], conv_y[:, (n - 1) % 2, :], ACT.Silu).then_inc(silu_done, 1)
        for g in range(G):
            act.wait_ge(sel_done, g + 1)
            act.copy(dt_rows[:, g % 2, :], ps[:, SEL, :]).then_inc(dt_copied, 1)
        for n in range(NM):
            act.wait_ge(m.unit_done, gate_unit + n + 1)
            if n >= 2:
                act.wait_ge(gate_stored[n % 2], 16 * (n // 2))
            act.activation(gate_out[:, n % 2, :], ps[:, LIN + n % 4, :], ACT.Silu).then_inc(gate_silu, 1)
            act.wait_ge(gate_silu, n + 1)
            act.dma_start(gates[:, n, :], gate_out[:, n % 2, :]).then_inc(gate_stored[n % 2], 16)
        act.dma_start(mask[:, :], m.d["causal"]).then_inc(late_consts, 16)
        act.dma_start(ones[:, :], m.d["group_ones"]).then_inc(late_consts, 16)
        for n in range(2):
            act.wait_ge(gate_stored[n], 16 * NM // 2)

        def norms(g, j):
            act.wait_ge(m.unit_done, bc_unit + 8 * g + (2 * j + 2))
            if j or not (isinstance(g, int) and g == 0):
                act.wait_ge(bc_ready, 4 * g + j)
            act.activation(sq[:, :], ps[:, LIN + j, :], ACT.Square).then_inc(squared, 1)
            act.wait_ge(sums_done, 4 * g + j + 1)
            act.activation(sq[:, :], ps[:, SUM, :], ACT.Sqrt).then_inc(rooted, 1)

        def value_rows(g):
            act.wait_ge(w_used, g + 1)
            act.dma_start(aw[:, 1, bass.ds(g, 1), :, :].rearrange("p o b t -> p (o b t)"),
                          gates[:, bass.ds(g, 1), :].rearrange("p o n -> p (o n)")).then_inc(gate_loaded, 16)
            act.wait_ge(ur_done, g + 1)
            act.copy(ur[:, :, :].rearrange("p t n -> p (t n)"), ps[:, YB, :]).then_inc(ur_ready, 1)

        def group(g, bc=True, out=True):
            if bc:
                for j in range(4):
                    norms(g, j)
            if out:
                value_rows(g - 1)

        group(0, out=False)
        with act.Fori(1, G) as g:
            group(g)
        group(G, bc=False)
        act.wait_ge(y_ready, G)
        for cc in range(NM):
            act.copy(vh[:, cc, :], qs[:, 0, 0, cc, :, 1:L + 1].rearrange("p b t -> p b t")).then_inc(y_high, 1)

    def vector(dve):
        steps = m.dve_steps
        if k:
            dve.wait_ge(m.x_ready, TT * k)
        dve.wait_ge(consts, loaded + 7 * 16)
        steps.done(dve.tensor_copy(wph[:, :, :], wp_raw))
        dve.tensor_tensor(wpl[:, :, :], wp_raw, f32(wph[:, :, :]), ALU.subtract).then_inc(wp_split, 1)
        ln.vector_rows(dve, steps)
        steps.done(dve.memset(compact, 0.0))
        ln.vector_low(dve)
        dve.wait_ge(e_ready, 1)
        d32 = slice(0, 32)
        steps.done(dve.tensor_scalar(e_u[d32, :], e_u[d32, :], 1e4, None, ALU.min))
        steps.done(dve.tensor_scalar(e_w[d32, :], e_u[d32, :], 1.0, None, ALU.add))
        dve.tensor_scalar(e_d[d32, :], e_w[d32, :], -1.0, 1e-30, ALU.add, ALU.max).then_inc(w_ready, 1)
        dve.wait_ge(w_ready, 1)
        steps.done(dve.reciprocal(e_d[d32, :], e_d[d32, :]))
        steps.done(dve.tensor_tensor(e_u[d32, :], e_u[d32, :], e_d[d32, :], ALU.mult))
        dve.wait_ge(l_ready, 1)
        steps.done(dve.tensor_tensor(e_u[d32, :], e_u[d32, :], e_l[d32, :], ALU.mult))
        steps.mark(dve.tensor_scalar(compact[d32, :], e_u[d32, :], 1e-4, 0.1, ALU.max, ALU.min))
        dve.wait_ge(k_ready, 1)
        dve.tensor_scalar(compact[32:64, :], e_l[32:64, :], 0.5, None, ALU.mult).then_inc(compact_ready, 1)

        by_batch = lambda ap: ap.rearrange("p (b t) -> p b t", b=B)

        def convolve(n):
            dve.wait_ge(tap, n + 1)
            y, v = by_batch(conv_y[:, n % 2, :]), by_batch(ps[:, LIN + n % 4, :])
            for j in range(1, CONV):
                ins = dve.scalar_tensor_tensor(y[:, :, j:], v[:, :, 0:L - j], conv_w[:, n, 3 - j:4 - j], y[:, :, j:],
                                               ALU.mult, ALU.add)
                if j < CONV - 1:
                    steps.done(ins)
            ins.then_inc(conv_done, 1)

        def split_value(n):
            dve.wait_ge(silu_done, n + 1)
            steps.done(dve.tensor_copy(vh[:, n, :], silu_y[:, n % 2, :]))
            dve.tensor_tensor(vl[:, n, :], silu_y[:, n % 2, :], f32(vh[:, n, :]), ALU.subtract).then_inc(v_split, 1)

        for n in range(NM + 1):
            if n < NM:
                convolve(n)
            if n:
                split_value(n - 1)
        dve.wait_ge(roots, 1)
        for g in range(G):
            a_g, w_g = (aw[:, n, g, :, :].rearrange("p b t -> p (b t)") for n in range(2))
            dve.wait_ge(dt_copied, g + 1)
            steps.mark(dve.tensor_tensor(a_g, dt_rows[:, g % 2, :], ps[:, SEL + 1, :], ALU.mult))
            steps.done(dve.tensor_scalar(w_g, dt_rows[:, g % 2, :], root_a[:, g:g + 1], None, ALU.mult))
            dve.tensor_scalar(a_g, a_g, 1.0, None, ALU.add).then_inc(aw_ready, 1)
        dve.wait_ge(aw_ready, G)

        qt = qs[:, :, :, :, :, :].rearrange("p r c g b t -> p r c (g b) t")
        at = aw[:, :, :, :, :].rearrange("p c g b t -> p c (g b) t")
        for r in range(2):
            for c in range(2):
                steps.mark(dve.memset(qt[:, r, c, :, 0], 1.0 if r == c else 0.0))
        steps.wait()
        col = lambda ap: ap.rearrange("p r n o -> p r (n o)")
        with dve.Fori(0, L) as t:
            steps.enter(t, 4)
            q_a, q_c = (col(qt[:, :, c, :, bass.ds(t, 1)]) for c in range(2))
            n_a, n_c = (col(qt[:, :, c, :, bass.ds(t + 1, 1)]) for c in range(2))
            a_w = col(at[:, :, :, bass.ds(t, 1)])
            steps.mark(dve.tensor_tensor(u3[:, 0:2, :, :], a_w.unsqueeze(2).to_broadcast([P, 2, 2, G * B]),
                                         q_a.unsqueeze(1).to_broadcast([P, 2, 2, G * B]), ALU.mult))
            steps.mark(dve.tensor_tensor(u3[:, 2, :, :], a_w[:, 1:2, :].to_broadcast([P, 2, G * B]), q_c, ALU.mult))
            steps.wait()
            steps.mark(dve.tensor_tensor(n_a, u3[:, 0, :, :], u3[:, 2, :, :], ALU.subtract))
            steps.mark(dve.tensor_tensor(n_c, u3[:, 1, :, :], q_c, ALU.add))
            steps.wait()
            steps.leave(L)

        def normalize(g, j):
            dve.wait_ge(rooted, 4 * g + j + 1)
            steps.done(dve.tensor_scalar(sq[:, :], sq[:, :], 1e-8, None, ALU.add))
            steps.done(dve.reciprocal(sq[:, :], sq[:, :]))
            dve.tensor_tensor(bc[:, j, :], ps[:, LIN + j, :], sq[:, :], ALU.mult).then_inc(bc_ready, 1)

        def inputs_and_outputs(g):
            at_g = lambda r, c, d: qs[:, r, c, bass.ds(g, 1), :, d:d + L].rearrange("p o b t -> p (o b) t")
            w_g = aw[:, 1, bass.ds(g, 1), :, :].rearrange("p o b t -> p (o b t)")
            ir = inv_root[:, bass.ds(g, 1)]
            mul = lambda out, x, y: steps.mark(dve.tensor_tensor(out, x, y, ALU.mult))
            sub = lambda out, x, y: steps.mark(dve.tensor_tensor(out, x, y, ALU.subtract))
            dve.wait_ge(bc_ready, 4 * g + 4)
            if not (isinstance(g, int) and g == 0):
                dve.wait_ge(y_done, 2 * g)
            dve.tensor_tensor(vg[:, :], f32(vh[:, bass.ds(g, 1), :]).rearrange("p o n -> p (o n)"),
                              f32(vl[:, bass.ds(g, 1), :]).rearrange("p o n -> p (o n)"), ALU.add).then_inc(vg_ready, 1)
            mul(v2, w_g, bc[:, 1, :])
            steps.wait()
            steps.done(dve.scalar_tensor_tensor(v1, bc[:, 0, :], ir, v2, ALU.mult, ALU.add))
            dve.tensor_tensor(v1, v1, w_g, ALU.mult).then_inc(w_used, 1)
            dve.wait_ge(w_used, g + 1)
            for r, out in ((0, g0), (1, g1)):
                mul(by_batch(ta), at_g(r, 0, 0), by_batch(v1))
                mul(by_batch(tb), at_g(r, 1, 0), by_batch(v2))
                steps.wait()
                steps.done(dve.tensor_tensor(out, ta, tb, ALU.add))
            mul(by_batch(ta), at_g(0, 0, 1), at_g(1, 1, 1))
            mul(by_batch(tb), at_g(1, 0, 1), at_g(0, 1, 1))
            steps.mark(dve.tensor_scalar(bc[:, 3, :], bc[:, 3, :], ir, None, ALU.mult))
            steps.wait()
            sub(v1, ta, tb)
            steps.wait()
            steps.mark(dve.reciprocal(v1, v1))
            for (ra, ca, xa), (rb, cb, xb), out in (((1, 1, 2), (1, 0, 3), e0), ((0, 0, 3), (0, 1, 2), e1)):
                mul(by_batch(ta), at_g(ra, ca, 1), by_batch(bc[:, xa, :]))
                mul(by_batch(tb), at_g(rb, cb, 1), by_batch(bc[:, xb, :]))
                steps.wait()
                sub(ta, ta, tb)
                steps.wait()
                last = dve.tensor_tensor(out, ta, v1, ALU.mult)
                if out is e0:
                    steps.done(last)
            last.then_inc(ge_ready, 1)
            dve.wait_ge(ge_ready, g + 1)

        def gated_output(g):
            for half in range(2):
                dve.wait_ge(head_done, 8 * g + 4 * half + 4)
                if half or not (isinstance(g, int) and g == 0):
                    dve.wait_ge(y_done, 2 * g + half)
                for n in range(2):
                    dve.tensor_tensor(gt[:, n, :, :], ps[:, GB[n], :].rearrange("p (a t) -> p a t", a=4),
                                      mask[:, :].unsqueeze(1).to_broadcast([P, 4, P]), ALU.mult).then_inc(gt_ready, 1)
            dve.wait_ge(y_done, 2 * g + 2)
            dve.wait_ge(gate_loaded, 16 * (g + 1))
            steps.done(dve.scalar_tensor_tensor(ta, vg[:, :], skip[:, bass.ds(g, 1)], ps[:, YB, :], ALU.mult, ALU.add))
            dve.tensor_tensor(qs[:, 0, 0, bass.ds(g, 1), :, 1:L + 1].rearrange("p o b t -> p (o b) t"), by_batch(ta),
                              aw[:, 1, bass.ds(g, 1), :, :].rearrange("p o b t -> p (o b) t"), ALU.mult).then_inc(y_ready, 1)
            dve.wait_ge(y_ready, g + 1)

        def group(g, bc_part=True, out=True):
            if out:
                inputs_and_outputs(g - 1)
            if bc_part:
                for j in range(4):
                    normalize(g, j)
            if out:
                gated_output(g - 1)

        dve.wait_ge(late_consts, 2 * 16)
        group(0, out=False)
        with dve.Fori(1, G) as g:
            steps.enter(g - 1, 29)
            group(g)
            steps.leave(G - 1)
        group(G, bc_part=False)
        for cc in range(NM):
            dve.wait_ge(y_high, halves + cc + 1)
            dve.tensor_tensor(by_batch(vl[:, cc, :]), qs[:, 0, 0, cc, :, 1:L + 1], by_batch(f32(vh[:, cc, :])), ALU.subtract)\
               .then_inc(y_split, 1)
        for t in range(TT):
            if t < TT - 1:
                dve.wait_ge(out_done, outs + t + 1)
            else:
                dve.wait_ge(m.unit_done, out_unit + NM)
            dve.tensor_tensor(m.x[:, t, :], m.x[:, t, :], ps[:, LIN + t, :], ALU.add).then_inc(m.x_ready, 1)

    return tensor, scalar, vector, None


def bit_ffn(nc, m, first_unit, k):
    H = 2048
    NH = H // P
    HT = 4
    with ExitStack() as mem:
        sb = lambda name, shape, dt=F32: mem.enter_context(nc.sbuf_tensor("bf_" + name, shape, dt))
        w1, w2 = sb("w1", [P, KC, H]), sb("w2", [P, NH, D])
        w1q, w2q = sb("w1q", [P, KC, H], BF16), sb("w2q", [P, NH, D], BF16)
        rows = sb("rows", [P, TT, D])
        rq = sb("rq", [P, TT, D], BF16)
        xq = sb("xq", [P, KC, T], BF16)
        hid = sb("hid", [P, NH // 2, T])
        top = sb("top", [P, T])
        scaled, conv_y, magnitude = sb("scaled", [P, T]), sb("conv_y", [P, 2, T]), sb("magnitude", [P, T])
        inv_row = sb("inv_row", [P, T])
        diag = sb("diag", [P, TT, P])
        ones, ident16 = sb("ones", [P, P]), sb("ident16", [P, P], BF16)
        small = sb("small", [P, 256])
    stats = small[:, 0:24].rearrange("p (t n) -> p t n", n=6)
    mv = small[:, 24:32].rearrange("p (t n) -> p t n", n=2)
    ve, rstd, tmp = small[:, 32:36], small[:, 36:40], small[:, 40:44]
    row_max, row_scale, row_inv = small[:, 44:48], small[:, 48:52], small[:, 52:56]
    hid_max, hid_scale, hid_inv = small[:, 56:60], small[:, 60:64], small[:, 64:68]
    w_sums, w_sum, w_mean, w_scale = small[:, 72:104], small[:, 104:106], small[:, 106:108], small[:, 108:110]
    conv_w, conv_b = small[:, 112:160].rearrange("p (n j) -> p n j", j=3), small[:, 160:176]
    s = lambda name: m.sem("bf_" + name)
    consts, loaded = m.shared("stage_consts", 3 * 16)
    w_loaded = [s("w1_loaded"), s("w2_loaded")]
    summed, sum_ready, total_done, scale_ready = (s(n) for n in ("summed", "sum_ready", "total_done", "scale_ready"))
    shifted, w_ready = s("shifted"), s("w_ready")
    ln_stats, ln_guess, rq_ready, rows_turned, xq_ready = (s(n) for n in ("ln_stats", "ln_guess", "rq_ready", "rows_turned", "xq_ready"))
    diag_ready, spread_done, spread_ready = s("diag_ready"), s("spread_done"), s("spread_ready")
    h_done, scaled_ready, tap, conv_done, silu_done, mag_ready, top_ready = (
        s(n) for n in ("h_done", "scaled_ready", "tap", "conv_done", "silu_done", "mag_ready", "top_ready"))
    top_turned, diag2_ready, spread2_done, q_ready = (
        s(n) for n in ("top_turned", "diag2_ready", "spread2_done", "q_ready"))
    out_done, outs = m.shared("out_done", TT)
    TURN, LIN, SPREAD, TOT = 0, 1, 5, 6
    ps = m.ps
    w1_flat = w1[:, :, :].rearrange("p c n -> p (c n)")
    w2_flat = w2[:, :, :].rearrange("p c n -> p (c n)")
    hidden = lambda n: hid[:, n, :] if n < NH // 2 else w1_flat[:, (n - NH // 2) * T:(n - NH // 2 + 1) * T]
    q2 = w2_flat.bitcast(BF16)[:, 0:NH * T].rearrange("p (n t) -> p n t", n=NH)

    def tensor(pe):
        pe.wait_ge(sum_ready, 1)
        pe.wait_ge(consts, loaded + 3 * 16)
        pe.wait_ge(m.consts, 16)
        pe.matmul(ps[:, TOT, 0:2], ones[:, :], w_sum, start=True, stop=True).then_inc(total_done, 1)
        turned = ps[:, TURN, :].bitcast(BF16)
        for c in range(KC):
            pe.wait_ge(rq_ready, 1)
            if c:
                pe.wait_ge(xq_ready, c)
            for t in range(TT):
                last = pe.transpose(turned[:, t * P:(t + 1) * P], rq[:, t, c * P:(c + 1) * P], ident16[:, :])
            last.then_inc(rows_turned, 1)
        pe.wait_ge(diag_ready, 1)
        for t in range(TT):
            last = pe.matmul(ps[:, SPREAD, t * P:(t + 1) * P], ones[:, :], diag[:, t, :], start=True, stop=True)
        last.then_inc(spread_done, 1)
        pe.wait_ge(xq_ready, KC)
        pe.wait_ge(w_ready, 4)
        for n in range(NH):
            if n >= 4:
                pe.wait_ge(scaled_ready, n - 3)
            for c in range(KC):
                last = pe.matmul(ps[:, LIN + n % 4, :], w1q[:, c, n * P:(n + 1) * P], xq[:, c, :], start=c == 0, stop=c == KC - 1)
            last.then_inc(h_done, 1)
        pe.wait_ge(top_ready, NH)
        for t in range(TT):
            last = pe.transpose(ps[:, TURN, t * P:(t + 1) * P], top[:, t * P:(t + 1) * P], m.ident[:, :])
        last.then_inc(top_turned, 1)
        pe.wait_ge(diag2_ready, 1)
        for t in range(TT):
            last = pe.matmul(ps[:, SPREAD, t * P:(t + 1) * P], ones[:, :], diag[:, t, :], start=True, stop=True)
        last.then_inc(spread2_done, 1)
        pe.wait_ge(w_ready, 8)
        for n in range(NH):
            pe.wait_ge(q_ready, n + 1)
            for t in range(TT):
                last = pe.matmul(ps[:, LIN + t, :], q2[:, n, t * P:(t + 1) * P], w2q[:, n, :], start=n == 0, stop=n == NH - 1)
                if n == NH - 1:
                    last.then_inc(out_done, 1)

    def scalar(act):
        steps = m.act_steps
        act.wait_ge(m.x_loaded, 16)
        if k:
            act.wait_ge(m.x_ready, TT * k)
        act.dma_start(w1_flat, m.d["ffn_w1"]).then_inc(w_loaded[0], 16)
        act.dma_start(w2_flat, m.d["ffn_w2"]).then_inc(w_loaded[1], 16)
        for out, src in ((conv_w, m.d["ffn_conv_w"]), (conv_b, m.d["ffn_conv_b"]), (ones[:, :], m.d["ones"])):
            act.dma_start(out, src).then_inc(consts, 16)
        act.wait_ge(ln_stats, 1)
        guess_rstd(act, steps, ve, rstd).then_inc(ln_guess, 1)
        for j, (w, wq) in enumerate(((w1_flat, w1q), (w2_flat, w2q))):
            act.wait_ge(w_loaded[j], 16)
            for n in range(4):
                if j or n:
                    act.wait_ge(summed, 4 * j + n)
                act.activation(wq[:, :, :].rearrange("p c n -> p (c n)")[:, n * H:(n + 1) * H], w[:, n * H:(n + 1) * H],
                               ACT.Abs, accum_out=w_sums[:, 4 * j + n:4 * j + n + 1]).then_inc(summed, 1)
        act.wait_ge(scale_ready, 1)
        for j, w in enumerate((w1_flat, w2_flat)):
            for n in range(4):
                cols = slice(n * H, (n + 1) * H)
                act.activation(w[:, cols], w[:, cols], ACT.Copy, scale=w_scale[:, j:j + 1]).then_inc(shifted, 1)
        for c in range(KC):
            act.wait_ge(rows_turned, c + 1)
            act.copy(xq[:, c, :], ps[:, TURN, :].bitcast(BF16)[:, 0:T]).then_inc(xq_ready, 1)
        act.wait_ge(spread_done, 1)
        act.activation(inv_row[:, :], ps[:, SPREAD, :], ACT.Copy, scale=w_mean[:, 0:1]).then_inc(spread_ready, 1)
        for n in range(NH):
            act.wait_ge(scaled_ready, n + 1)
            if n >= 2:
                act.wait_ge(silu_done, n - 1)
            act.activation(conv_y[:, n % 2, :], scaled[:, :], ACT.Identity, scale=conv_w[:, n, 1:2], bias=conv_b[:, n:n + 1])\
               .then_inc(tap, 1)
            act.wait_ge(conv_done, n + 1)
            act.activation(hidden(n), conv_y[:, n % 2, :], ACT.Silu).then_inc(silu_done, 1)
            act.wait_ge(silu_done, n + 1)
            if n:
                act.wait_ge(top_ready, n)
            act.activation(magnitude[:, :], hidden(n), ACT.Abs).then_inc(mag_ready, 1)

    def vector(dve):
        steps = m.dve_steps
        dve.wait_ge(m.x_loaded, 16)
        if k:
            dve.wait_ge(m.x_ready, TT * k)
        dve.wait_ge(m.consts, 16)
        steps.done(dve.tensor_copy(ident16[:, :], m.ident[:, :]))
        row_stats(dve, steps, m.x, stats, mv, ve).then_inc(ln_stats, 1)
        dve.wait_ge(ln_guess, 1)
        refine_rstd(dve, steps, ve, rstd, tmp)
        steps.done(normalize_rows(dve, rows, m.x, mv, rstd))

        def scales(top_values, scale, inverse):
            steps.done(dve.tensor_scalar(top_values, top_values, 1e-5, None, ALU.max))
            steps.done(dve.reciprocal(scale, top_values))
            steps.done(dve.tensor_scalar(scale, scale, 127.0, None, ALU.mult))
            steps.done(dve.reciprocal(inverse, scale))

        steps.done(dve.tensor_reduce(row_max, rows[:, :, :], AX.X, ALU.max, apply_absolute_value=True))
        scales(row_max, row_scale, row_inv)
        for t in range(TT):
            steps.mark(dve.tensor_scalar(rows[:, t, :], rows[:, t, :], row_scale[:, t:t + 1], 127.0, ALU.mult, ALU.min))
        steps.wait()
        steps.done(dve.tensor_scalar(rows[:, :, :], rows[:, :, :], -128.0, MAGIC, ALU.max, ALU.add))
        dve.tensor_scalar(rq[:, :, :], rows[:, :, :], -MAGIC, None, ALU.add).then_inc(rq_ready, 1)
        for t in range(TT):
            last = dve.tensor_scalar(diag[:, t, :], m.ident[:, :], row_inv[:, t:t + 1], None, ALU.mult)
        last.then_inc(diag_ready, 1)
        dve.wait_ge(summed, 8)
        dve.tensor_reduce(w_sum, w_sums[:, 0:8].rearrange("p (j n) -> p j n", j=2), AX.X, ALU.add).then_inc(sum_ready, 1)
        dve.wait_ge(total_done, 1)
        steps.done(dve.tensor_scalar(w_mean, ps[:, TOT, 0:2], 1.0 / (H * D), 1e-5, ALU.mult, ALU.max))
        dve.reciprocal(w_scale, w_mean).then_inc(scale_ready, 1)
        for j, (w, wq) in enumerate(((w1_flat, w1q), (w2_flat, w2q))):
            q = wq[:, :, :].rearrange("p c n -> p (c n)")
            for n in range(4):
                cols = slice(n * H, (n + 1) * H)
                dve.wait_ge(shifted, 4 * j + n + 1)
                steps.done(dve.tensor_scalar(w[:, cols], w[:, cols], 1.0, -1.0, ALU.min, ALU.max))
                dve.tensor_scalar(q[:, cols], w[:, cols], MAGIC, -MAGIC, ALU.add, ALU.add).then_inc(w_ready, 1)
        by_batch = lambda ap: ap.rearrange("p (b t) -> p b t", b=B)
        steps.done(dve.memset(top[:, :], 0.0))
        dve.wait_ge(spread_ready, 1)
        for n in range(NH):
            dve.wait_ge(h_done, n + 1)
            if n:
                dve.wait_ge(conv_done, n)
            dve.tensor_tensor(scaled[:, :], ps[:, LIN + n % 4, :], inv_row[:, :], ALU.mult).then_inc(scaled_ready, 1)
            dve.wait_ge(tap, n + 1)
            y, v = by_batch(conv_y[:, n % 2, :]), by_batch(scaled[:, :])
            steps.done(dve.scalar_tensor_tensor(y[:, :, 1:], v[:, :, 0:L - 1], conv_w[:, n, 0:1], y[:, :, 1:], ALU.mult, ALU.add))
            dve.scalar_tensor_tensor(y[:, :, 0:L - 1], v[:, :, 1:], conv_w[:, n, 2:3], y[:, :, 0:L - 1], ALU.mult, ALU.add)\
               .then_inc(conv_done, 1)
            dve.wait_ge(mag_ready, n + 1)
            dve.tensor_tensor(top[:, :], top[:, :], magnitude[:, :], ALU.max).then_inc(top_ready, 1)
        dve.wait_ge(top_turned, 1)
        steps.done(dve.tensor_reduce(hid_max, ps[:, TURN, :].rearrange("p (t n) -> p t n", t=TT), AX.X, ALU.max))
        scales(hid_max, hid_scale, hid_inv)
        for t in range(TT):
            last = dve.tensor_scalar(diag[:, t, :], m.ident[:, :], hid_scale[:, t:t + 1], None, ALU.mult)
        last.then_inc(diag2_ready, 1)
        steps.done(dve.tensor_scalar(hid_inv, hid_inv, w_mean[:, 1:2], None, ALU.mult))
        dve.wait_ge(spread2_done, 1)
        dve.wait_ge(w_ready, 8)
        for n in range(NH):
            steps.done(dve.tensor_tensor(hidden(n), hidden(n), ps[:, SPREAD, :], ALU.mult))
            steps.done(dve.tensor_scalar(hidden(n), hidden(n), 127.0, -128.0, ALU.min, ALU.max))
            dve.tensor_scalar(q2[:, n, :], hidden(n), MAGIC, -MAGIC, ALU.add, ALU.add).then_inc(q_ready, 1)
        for t in range(TT):
            dve.wait_ge(out_done, outs + t + 1)
            dve.scalar_tensor_tensor(m.x[:, t, :], ps[:, LIN + t, :], hid_inv[:, t:t + 1], m.x[:, t, :], ALU.mult, ALU.add)\
               .then_inc(m.x_ready, 1)

    return tensor, scalar, vector, None


def context_attention(nc, m, first_unit, k):
    SCALE = 32 ** -0.5
    PAIRS = 8
    with ExitStack() as mem:
        sb = lambda name, shape, dt=F32: mem.enter_context(nc.sbuf_tensor("ca_" + name, shape, dt))
        ctx = sb("ctx", [P, 2, KC, KEYS])
        xh, xl = sb("xh", [P, 2, KC, T], F32R), sb("xl", [P, 2, KC, T], F32R)
        rows = sb("rows", [P, TT, D])
        q = sb("q", [P, KC, B, L])
        q_pairs = sb("q_pairs", [P, 2, KC, 2, 2, L])
        kt = sb("kt", [P, 2, KC, KEYS])
        v = sb("v", [P, 2, TT, D])
        p, pt = sb("p", [P, 2, KEYS]), sb("pt", [P, TT, P])
        o = sb("o", [P, KC, T])
        bias = sb("bias", [P, D])
        small = sb("small", [P, 56])
    nmax, rsum, rinv = small[:, 44:46], small[:, 46:48], small[:, 48:50]
    oh, ol = xh[:, 0], xl[:, 0]
    latents = NormalizedColumns(m, k, rows, small, xh[:, 1], xl[:, 1], 1)
    s = lambda name: m.sem("ca_" + name)
    (ctx_loaded0, loads0), (ctx_loaded1, _) = (m.shared(f"ctx_loaded{n}", 16 * B // 2) for n in range(2))
    ctx_loaded = (ctx_loaded0, ctx_loaded1)
    bias_loaded, q_zero, q_ready, staged = s("bias_loaded"), s("q_zero"), s("q_ready"), s("staged")
    ctx_high, ctx_split, kt_ready = s("ctx_high"), s("ctx_split"), s("kt_ready")
    (lin_done, lins), (v_ready, vals) = m.shared("lin_done", 8 * B), m.shared("v_ready", 4 * B)
    (scores, before), (nmax_ready, _), (exp_done, _), (p_ready, _), (pt_done, _), (pt_ready, _), (pv_done, _), (o_ready, _) = (
        m.shared(n, PAIRS * B) for n in ("scores", "nmax_ready", "exp_done", "p_ready", "pt_done", "pt_ready", "pv_done", "o_ready"))
    (o_high, halves), (o_split, _) = m.shared("out_high", 4), m.shared("out_split", 4)
    out_done, outs = m.shared("out_done", TT - 1)
    SC, LIN, PTB, PV = (0, 5), 1, 6, 7
    QB = (5, 6, 7, 0)
    ps = m.ps
    first = lambda b, value: isinstance(b, int) and b == value

    def lhs(h, n, c):
        return h[:, n % RING_UNITS, c * P:(c + 1) * P]

    def tensor(pe):
        latents.tensor(pe)
        for n in range(KC):
            u = first_unit + n
            pe.wait_ge(m.unit_ready, u + 1)
            for c in range(KC):
                latents.wait_split(pe, c + 1)
                last = product(pe, ps[:, QB[n], :], (lhs(m.wh, u, c), lhs(m.wl, u, c)),
                               (xh[:, 1, c, :], xl[:, 1, c, :]), c == 0, c == KC - 1)
            last.then_inc(m.unit_done, 1)

        def linear(b, par, l, chunks):
            bank = ps[:, LIN + l % 4, :]
            if chunks[0] == 0 and l < 4 and not first(b, 0):
                pe.wait_ge(v_ready, vals + 4 * b + l - 3)
            elif chunks[0] == 0 and l >= 4:
                pe.wait_ge(kt_ready, 4 * b + l - 3)
            for c in chunks:
                if l == 0:
                    pe.wait_ge(ctx_split, KC * b + c + 1)
                x_c = (xh[:, par, c, :], xl[:, par, c, :])
                if l < 4:
                    u = first_unit + 4 + l
                    pe.wait_ge(m.unit_ready, u + 1)
                    last = product(pe, bank, (lhs(m.wh, u, c), lhs(m.wl, u, c)), x_c, c == 0, c == KC - 1)
                else:
                    u = first_unit + 8 + c
                    pe.wait_ge(m.unit_ready, u + 1)
                    t = slice((l - 4) * P, (l - 3) * P)
                    last = product(pe, bank, (x_c[0][:, t], x_c[1][:, t]),
                                   (m.wh[:, u % RING_UNITS, :], m.wl[:, u % RING_UNITS, :]), c == 0, c == KC - 1)
            if chunks[-1] == KC - 1:
                last.then_inc(lin_done, 1)

        def attention_scores(b, par, hp):
            if hp == 0:
                pe.wait_ge(staged, b + 1)
                pe.wait_ge(kt_ready, 4 * b + 4)
            if not (first(b, 0) and hp < 2):
                pe.wait_ge(exp_done, before + PAIRS * b + hp - 1)
            pe.matmul(ps[:, SC[hp % 2], :], q_pairs[:, par, hp // 2, hp % 2, :, :].rearrange("p e l -> p (e l)"),
                      kt[:, par, hp // 2, :], start=True, stop=True).then_inc(scores, 1)

        def probability_transposes(b, hp):
            pe.wait_ge(p_ready, before + PAIRS * b + hp + 1)
            if not (first(b, 0) and hp == 0):
                pe.wait_ge(pt_ready, before + PAIRS * b + hp)
            for t in range(TT):
                last = pe.transpose(ps[:, PTB, t * P:(t + 1) * P], p[:, hp % 2, t * P:(t + 1) * P], m.ident[:, :])
            last.then_inc(pt_done, 1)

        def values(b, par, hp):
            pe.wait_ge(pt_ready, before + PAIRS * b + hp + 1)
            pe.wait_ge(v_ready, vals + 4 * b + 4)
            if not (first(b, 0) and hp == 0):
                pe.wait_ge(o_ready, before + PAIRS * b + hp)
            for t in range(TT):
                last = pe.matmul(ps[:, PV, 0:P], v[:, par, t, (hp // 2) * P:(hp // 2 + 1) * P], pt[:, t, :],
                                 start=t == 0, stop=t == TT - 1)
            last.then_inc(pv_done, 1)

        def step(b, par, lin=True, att=True, carry=True):
            for hp in range(PAIRS):
                behind = (b - 1, 1 - par, hp - 1) if hp else (b - 2, par, PAIRS - 1)
                follow = att and (hp or carry)
                if att:
                    attention_scores(b - 1, 1 - par, hp)
                if lin:
                    linear(b, par, hp, range(0, 2))
                if follow:
                    probability_transposes(behind[0], behind[2])
                if lin:
                    linear(b, par, hp, range(2, 4))
                if follow:
                    values(*behind)

        latents.wait_split(pe, KC)
        step(0, 0, att=False)
        pe.wait_ge(q_ready, KC)
        step(1, 1, carry=False)
        with pe.Fori(1, B // 2) as i:
            step(2 * i, 0)
            step(2 * i + 1, 1)
        pe.wait_ge(lin_done, lins + 8 * B)
        pe.sem_inc(m.unit_done, 8)
        step(B, 0, lin=False)
        probability_transposes(B - 1, PAIRS - 1)
        values(B - 1, 1, PAIRS - 1)

        for c in range(KC):
            u = first_unit + 12 + c
            pe.wait_ge(m.unit_ready, u + 1)
            pe.wait_ge(o_split, halves + c + 1)
            for t in range(TT):
                last = product(pe, ps[:, LIN + t, :], (oh[:, c, t * P:(t + 1) * P], ol[:, c, t * P:(t + 1) * P]),
                               (m.wh[:, u % RING_UNITS, :], m.wl[:, u % RING_UNITS, :]), c == 0, c == KC - 1)
                if c == KC - 1 and t < TT - 1:
                    last.then_inc(out_done, 1)
            last.then_inc(m.unit_done, 1)

    def scalar(act):
        steps = m.act_steps
        act.wait_ge(m.x_loaded, 16)
        if k:
            act.wait_ge(m.x_ready, TT * k)
        for b in range(2):
            act.dma_start(ctx[:, b, :, :], m.d["ctx_columns"][b]).then_inc(ctx_loaded[b], 16)
        act.dma_start(bias[:, :], m.d["ca_bias"]).then_inc(bias_loaded, 16)
        latents.scalar_guess(act, steps)
        latents.scalar_high(act)

        def high(b, par, c):
            if c == 0:
                act.wait_ge(ctx_loaded[par], loads0 + 8 * (b - par) + 16)
                if not first(b, 0):
                    act.wait_ge(lin_done, lins + 8 * (b - 1))
            act.copy(xh[:, par, c, :], ctx[:, par, c, :]).then_inc(ctx_high, 1)

        def stage_queries(b, par):
            if first(b, 0):
                act.wait_ge(q_zero, 1)
                act.wait_ge(q_ready, KC)
            for h in range(4):
                part = slice(32 * h, 32 * h + 32)
                last = act.copy(q_pairs[part, par, :, h // 2, h % 2, :],
                                q[part, :, bass.ds(b, 1), :].rearrange("p c o l -> p c (o l)"))
            last.then_inc(staged, 1)

        def exponentials(b, hp):
            act.wait_ge(nmax_ready, before + PAIRS * b + hp + 1)
            act.activation(p[:, hp % 2, :], ps[:, SC[hp % 2], :], ACT.Exp, bias=nmax[:, hp % 2:hp % 2 + 1],
                           accum_out=rsum[:, hp % 2:hp % 2 + 1]).then_inc(exp_done, 1)

        def transposed(b, hp):
            act.wait_ge(pt_done, before + PAIRS * b + hp + 1)
            if not (first(b, 0) and hp == 0):
                act.wait_ge(pv_done, before + PAIRS * b + hp)
            act.copy(pt[:, :, :].rearrange("p t n -> p (t n)"), ps[:, PTB, :]).then_inc(pt_ready, 1)

        def output(b, hp):
            act.wait_ge(pv_done, before + PAIRS * b + hp + 1)
            for e in range(2):
                part = slice(64 * (hp % 2) + 32 * e, 64 * (hp % 2) + 32 * e + 32)
                last = act.copy(o[part, hp // 2, bass.ds(b * L, L)], ps[part, PV, 64 * e:64 * e + 64])
            last.then_inc(o_ready, 1)

        def step(b, par, lin=True, att=True, carry=True, nxt=True):
            for hp in range(PAIRS):
                behind = (b - 1, hp - 1) if hp else (b - 2, PAIRS - 1)
                follow = att and (hp or carry)
                if att:
                    exponentials(b - 1, hp)
                if follow:
                    transposed(*behind)
                if lin and hp >= 4:
                    t = hp - 4
                    act.wait_ge(lin_done, lins + 8 * b + 5 + t)
                    act.copy(v[:, par, t, :], ps[:, LIN + t, :]).then_inc(v_ready, 1)
                if follow:
                    output(*behind)
                if nxt and hp % 2:
                    high(b + 1, 1 - par, hp // 2)
            if lin:
                stage_queries(b, par)

        for c in range(KC):
            high(0, 0, c)
        for n in range(KC):
            act.wait_ge(m.unit_done, first_unit + n + 1)
            act.activation(q[:, n, :, :].rearrange("p b l -> p (b l)"), ps[:, QB[n], :], ACT.Copy, scale=SCALE)\
               .then_inc(q_ready, 1)
        step(0, 0, att=False)
        step(1, 1, carry=False)
        with act.Fori(1, B // 2 - 1) as i:
            step(2 * i, 0)
            step(2 * i + 1, 1)
        step(B - 2, 0)
        step(B - 1, 1, nxt=False)
        step(B, 0, lin=False, nxt=False)
        transposed(B - 1, PAIRS - 1)
        output(B - 1, PAIRS - 1)
        act.wait_ge(o_ready, before + PAIRS * B)
        for c in range(KC):
            act.copy(oh[:, c, :], o[:, c, :]).then_inc(o_high, 1)

    def vector(dve):
        steps = m.dve_steps
        latents.vector_rows(dve, steps)
        dve.memset(q_pairs[:, :, :, :, :, :].rearrange("p s c r e l -> p (s c r e l)"), 0.0).then_inc(q_zero, 1)
        latents.vector_low(dve)

        def low(b, par, c):
            dve.wait_ge(ctx_high, KC * b + c + 1)
            dve.tensor_tensor(xl[:, par, c, :], ctx[:, par, c, :], f32(xh[:, par, c, :]), ALU.subtract)\
               .then_inc(ctx_split, 1)

        def softmax(b, hp):
            slot = slice(hp % 2, hp % 2 + 1)
            dve.wait_ge(scores, before + PAIRS * b + hp + 1)
            dve.tensor_reduce(nmax[:, slot], ps[:, SC[hp % 2], :], AX.X, ALU.max, negate=True).then_inc(nmax_ready, 1)
            dve.wait_ge(exp_done, before + PAIRS * b + hp + 1)
            steps.done(dve.reciprocal(rinv[:, slot], rsum[:, slot]))
            dve.tensor_scalar(p[:, hp % 2, :], p[:, hp % 2, :], rinv[:, slot], None, ALU.mult).then_inc(p_ready, 1)

        def step(b, par, lin=True, att=True, nxt=True):
            for hp in range(PAIRS):
                if att:
                    softmax(b - 1, hp)
                if lin and hp < 4:
                    dve.wait_ge(lin_done, lins + 8 * b + hp + 1)
                    dve.tensor_copy(kt[:, par, hp, :], ps[:, LIN + hp, :]).then_inc(kt_ready, 1)
                if nxt and hp % 2:
                    low(b + 1, 1 - par, hp // 2)

        for c in range(KC):
            low(0, 0, c)
        dve.wait_ge(bias_loaded, 16)
        latents.wait_rows(dve)
        for t in range(TT):
            steps.mark(dve.tensor_tensor(m.x[:, t, :], m.x[:, t, :], bias[:, :], ALU.add))
        steps.wait()
        step(0, 0, att=False)
        step(1, 1)
        with dve.Fori(1, B // 2 - 1) as i:
            steps.enter(i - 1, 16)
            step(2 * i, 0)
            step(2 * i + 1, 1)
            steps.leave(B // 2 - 2)
        step(B - 2, 0)
        step(B - 1, 1, nxt=False)
        step(B, 0, lin=False, nxt=False)
        for c in range(KC):
            dve.wait_ge(o_high, halves + c + 1)
            dve.tensor_tensor(ol[:, c, :], o[:, c, :], f32(oh[:, c, :]), ALU.subtract).then_inc(o_split, 1)
        for t in range(TT):
            if t < TT - 1:
                dve.wait_ge(out_done, outs + t + 1)
            else:
                dve.wait_ge(m.unit_done, first_unit + 16)
            dve.tensor_tensor(m.x[:, t, :], m.x[:, t, :], ps[:, LIN + t, :], ALU.add).then_inc(m.x_ready, 1)

    def loads(sp):
        with sp.Fori(1, B // 2) as i:
            for par in range(2):
                b = 2 * i + par
                sp.wait_ge(ctx_split, KC * (b - 1))
                sp.dma_start(ctx[:, par, :, :], m.d["ctx_columns"][bass.ds(b, 1)].rearrange("o p c n -> (o p) c n"))\
                  .then_inc(ctx_loaded[par], 16)

    return tensor, scalar, vector, loads


def linear_attention(nc, m, first_unit, k):
    HEADS, HD, FEATURES = 16, 32, 64
    PAIRS = HEADS // 2
    GROUP = 3
    GROUPS = (HEADS + GROUP - 1) // GROUP
    with ExitStack() as mem:
        sb = lambda name, shape, dt=F32: mem.enter_context(nc.sbuf_tensor("li_" + name, shape, dt))
        rows = sb("rows", [P, TT, D])
        xh, xl = sb("xh", [P, KC, T], F32R), sb("xl", [P, KC, T], F32R)
        qk = sb("qk", [P, 2, KC, T])
        feat = sb("feat", [P, 2, PAIRS, T])
        v = sb("v", [P, TT, HEADS, HD + 1])
        masked = sb("masked", [P, 2, TT, P])
        proj = sb("proj", [P, KC, 2, P])
        causal = sb("causal", [P, P])
        v_bias, out_bias = sb("v_bias", [P, D]), sb("out_bias", [P, D])
        small = sb("small", [P, 80])
    qk_bias = small[:, 44:52]
    inv = small[:, 52:52 + GROUP * TT].rearrange("p (h t) -> p h t", t=TT)
    latents = NormalizedColumns(m, k, rows, small, xh, xl, 0)
    s = lambda name: m.sem("li_" + name)
    consts, loaded = m.shared("stage_consts", 4 * 16)
    proj_zero, proj_loaded, ones_ready = s("proj_zero"), s("proj_loaded"), s("ones_ready")
    q_ready, k_ready, v_done, v_ready = s("q_ready"), s("k_ready"), s("v_done"), s("v_ready")
    feat_done, fq_ready, fk_ready = s("feat_done"), s("fq_ready"), s("fk_ready")
    scores, mask_done, group_done, rows_out = s("scores"), s("mask_done"), s("group_done"), s("rows_out")
    o_turned = s("o_turned")
    (o_high, halves), (o_split, _) = m.shared("out_high", 4), m.shared("out_split", 4)
    out_done, outs = m.shared("out_done", TT - 1)
    QB, KB, VB, FB, SB, CB, OT, OB = 4, 0, 4, 0, 0, 2, 0, 4
    ps = m.ps

    def tensor(pe):
        latents.tensor(pe)
        for j, bank in enumerate((QB, KB)):
            for n in range(KC):
                u = first_unit + 4 * j + n
                pe.wait_ge(m.unit_ready, u + 1)
                at = u % RING_UNITS
                for c in range(KC):
                    latents.wait_split(pe, c + 1)
                    last = product(pe, ps[:, bank + n, :], (m.wh[:, at, c * P:(c + 1) * P], m.wl[:, at, c * P:(c + 1) * P]),
                                   (xh[:, c, :], xl[:, c, :]), c == 0, c == KC - 1)
                last.then_inc(m.unit_done, 1)
        for c in range(KC):
            u = first_unit + 8 + c
            pe.wait_ge(m.unit_ready, u + 1)
            for t in range(TT):
                if c == 0:
                    pe.wait_ge(q_ready, t + 1)
                last = product(pe, ps[:, VB + t, :], (xh[:, c, t * P:(t + 1) * P], xl[:, c, t * P:(t + 1) * P]),
                               (m.wh[:, u % RING_UNITS, :], m.wl[:, u % RING_UNITS, :]), c == 0, c == KC - 1)
            last.then_inc(m.unit_done, 1)
        pe.wait_ge(proj_loaded, 4 * 16)
        pe.wait_ge(q_ready, KC)
        pe.wait_ge(k_ready, KC)
        for pair in range(PAIRS):
            if pair >= 2:
                pe.wait_ge(fq_ready, pair - 1)
                pe.wait_ge(fk_ready, pair - 1)
            for j in range(2):
                pe.matmul(ps[:, FB + 2 * (pair % 2) + j, :], proj[:, pair // 2, pair % 2, :], qk[:, j, pair // 2, :],
                          start=True, stop=True).then_inc(feat_done, 1)
        pe.wait_ge(fq_ready, PAIRS)
        pe.wait_ge(fk_ready, PAIRS)
        pe.wait_ge(v_ready, TT)
        pe.wait_ge(ones_ready, 1)

        def context(h):
            pe.wait_ge(mask_done, h + 1)
            for t in range(TT):
                at = ((h % GROUP) * TT + t) * (HD + 1)
                last = pe.matmul(ps[:, CB + h // GROUP, at:at + HD + 1], masked[:, h % 2, t, :], v[:, t, h, :],
                                 start=True, stop=True)
            last.then_inc(group_done, 1)

        for h in range(HEADS):
            part = slice(FEATURES * (h % 2), FEATURES * (h % 2) + FEATURES)
            if h >= 2:
                pe.wait_ge(mask_done, h - 1)
            for t in range(TT):
                tok = slice(t * P, (t + 1) * P)
                last = pe.matmul(ps[:, SB + h % 2, tok], feat[part, 1, h // 2, tok], feat[part, 0, h // 2, tok],
                                 start=True, stop=True)
            last.then_inc(scores, 1)
            if h:
                context(h - 1)
        context(HEADS - 1)
        pe.wait_ge(rows_out, GROUPS)
        for c in range(KC):
            for t in range(TT):
                last = pe.transpose(ps[:, OT + c, t * P:(t + 1) * P], rows[:, t, c * P:(c + 1) * P], m.ident[:, :])
            last.then_inc(o_turned, 1)
        for c in range(KC):
            u = first_unit + 12 + c
            pe.wait_ge(m.unit_ready, u + 1)
            pe.wait_ge(o_split, halves + c + 1)
            for t in range(TT):
                last = product(pe, ps[:, OB + t, :], (xh[:, c, t * P:(t + 1) * P], xl[:, c, t * P:(t + 1) * P]),
                               (m.wh[:, u % RING_UNITS, :], m.wl[:, u % RING_UNITS, :]), c == 0, c == KC - 1)
                if c == KC - 1 and t < TT - 1:
                    last.then_inc(out_done, 1)
            last.then_inc(m.unit_done, 1)

    def scalar(act):
        steps = m.act_steps
        act.wait_ge(m.x_loaded, 16)
        if k:
            act.wait_ge(m.x_ready, TT * k)
        for out, src in ((causal[:, :], m.d["causal"]), (v_bias[:, :], m.d["v_bias"]), (out_bias[:, :], m.d["li_bias"]),
                         (qk_bias, m.d["qk_bias"])):
            act.dma_start(out, src).then_inc(consts, 16)
        act.wait_ge(proj_zero, 1)
        for h in range(4):
            act.dma_start(proj[32 * h:32 * h + 32, :, h // 2, 64 * (h % 2):64 * (h % 2) + 64], m.d["proj"][h])\
               .then_inc(proj_loaded, 16)
        latents.scalar_guess(act, steps)
        latents.scalar_high(act)
        act.wait_ge(consts, loaded + 4 * 16)
        for n in range(KC):
            act.wait_ge(m.unit_done, first_unit + n + 1)
            act.activation(qk[:, 0, n, :], ps[:, QB + n, :], ACT.Identity, bias=qk_bias[:, n:n + 1]).then_inc(q_ready, 1)
        for pair in range(PAIRS):
            act.wait_ge(feat_done, 2 * pair + 1)
            act.activation(feat[:, 0, pair, :], ps[:, FB + 2 * (pair % 2), :], ACT.Relu).then_inc(fq_ready, 1)
        for c in range(KC):
            act.wait_ge(o_turned, c + 1)
            act.copy(xh[:, c, :], ps[:, OT + c, :]).then_inc(o_high, 1)

    def vector(dve):
        steps = m.dve_steps
        dve.wait_ge(m.x_loaded, 16)
        if k:
            dve.wait_ge(m.x_ready, TT * k)
        dve.memset(proj[:, :, :, :].rearrange("p c r n -> p (c r n)"), 0.0).then_inc(proj_zero, 1)
        latents.vector_rows(dve, steps)
        dve.memset(v[:, :, :, HD:HD + 1], 1.0).then_inc(ones_ready, 1)
        latents.vector_low(dve)
        dve.wait_ge(consts, loaded + 4 * 16)
        latents.wait_rows(dve)
        for t in range(TT):
            steps.mark(dve.tensor_tensor(m.x[:, t, :], m.x[:, t, :], out_bias[:, :], ALU.add))
        steps.wait()
        for n in range(KC):
            dve.wait_ge(m.unit_done, first_unit + 4 + n + 1)
            dve.tensor_scalar(qk[:, 1, n, :], ps[:, KB + n, :], qk_bias[:, 4 + n:5 + n], None, ALU.add).then_inc(k_ready, 1)
        dve.wait_ge(m.unit_done, first_unit + 12)
        by_head = lambda ap: ap.rearrange("p (h d) -> p h d", d=HD)
        for t in range(TT):
            dve.tensor_tensor(v[:, t, :, 0:HD], by_head(ps[:, VB + t, :]), by_head(v_bias[:, :]), ALU.add).then_inc(v_ready, 1)
        for pair in range(PAIRS):
            dve.wait_ge(feat_done, 2 * pair + 2)
            dve.tensor_scalar(feat[:, 1, pair, :], ps[:, FB + 2 * (pair % 2) + 1, :], 0.0, None, ALU.max).then_inc(fk_ready, 1)

        def divide(g):
            h0, h1 = g * GROUP, min((g + 1) * GROUP, HEADS)
            n = h1 - h0
            dve.wait_ge(group_done, h1)
            if g:
                dve.wait_ge(rows_out, g)
            out = ps[:, CB + g, 0:n * TT * (HD + 1)].rearrange("p (h t d) -> p h t d", h=n, t=TT)
            steps.done(dve.tensor_scalar(inv[:, 0:n, :], out[:, :, :, HD], 1e-6, None, ALU.add))
            steps.done(dve.reciprocal(inv[:, 0:n, :], inv[:, 0:n, :]))
            for t in range(TT):
                last = dve.tensor_tensor(by_head(rows[:, t, h0 * HD:h1 * HD]), out[:, :, t, 0:HD],
                                         inv[:, 0:n, t:t + 1].to_broadcast([P, n, HD]), ALU.mult)
            last.then_inc(rows_out, 1)

        for h in range(HEADS):
            dve.wait_ge(scores, h + 1)
            if h >= 2:
                dve.wait_ge(group_done, h - 1)
            dve.tensor_tensor(masked[:, h % 2, :, :], ps[:, SB + h % 2, :].rearrange("p (t n) -> p t n", t=TT),
                              causal[:, :].rearrange("p (o n) -> p o n", o=1).to_broadcast([P, TT, P]), ALU.mult)\
               .then_inc(mask_done, 1)
            if h % GROUP == 1 and h > GROUP:
                divide(h // GROUP - 1)
        for g in range((HEADS - 1) // GROUP - 1, GROUPS):
            divide(g)
        for c in range(KC):
            dve.wait_ge(o_high, halves + c + 1)
            dve.tensor_tensor(xl[:, c, :], ps[:, OT + c, :], f32(xh[:, c, :]), ALU.subtract).then_inc(o_split, 1)
        for t in range(TT):
            if t < TT - 1:
                dve.wait_ge(out_done, outs + t + 1)
            else:
                dve.wait_ge(m.unit_done, first_unit + 16)
            dve.tensor_tensor(m.x[:, t, :], m.x[:, t, :], ps[:, OB + t, :], ALU.add).then_inc(m.x_ready, 1)

    return tensor, scalar, vector, None


def experts(nc, m, first_unit, k):
    E, F = 8, 1024
    NF = F // P
    LIMIT, ALPHA = 9.0, 1.702
    with ExitStack() as mem:
        sb = lambda name, shape, dt=F32: mem.enter_context(nc.sbuf_tensor("ex_" + name, shape, dt))
        xh, xl = sb("xh", [P, KC, T], F32R), sb("xl", [P, KC, T], F32R)
        hh, hl = sb("hh", [P, NF, T], F32R), sb("hl", [P, NF, T], F32R)
        rows = sb("rows", [P, TT, D])
        g, u, sg, h = sb("g", [P, 2, T]), sb("u", [P, 2, T]), sb("sg", [P, 2, T]), sb("h", [P, 2, T])
        b1 = sb("b1", [P, E, NF, 2])
        b2 = sb("b2", [E, D])
        gw_raw = sb("gw_raw", [P, KC, E])
        gwh, gwl = sb("gwh", [P, KC, E], F32R), sb("gwl", [P, KC, E], F32R)
        before = sb("before", [P, E, E])
        small = sb("small", [P, 44])
        gates, rank, best, second, coef = (sb(n, [P, TT, E]) for n in ("gates", "rank", "best", "second", "coef"))
        greater, equal = sb("greater", [P, TT, E, E]), sb("equal", [P, TT, E, E])
        v1, v2, w1, w2 = (sb(n, [P, TT]) for n in ("v1", "v2", "w1", "w2"))
        coef_t = sb("coef_t", [E, T])
    s = lambda name: m.sem("ex_" + name)
    consts, loaded = m.shared("stage_consts", 4 * 16)
    ln = NormalizedColumns(m, k, rows, small, xh, xl, 1)
    gw_split, gates_done, diff_ready, diff_exp = (s(n) for n in ("gw_split", "gates_done", "diff_ready", "diff_exp"))
    coef_ready, coef_turned, coef_t_ready, bias_done, bias_added = (
        s(n) for n in ("coef_ready", "coef_turned", "coef_t_ready", "bias_done", "bias_added"))
    g_ready, u_ready, sg_ready, h_ready, h_high, h_split = (
        s(n) for n in ("g_ready", "u_ready", "sg_ready", "h_ready", "h_high", "h_split"))
    tile_done, added = s("tile_done"), s("added")
    LIN, OUT, GATE = 1, (0, 5, 6, 7), 5
    ps = m.ps

    def tensor(pe):
        ln.tensor(pe)
        ln.wait_split(pe, KC)
        pe.wait_ge(gw_split, 1)
        for t in range(TT):
            for c in range(KC):
                cols = slice(t * P, (t + 1) * P)
                last = product(pe, ps[:, GATE, t * E:(t + 1) * E], (xh[:, c, cols], xl[:, c, cols]),
                               (gwh[:, c, :], gwl[:, c, :]), c == 0, c == KC - 1)
        last.then_inc(gates_done, 1)
        pe.wait_ge(coef_ready, 1)
        for t in range(TT):
            last = pe.transpose(ps[0:E, 6, t * P:(t + 1) * P], coef[:, t, :], m.ident[:, :])
        last.then_inc(coef_turned, 1)
        pe.wait_ge(coef_t_ready, 1)
        for t in range(TT):
            pe.matmul(ps[:, OUT[t], :], coef_t[:, t * P:(t + 1) * P], b2[:, :], start=True, stop=True).then_inc(bias_done, 1)

        def expert(e, is_first):
            for n in range(2 * NF):
                u0 = first_unit + n
                bank = LIN + n % 4
                pe.wait_ge(m.unit_ready, first_unit + 24 * e + (n + 1))
                if n >= 4 or not is_first:
                    pe.wait_ge((g_ready, u_ready)[n % 2], 8 * e + (n // 2 - 1))
                for c in range(KC):
                    w = (m.wh[:, u0 % RING_UNITS, c * P:(c + 1) * P], m.wl[:, u0 % RING_UNITS, c * P:(c + 1) * P])
                    last = product(pe, ps[:, bank, :], w, (xh[:, c, :], xl[:, c, :]), c == 0, c == KC - 1)
                last.then_inc(m.unit_done, 1)
            for n in range(NF):
                at = 2 * NF + n
                slot = (first_unit + at) % RING_UNITS
                pe.wait_ge(m.unit_ready, first_unit + 24 * e + (at + 1))
                pe.wait_ge(h_split, 8 * e + (n + 1))
                for t in range(TT):
                    if n == 0:
                        if is_first:
                            pe.wait_ge(bias_added, t + 1)
                        else:
                            pe.wait_ge(added, 4 * e + (t - 3))
                    cols = slice(t * P, (t + 1) * P)
                    last = product(pe, ps[:, OUT[t], :], (hh[:, n, cols], hl[:, n, cols]),
                                   (m.wh[:, slot, :], m.wl[:, slot, :]), n == 0, n == NF - 1)
                    if n == NF - 1 and t < TT - 1:
                        last.then_inc(tile_done, 1)
                last.then_inc(m.unit_done, 1)

        expert(0, True)
        with pe.Fori(1, E) as e:
            expert(e, False)

    def scalar(act):
        steps = m.act_steps
        act.wait_ge(m.x_loaded, 16)
        if k:
            act.wait_ge(m.x_ready, TT * k)
        for out, src in ((b1[:, :, :, :], m.d["expert_b1"]), (b2[:, :], m.d["expert_b2"]), (gw_raw[:, :, :], m.d["gate_w"]),
                         (before[:, :, :], m.d["before"])):
            act.dma_start(out, src).then_inc(consts, 16)
        ln.scalar_guess(act, steps)
        ln.scalar_high(act)
        act.wait_ge(diff_ready, 1)
        act.activation(w2[:, :], v2[:, :], ACT.Exp).then_inc(diff_exp, 1)
        act.wait_ge(coef_turned, 1)
        act.copy(coef_t[:, :], ps[0:E, 6, :]).then_inc(coef_t_ready, 1)

        def expert(e, is_first):
            for n in range(NF + 1):
                if n < NF:
                    act.wait_ge(m.unit_done, first_unit + 24 * e + (2 * n + 2))
                    if n >= 2 or not is_first:
                        act.wait_ge(h_ready, 8 * e + (n - 1))
                    act.activation(u[:, n % 2, :], ps[:, LIN + (2 * n + 1) % 4, :], ACT.Identity,
                                   bias=b1[:, bass.ds(e, 1), n, 1:2].rearrange("p o n -> p (o n)")).then_inc(u_ready, 1)
                    act.wait_ge(g_ready, 8 * e + (n + 1))
                    act.activation(sg[:, n % 2, :], g[:, n % 2, :], ACT.Sigmoid, scale=ALPHA).then_inc(sg_ready, 1)
                if n:
                    act.wait_ge(h_ready, 8 * e + n)
                    act.copy(hh[:, n - 1, :], h[:, (n - 1) % 2, :]).then_inc(h_high, 1)

        expert(0, True)
        with act.Fori(1, E) as e:
            expert(e, False)

    def vector(dve):
        steps = m.dve_steps
        if k:
            dve.wait_ge(m.x_ready, TT * k)
        ln.vector_rows(dve, steps)
        dve.wait_ge(consts, loaded + 4 * 16)
        steps.done(dve.tensor_copy(gwh[:, :, :], gw_raw[:, :, :]))
        dve.tensor_tensor(gwl[:, :, :], gw_raw[:, :, :], f32(gwh[:, :, :]), ALU.subtract).then_inc(gw_split, 1)
        ln.vector_low(dve)
        dve.wait_ge(gates_done, 1)
        steps.done(dve.tensor_copy(gates[:, :, :].rearrange("p t e -> p (t e)"), ps[:, GATE, 0:TT * E]))
        of_e = gates[:, :, :].unsqueeze(3).to_broadcast([P, TT, E, E])
        of_f = gates[:, :, :].unsqueeze(2).to_broadcast([P, TT, E, E])
        steps.mark(dve.tensor_tensor(greater[:, :, :, :], of_f, of_e, ALU.is_gt))
        steps.done(dve.tensor_tensor(equal[:, :, :, :], of_f, of_e, ALU.is_equal))
        flat = lambda ap: ap.rearrange("p t e f -> p t (e f)")
        steps.done(dve.tensor_tensor(flat(equal[:, :, :, :]), flat(equal[:, :, :, :]),
                                     before[:, :, :].rearrange("p e f -> p (e f)").unsqueeze(1).to_broadcast([P, TT, E * E]), ALU.mult))
        steps.done(dve.tensor_tensor(flat(greater[:, :, :, :]), flat(greater[:, :, :, :]), flat(equal[:, :, :, :]), ALU.add))
        steps.done(dve.tensor_reduce(rank[:, :, :], greater[:, :, :, :], AX.X, ALU.add))
        steps.mark(dve.tensor_scalar(best[:, :, :], rank[:, :, :], 0.0, None, ALU.is_equal))
        steps.mark(dve.tensor_scalar(second[:, :, :], rank[:, :, :], 1.0, None, ALU.is_equal))
        steps.mark(dve.tensor_reduce(v1[:, :], gates[:, :, :], AX.X, ALU.max))
        steps.wait()
        steps.done(dve.tensor_tensor(coef[:, :, :], gates[:, :, :], second[:, :, :], ALU.mult))
        steps.done(dve.tensor_reduce(v2[:, :], coef[:, :, :], AX.X, ALU.add))
        dve.tensor_tensor(v2[:, :], v2[:, :], v1[:, :], ALU.subtract).then_inc(diff_ready, 1)
        dve.wait_ge(diff_exp, 1)
        steps.done(dve.tensor_scalar(w1[:, :], w2[:, :], 1.0, None, ALU.add))
        steps.done(dve.reciprocal(w1[:, :], w1[:, :]))
        steps.mark(dve.tensor_tensor(w2[:, :], w2[:, :], w1[:, :], ALU.mult))
        spread = lambda ap: ap.unsqueeze(2).to_broadcast([P, TT, E])
        steps.done(dve.tensor_tensor(best[:, :, :], best[:, :, :], spread(w1[:, :]), ALU.mult))
        steps.done(dve.tensor_tensor(second[:, :, :], second[:, :, :], spread(w2[:, :]), ALU.mult))
        dve.tensor_tensor(coef[:, :, :], best[:, :, :], second[:, :, :], ALU.add).then_inc(coef_ready, 1)
        for t in range(TT):
            dve.wait_ge(bias_done, t + 1)
            dve.tensor_tensor(m.x[:, t, :], m.x[:, t, :], ps[:, OUT[t], :], ALU.add).then_inc(bias_added, 1)

        def expert(e, is_first):
            for n in range(NF + 1):
                if n < NF:
                    s0 = n % 2
                    dve.wait_ge(m.unit_done, first_unit + 24 * e + (2 * n + 1))
                    if n or not is_first:
                        steps.wait()
                    dve.tensor_scalar(g[:, s0, :], ps[:, LIN + (2 * n) % 4, :], b1[:, bass.ds(e, 1), n, 0:1].rearrange("p o n -> p (o n)"),
                                      LIMIT, ALU.add, ALU.min).then_inc(g_ready, 1)
                    dve.wait_ge(u_ready, 8 * e + (n + 1))
                    steps.mark(dve.tensor_scalar(u[:, s0, :], u[:, s0, :], LIMIT, -LIMIT, ALU.min, ALU.max))
                    dve.wait_ge(sg_ready, 8 * e + (n + 1))
                    steps.done(dve.tensor_tensor(g[:, s0, :], g[:, s0, :], sg[:, s0, :], ALU.mult))
                    if n >= 2 or not is_first:
                        dve.wait_ge(h_split, 8 * e + (n - 1))
                    dve.scalar_tensor_tensor(h[:, s0, :], u[:, s0, :], 1.0, g[:, s0, :], ALU.add, ALU.mult).then_inc(h_ready, 1)
                if n:
                    dve.wait_ge(h_high, 8 * e + n)
                    dve.tensor_tensor(hl[:, n - 1, :], h[:, (n - 1) % 2, :], f32(hh[:, n - 1, :]), ALU.subtract).then_inc(h_split, 1)
            for t in range(TT):
                if t < TT - 1:
                    dve.wait_ge(tile_done, 3 * e + (t + 1))
                else:
                    dve.wait_ge(m.unit_done, first_unit + 24 * e + 24)
                dve.scalar_tensor_tensor(m.x[:, t, :], ps[:, OUT[t], :], coef[:, t, bass.ds(e, 1)], m.x[:, t, :], ALU.mult, ALU.add)\
                   .then_inc(added, 1)

        expert(0, True)
        with dve.Fori(1, E) as e:
            steps.enter(e - 1, 16)
            expert(e, False)
            steps.leave(E - 1)
        dve.wait_ge(added, TT * E)
        dve.sem_inc(m.x_ready, TT)

    return tensor, scalar, vector, None


class Memory:

    def __init__(self):
        self.sems = {}

    def shared(self, name, raised):
        if name not in self.sems:
            self.sems[name] = [self.sem(name), 0]
        sem, before = self.sems[name]
        self.sems[name][1] += raised
        return sem, before


def program(nc, d, out, stages):
    m = Memory()
    m.d = d
    n_blocks = sum(STAGE_BLOCKS[name] for name, _ in stages)
    with ExitStack() as whole:
        sb = lambda name, shape, dt=F32: whole.enter_context(nc.sbuf_tensor(name, shape, dt))
        m.sem = lambda name: whole.enter_context(nc.semaphore(name))
        m.x = sb("x_rows", [P, TT, D])
        m.ident = sb("ident", [P, P])
        m.wh, m.wl = sb("w_high", [P, RING_UNITS, 512], F32R), sb("w_low", [P, RING_UNITS, 512], F32R)
        w_raw = sb("w_raw", [P, 2, 4, 512])
        one, one_ready = sb("one", [P, 1]), m.sem("one_ready")
        m.ps = whole.enter_context(nc.psum_tensor("ps", [P, 8, 512], F32))
        m.consts, m.x_loaded, m.x_ready = m.sem("consts"), m.sem("x_loaded"), m.sem("x_ready")
        raw_loaded = [m.sem("raw_loaded0"), m.sem("raw_loaded1")]
        unit_high, m.unit_ready, m.unit_done = m.sem("unit_high"), m.sem("unit_ready"), m.sem("unit_done")
        stored = m.sem("stored")
        act_steps, dve_steps = m.sem("act_steps"), m.sem("dve_steps")
        first, made = 0, []
        for k, (name, stage) in enumerate(stages):
            made.append((first, STAGE_BLOCKS[name], stage(nc, m, 4 * first, k)))
            first += STAGE_BLOCKS[name]
        block = whole.enter_context(nc.Block())

        @block.sync
        def _(sp):
            def load_block(n, slot):
                if not isinstance(n, int) or n >= 2:
                    sp.wait_ge(m.unit_ready, 4 * (n - 1))
                sp.dma_start(w_raw[:, slot, :, :], d["weights"][bass.ds(n, 1)].rearrange("o p u n -> (o p) u n"))\
                  .then_inc(raw_loaded[slot], 16)

            sp.dma_start(m.x[:, :, :], d["x"]).then_inc(m.x_loaded, 16)
            sp.dma_start(m.ident[:, :], d["ident"]).then_inc(m.consts, 16)
            done = 0
            for first, count, (_, _, _, loads) in made:
                last = min(first + count + (1 if count else 0), n_blocks)
                while done < min(2, last):
                    load_block(done, done)
                    done += 1
                if last - done > 4:
                    if done % 2:
                        load_block(done, 1)
                        done += 1
                    with sp.Fori(done // 2, last // 2) as i:
                        load_block(2 * i, 0)
                        load_block(2 * i + 1, 1)
                    done = last // 2 * 2
                for n in range(done, last):
                    load_block(n, n % 2)
                done = max(done, last)
                if loads:
                    loads(sp)
            sp.wait_ge(m.x_ready, TT * len(stages))
            sp.dma_start(out, m.x[:, :, :]).then_inc(stored, 16)
            sp.wait_ge(stored, 16)

        @block.gpsimd
        def _(pool):
            def split(pair, first_pair):
                for slot in range(2):
                    pool.wait_ge(raw_loaded[slot], 16 * (pair + 1))
                    for u in range(4):
                        n, at = 8 * pair + 4 * slot + u, 4 * slot + u
                        if not first_pair:
                            pool.wait_ge(m.unit_done, n - 7)
                        pool.tensor_tensor(m.wh[:, at, :], w_raw[:, slot, u, :], one[:, :].to_broadcast([P, 512]), ALU.mult).then_inc(unit_high, 1)
                        pool.wait_ge(unit_high, n + 1)
                        pool.tensor_tensor(m.wl[:, at, :], w_raw[:, slot, u, :], f32(m.wh[:, at, :]), ALU.subtract)\
                            .then_inc(m.unit_ready, 1)

            pool.memset(one[:, :], 1.0).then_inc(one_ready, 1)
            pool.wait_ge(one_ready, 1)
            if n_blocks:
                split(0, True)
            if n_blocks > 2:
                with pool.Fori(1, n_blocks // 2) as i:
                    split(i, False)

        @block.scalar
        def _(act):
            m.act_steps = Steps(act, act_steps)
            for _, _, (_, scalar, _, _) in made:
                scalar(act)

        @block.vector
        def _(dve):
            m.dve_steps = Steps(dve, dve_steps)
            for _, _, (_, _, vector, _) in made:
                vector(dve)

        @block.tensor
        def _(pe):
            for _, _, (tensor, _, _, _) in made:
                tensor(pe)


STAGES = (("latent_attention", latent_attention), ("oscillator", oscillator), ("bit_ffn", bit_ffn),
          ("context_attention", context_attention), ("linear_attention", linear_attention), ("experts", experts))


def columns_unit(w):
    k, n = w.shape
    return w.reshape(k // 128, 128, n // 512, 4, 128).transpose(2, 1, 3, 0, 4).reshape(n // 512, 128, 4, k)


def rows_unit(w):
    return w.reshape(-1, 4, 128, 512).transpose(0, 2, 1, 3)


def per_partition(v):
    return np.ascontiguousarray(v.reshape(-1, 128).T)


def lay_out(i):
    i = {k: np.asarray(v) for k, v in i.items()}
    d = {"x": i["x"].reshape(4, 128, 512).transpose(1, 0, 2), "ident": np.eye(128, dtype=np.float32)}
    blocks = []
    at = np.arange(128)
    halves = np.arange(512).reshape(2, 4, 2, 32).transpose(2, 0, 1, 3).reshape(512)
    wkv = i["L0_xattn_Wkv"]
    blocks += [columns_unit(i["L0_xattn_Wq"][:, halves]), columns_unit(wkv[:, :512][:, halves]),
               rows_unit(wkv[:, 512:]), rows_unit(i["L0_xattn_Wo"])]
    d["ctx_rows"] = i["ctx_1024"].reshape(8, 4, 128, 512).transpose(0, 2, 1, 3)
    for name in ("gamma_x", "beta_x", "gamma_l", "beta_l"):
        d[name] = per_partition(i["L0_xattn_" + name])
    freq = (1.0 / np.float32(10000.0) ** (np.arange(0, 64, 2, dtype=np.float32) / np.float32(64))).astype(np.float32)
    angle = np.tile(freq[:, None] * np.arange(512, dtype=np.float32)[None, :], (4, 1))
    d["rope_cos"], d["rope_sin"] = np.cos(angle), np.sin(angle)
    w_in, w_bc = i["L0_attn_W_in"], i["L0_attn_W_bc"]
    bc = w_bc.reshape(8, 4, 4, 32, 8, 128).transpose(0, 5, 2, 4, 1, 3).reshape(8, 128, 2, 4, 512)
    blocks += [columns_unit(w_in[1024:2048].T), columns_unit(w_in[:1024].T),
               bc.transpose(0, 2, 1, 3, 4).reshape(16, 128, 4, 512), rows_unit(i["L0_attn_W_out"].T)]
    params = w_in[2048:].reshape(32, 2, 512).transpose(1, 0, 2).reshape(64, 512)
    d["w_params"] = np.concatenate([params, params]).T.reshape(4, 128, 128).transpose(1, 0, 2)
    d["conv_w"] = i["L0_attn_dw_weight"].reshape(8, 128, 4).transpose(1, 0, 2)
    d["conv_b"], d["skip"] = per_partition(i["L0_attn_dw_bias"]), per_partition(i["L0_attn_skip"])
    d["a_log"] = i["L0_attn_A_log"].reshape(8, 4, 32).transpose(1, 2, 0).reshape(128, 8)
    d["dt_bias"] = i["L0_attn_dt_bias"][:, None]
    select = np.zeros((128, 16, 128), np.float32)
    for n in range(16):
        for p in range(128):
            select[32 * (n // 8) + 4 * (n % 8) + p // 32, n, p] = 1
    d["select"] = select
    d["causal"] = ((at[:, None] // 64 == at[None, :] // 64) & (at[:, None] <= at[None, :])).astype(np.float32)
    d["group_ones"] = (at[:, None] // 32 == at[None, :] // 32).astype(np.float32)
    d["ffn_w1"] = i["L0_ffn_w1"].T.reshape(4, 128, 2048).transpose(1, 0, 2).reshape(128, 8192)
    d["ffn_w2"] = i["L0_ffn_w2"].T.reshape(16, 128, 512).transpose(1, 0, 2).reshape(128, 8192)
    d["ffn_conv_w"] = i["L0_ffn_conv_w"].reshape(16, 128, 3).transpose(1, 0, 2)
    d["ffn_conv_b"] = per_partition(i["L0_ffn_conv_b"])
    d["ones"] = np.ones((128, 128), np.float32)
    wkv = i["L1_xattn_Wkv"]
    blocks += [columns_unit(i["L1_xattn_Wq"].T), columns_unit(wkv[:512].T), rows_unit(wkv[512:].T),
               rows_unit(i["L1_xattn_Wout"].T)]
    d["ctx_columns"] = i["ctx_1024"].reshape(8, 512, 4, 128).transpose(0, 3, 2, 1)
    d["ca_bias"] = np.broadcast_to(i["L1_xattn_bout"], (128, 512))
    w, b = i["L1_attn_qkv_w"], i["L1_attn_qkv_b"]
    blocks += [columns_unit(w[:, :512]), columns_unit(w[:, 512:1024]), rows_unit(w[:, 1024:]), rows_unit(i["L1_attn_out_w"])]
    d["qk_bias"] = per_partition(b[:1024])
    d["v_bias"], d["li_bias"] = np.broadcast_to(b[1024:], (128, 512)), np.broadcast_to(i["L1_attn_out_b"], (128, 512))
    d["proj"] = i["L1_attn_proj"].reshape(4, 4, 32, 64).transpose(1, 2, 0, 3)
    w1 = i["L1_ffn_dense_1_w"].reshape(8, 4, 2, 128, 2, 4, 128).transpose(0, 1, 6, 2, 4, 5, 3).reshape(8, 4, 128, 4, 512)
    w2 = i["L1_ffn_dense_2_w"].transpose(0, 2, 1).reshape(8, 2, 4, 128, 512).transpose(0, 1, 3, 2, 4)
    blocks.append(np.concatenate([w1, w2], axis=1).reshape(48, 128, 4, 512))
    d["expert_b1"] = i["L1_ffn_dense_1_b"].reshape(8, 8, 128, 2).transpose(2, 0, 1, 3)
    d["expert_b2"] = i["L1_ffn_dense_2_b"]
    d["gate_w"] = i["L1_ffn_gate_w"].reshape(4, 128, 8).transpose(1, 0, 2)
    e = np.arange(8)
    d["before"] = np.broadcast_to((e[None, :] < e[:, None]).astype(np.float32), (128, 8, 8))
    d["weights"] = np.concatenate(blocks)
    return {k: np.ascontiguousarray(v) for k, v in d.items()}


def kernel(**inputs):
    import concourse.bacc as _bacc
    from concourse.bass_utils import run_bass_kernel_spmd as _run

    nc = _bacc.Bacc("TRN2", target_bir_lowering=False, num_devices=1)
    arrays = lay_out(inputs)
    d = {name: nc.dram_tensor("in_" + name, a.shape, mybir.dt.from_np(a.dtype), kind="ExternalInput").ap()
         for name, a in arrays.items()}
    out = nc.dram_tensor("out_x", (P, TT, D), F32, kind="ExternalOutput").ap()
    program(nc, d, out, STAGES)
    r = _run(nc, [{"in_" + name: a for name, a in arrays.items()}], core_ids=[0])
    return np.ascontiguousarray(r.results[0]["out_x"].transpose(1, 0, 2).reshape(B, L, D))
```

```python
from contextlib import ExitStack

import concourse.bass as bass
from concourse import mybir
import numpy as np

P = 128
T = 512
D = 512
B = 8
L = 64
KEYS = 512
KC = D // P
TT = T // P
EPS = 1e-5
MAGIC = 12582912.0

F32 = mybir.dt.float32
F32R = mybir.dt.float32r
BF16 = mybir.dt.bfloat16
ALU = mybir.AluOpType
ACT = mybir.ActivationFunctionType
AX = mybir.AxisListType

STAGE_BLOCKS = {"latent_attention": 4, "oscillator": 22, "bit_ffn": 0, "context_attention": 4,
                "linear_attention": 4, "experts": 48}
RING_UNITS = 8


class Steps:

    def __init__(self, eng, sem):
        self.eng, self.sem, self.base, self.n = eng, sem, 0, 0

    def mark(self, ins):
        ins.then_inc(self.sem, 1)
        self.n += 1

    def wait(self):
        self.eng.wait_ge(self.sem, self.base + self.n)

    def done(self, ins):
        self.mark(ins)
        self.wait()

    def enter(self, i, per_trip):
        self.before, self.per_trip = self.base + self.n, per_trip
        self.base, self.n = self.before + i * per_trip, 0

    def leave(self, trips):
        assert self.n == self.per_trip, f"{self.n} steps a trip"
        self.base, self.n = self.before + trips * self.per_trip, 0


def product(pe, out, lhs, rhs, start, stop):
    (lh, ll), (rh, rl) = lhs, rhs
    pe.matmul(out, lh, rh, start=start, stop=False)
    pe.matmul(out, lh, rl, start=False, stop=False)
    return pe.matmul(out, ll, rh, start=False, stop=stop)


def f32(ap):
    return ap.bitcast(F32)


def row_stats(dve, steps, rows, stats, mean_var, var_eps, rstd):
    for t in range(TT):
        steps.mark(dve.bn_stats(stats[:, t, :], rows[:, t, :]))
    steps.wait()
    mean, half_gap = mean_var[:, :, 0], mean_var[:, :, 1]
    steps.mark(dve.tensor_tensor(mean, stats[:, :, 1], stats[:, :, 4], ALU.add))
    steps.mark(dve.tensor_tensor(half_gap, stats[:, :, 1], stats[:, :, 4], ALU.subtract))
    steps.mark(dve.tensor_tensor(var_eps, stats[:, :, 2], stats[:, :, 5], ALU.add))
    steps.wait()
    steps.mark(dve.tensor_scalar(mean, mean, 0.5, None, ALU.mult))
    steps.mark(dve.tensor_tensor(half_gap, half_gap, half_gap, ALU.mult))
    steps.mark(dve.tensor_scalar(var_eps, var_eps, 1.0 / D, EPS, ALU.mult, ALU.add))
    steps.wait()
    steps.done(dve.scalar_tensor_tensor(var_eps, half_gap, 0.25, var_eps, ALU.mult, ALU.add))
    return dve.reciprocal(rstd, var_eps)


def guess_rstd(act, rstd):
    return act.activation(rstd, rstd, ACT.Sqrt)


def refine_rstd(dve, steps, var_eps, rstd, tmp):
    steps.done(dve.tensor_tensor(tmp, rstd, rstd, ALU.mult))
    steps.done(dve.tensor_tensor(tmp, tmp, var_eps, ALU.mult))
    steps.done(dve.tensor_scalar(tmp, tmp, -0.5, 1.5, ALU.mult, ALU.add))
    steps.done(dve.tensor_tensor(rstd, rstd, tmp, ALU.mult))


def normalize_rows(dve, out, rows, mean_var, rstd):
    for t in range(TT):
        last = dve.tensor_scalar(out[:, t, :], rows[:, t, :], mean_var[:, t, 0:1], rstd[:, t:t + 1],
                                 ALU.subtract, ALU.mult)
    return last


class NormalizedColumns:

    def __init__(self, m, k, rows, small, high, low, banks):
        self.m, self.k, self.rows, self.high, self.low, self.banks = m, k, rows, high, low, banks
        self.stats = small[:, 0:24].rearrange("p (t n) -> p t n", n=6)
        self.mv = small[:, 24:32].rearrange("p (t n) -> p t n", n=2)
        self.ve, self.rstd, self.tmp = small[:, 32:36], small[:, 36:40], small[:, 40:44]
        (self.stats_ready, self.uses), (self.guessed, _), (self.rows_ready, _) = (
            m.shared("norm_" + n, 1) for n in ("stats", "guess", "rows"))
        (self.turned, self.chunks), (self.high_ready, _), (self.split, _) = (
            m.shared("norm_" + n, KC) for n in ("turned", "high", "split"))

    def wait_rows(self, eng):
        eng.wait_ge(self.rows_ready, self.uses + 1)

    def wait_split(self, eng, chunks):
        eng.wait_ge(self.split, self.chunks + chunks)

    def vector_rows(self, dve, steps):
        dve.wait_ge(self.m.x_loaded, 16)
        if self.k:
            dve.wait_ge(self.m.x_ready, TT * self.k)
        row_stats(dve, steps, self.m.x, self.stats, self.mv, self.ve, self.rstd).then_inc(self.stats_ready, 1)
        dve.wait_ge(self.guessed, self.uses + 1)
        refine_rstd(dve, steps, self.ve, self.rstd, self.tmp)
        normalize_rows(dve, self.rows, self.m.x, self.mv, self.rstd).then_inc(self.rows_ready, 1)

    def vector_low(self, dve):
        for c in range(KC):
            dve.wait_ge(self.high_ready, self.chunks + c + 1)
            dve.tensor_tensor(self.low[:, c, :], self.m.ps[:, self.banks[c], :], f32(self.high[:, c, :]), ALU.subtract)\
               .then_inc(self.split, 1)

    def scalar_guess(self, act):
        act.wait_ge(self.stats_ready, self.uses + 1)
        guess_rstd(act, self.rstd).then_inc(self.guessed, 1)

    def scalar_high(self, act):
        for c in range(KC):
            act.wait_ge(self.turned, self.chunks + c + 1)
            act.copy(self.high[:, c, :], self.m.ps[:, self.banks[c], :]).then_inc(self.high_ready, 1)

    def tensor(self, pe):
        pe.wait_ge(self.m.consts, 16)
        self.wait_rows(pe)
        for c in range(KC):
            for t in range(TT):
                last = pe.transpose(self.m.ps[:, self.banks[c], t * P:(t + 1) * P], self.rows[:, t, c * P:(c + 1) * P],
                                    self.m.ident[:, :])
            last.then_inc(self.turned, 1)


def latent_attention(nc, m, first_unit, k):
    SCALE = 64 ** -0.5
    PAIRS = 4
    NK = KEYS + L
    with ExitStack() as mem:
        sb = lambda name, shape, dt=F32: mem.enter_context(nc.sbuf_tensor("la_" + name, shape, dt))
        ctx = sb("ctx", [P, 2, TT, D])
        xh, xl = sb("xh", [P, 2, KC, T], F32R), sb("xl", [P, 2, KC, T], F32R)
        y = sb("y", [P, 2, T])
        q = sb("q", [P, KC, B, L])
        q_pairs = sb("q_pairs", [P, 2, KC, 2, 2, L])
        kl = sb("kl", [P, KC, B, L])
        kl_batch = sb("kl_batch", [P, 2, KC, L])
        vl = sb("vl", [L, B, D])
        vl_batch = sb("vl_batch", [L, D])
        kt = sb("kt", [P, 2, KC, KEYS])
        v = sb("v", [P, 2, TT, D])
        cos, sin = sb("cos", [P, KEYS]), sb("sin", [P, KEYS])
        by_sin = sb("by_sin", [P, 2, KEYS])
        p = sb("p", [P, 2, NK])
        pt = sb("pt", [P, TT + 1, P])
        o = sb("o", [P, PAIRS, T])
        small = sb("small", [P, 72])
    gx, bx, gl, bl = (small[:, KC * n:KC * n + KC] for n in range(4))
    stats, mv = small[:, 16:40].rearrange("p (t n) -> p t n", n=6), small[:, 40:48].rearrange("p (t n) -> p t n", n=2)
    ve, rstd, tmp = small[:, 48:52], small[:, 52:56], small[:, 56:60]
    nmax, rsum, rinv = small[:, 60:62], small[:, 62:64], small[:, 64:66]
    oh, ol = xh[:, 0], xl[:, 0]
    x = m.x
    s = lambda name: m.sem("la_" + name)
    consts, loaded = m.shared("stage_consts", 6 * 16)
    x_loaded = m.x_loaded
    (ctx_loaded0, _), (ctx_loaded1, _) = (m.shared(f"ctx_loaded{n}", 16 * B // 2) for n in range(2))
    ctx_loaded = (ctx_loaded0, ctx_loaded1)
    ctx_stats, ctx_guess, rows_ready = s("ctx_stats"), s("ctx_guess"), s("rows_ready")
    lat_stats, lat_guess, lat_rows = s("lat_stats"), s("lat_guess"), s("lat_rows")
    q_zero, staged, values_staged = s("q_zero"), s("staged"), s("values_staged")
    lat_done, lat_out = s("lat_done"), s("lat_out")
    xt_done, y_ready, x_split = s("xt_done"), s("y_ready"), s("x_split")
    (lin_done, _), (v_ready, _) = m.shared("lin_done", 8 * B), m.shared("v_ready", 4 * B)
    rotated = s("rotated")
    (scores, _), (nmax_ready, _), (exp_done, _), (p_ready, _), (pt_done, _), (pt_ready, _), (pv_done, _), (o_ready, _) = (
        m.shared(n, PAIRS * B) for n in ("scores", "nmax_ready", "exp_done", "p_ready", "pt_done", "pt_ready", "pv_done", "o_ready"))
    (o_high, halves), (o_split, _) = m.shared("out_high", 4), m.shared("out_split", 4)
    out_done, outs = m.shared("out_done", TT - 1)
    XT, LIN, PVB, SC, PTB = 0, 1, 4, 5, 7
    LB = [1, 2, 3, 1, 2, 3, 1, 2]
    ps = m.ps
    sc_all = ps[:, SC:SC + 2, :].rearrange("p a n -> p (a n)")[:, 0:NK]
    pt5 = ps[0:L, PVB, 0:128]
    pv = ps[:, PVB, 128:256]
    first = lambda b, value: isinstance(b, int) and b == value
    CHUNK = [0, 2, 1, 3]

    def lhs(h, n, c):
        return h[:, n % RING_UNITS, c * P:(c + 1) * P]

    def tensor(pe):
        def transposes(b, par, c):
            for t in range(TT):
                last = pe.transpose(ps[:, XT, t * P:(t + 1) * P], ctx[:, par, t, c * P:(c + 1) * P], m.ident[:, :])
            last.then_inc(xt_done, 1)

        def context_transposes(b, par, c):
            if c == 0:
                pe.wait_ge(rows_ready, b + 1)
            pe.wait_ge(y_ready, KC * (b + 1) + c)
            transposes(b, par, c)

        pe.wait_ge(m.consts, 16)
        pe.wait_ge(lat_rows, 1)
        for c in range(KC):
            if c:
                pe.wait_ge(y_ready, c)
            transposes(0, 1, c)
        for j in range(2):
            for n in range(KC):
                u = first_unit + 4 * j + n
                pe.wait_ge(m.unit_ready, u + 1)
                pe.wait_ge(x_split, KC)
                if j:
                    pe.wait_ge(lat_out, n + 1)
                for c in range(KC):
                    last = product(pe, ps[:, LIN + n, :], (lhs(m.wh, u, c), lhs(m.wl, u, c)),
                                   (xh[:, 1, c, :], xl[:, 1, c, :]), c == 0, c == KC - 1)
                last.then_inc(lat_done if j else m.unit_done, 1)
            for c in (2 * j, 2 * j + 1):
                context_transposes(0, 0, c)
        for t in range(TT):
            pe.wait_ge(lat_out, KC + t + 1)
            for c in range(KC):
                u = first_unit + 8 + c
                pe.wait_ge(m.unit_ready, u + 1)
                last = product(pe, ps[:, LIN + t, :],
                               (xh[:, 1, c, t * P:(t + 1) * P], xl[:, 1, c, t * P:(t + 1) * P]),
                               (m.wh[:, u % RING_UNITS, :], m.wl[:, u % RING_UNITS, :]), c == 0, c == KC - 1)
            last.then_inc(lat_done, 1)

        def linear(b, par, l, chunks=range(KC)):
            if l == 0:
                pe.wait_ge(x_split, KC * (b + 2))
            bank = ps[:, LB[l], :]
            if chunks[0] == 0 and l < 3:
                if not first(b, 0):
                    pe.wait_ge(v_ready, 4 * b + (-1, 0, -2)[l])
            elif chunks[0] == 0 and l < 7:
                pe.wait_ge(rotated, 2 * b + (1 if l < 5 else 2))
            elif chunks[0] == 0:
                pe.wait_ge(v_ready, 4 * b + 1)
            for c in chunks:
                x_c = (xh[:, par, c, :], xl[:, par, c, :])
                if l < 4:
                    u = first_unit + 4 + CHUNK[l]
                    last = product(pe, bank, (lhs(m.wh, u, c), lhs(m.wl, u, c)), x_c, c == 0, c == KC - 1)
                else:
                    u = first_unit + 8 + c
                    t = slice((l - 4) * P, (l - 3) * P)
                    last = product(pe, bank, (x_c[0][:, t], x_c[1][:, t]),
                                   (m.wh[:, u % RING_UNITS, :], m.wl[:, u % RING_UNITS, :]), c == 0, c == KC - 1)
            if chunks[-1] == KC - 1:
                last.then_inc(lin_done, 1)

        def attention_scores(b, par, hp):
            if hp == 0:
                pe.wait_ge(rotated, 2 * b + 2)
                pe.wait_ge(staged, b + 1)
            if not (first(b, 0) and hp == 0):
                pe.wait_ge(exp_done, 4 * b + hp)
            for half in range(2):
                c = hp // 2 + 2 * half
                pe.matmul(sc_all[:, 0:KEYS], q_pairs[:, par, c, hp % 2, :, :].rearrange("p e l -> p (e l)"),
                          kt[:, par, c, :], start=half == 0, stop=half == 1)
            for half in range(2):
                c = hp // 2 + 2 * half
                last = pe.matmul(sc_all[:, KEYS:NK], q_pairs[:, par, c, hp % 2, :, :].rearrange("p e l -> p (e l)"),
                                 kl_batch[:, par, c, :], start=half == 0, stop=half == 1)
            last.then_inc(scores, 1)

        def probability_transposes(b, hp):
            pe.wait_ge(p_ready, 4 * b + hp + 1)
            if not (first(b, 0) and hp == 0):
                pe.wait_ge(pt_ready, 4 * b + hp)
                pe.wait_ge(o_ready, 4 * b + hp)
            for t in range(TT):
                pe.transpose(ps[:, PTB, t * P:(t + 1) * P], p[:, hp % 2, t * P:(t + 1) * P], m.ident[:, :])
            pe.transpose(pt5, p[:, hp % 2, KEYS:NK], m.ident[:, :]).then_inc(pt_done, 1)

        def values(b, par, hp):
            pe.wait_ge(pt_ready, 4 * b + hp + 1)
            pe.wait_ge(v_ready, 4 * b + 4)
            pe.wait_ge(values_staged, b + 1)
            cols = slice(hp * P, (hp + 1) * P)
            for t in range(TT):
                pe.matmul(pv, v[:, par, t, cols], pt[:, t, :], start=t == 0, stop=False)
            pe.matmul(pv, vl_batch[:, cols], pt[0:L, TT, :],
                      start=False, stop=True).then_inc(pv_done, 1)

        def step(b, par, lin=True, att=True, nxt=True, carry=True):
            for hp in range(PAIRS):
                behind = (b - 1, 1 - par, hp - 1) if hp else (b - 2, par, PAIRS - 1)
                follow = att and (hp or carry)
                if att:
                    attention_scores(b - 1, 1 - par, hp)
                if lin:
                    linear(b, par, 2 * hp)
                if follow:
                    probability_transposes(behind[0], behind[2])
                if lin:
                    linear(b, par, 2 * hp + 1, range(0, 2))
                if follow:
                    values(*behind)
                if lin:
                    linear(b, par, 2 * hp + 1, range(2, 4))
                if nxt:
                    context_transposes(b + 1, 1 - par, hp)

        pe.wait_ge(lat_out, 3 * KC)
        step(0, 0, att=False)
        step(1, 1, carry=False)
        with pe.Fori(1, B // 2 - 1) as i:
            step(2 * i, 0)
            step(2 * i + 1, 1)
        step(B - 2, 0)
        step(B - 1, 1, nxt=False)
        pe.wait_ge(lin_done, 8 * B)
        pe.sem_inc(m.unit_done, 8)
        step(B, 0, lin=False, nxt=False)
        probability_transposes(B - 1, PAIRS - 1)
        values(B - 1, 1, PAIRS - 1)

        pe.wait_ge(o_split, halves + PAIRS)
        for c in range(KC):
            u = first_unit + 12 + c
            pe.wait_ge(m.unit_ready, u + 1)
            for t in range(TT):
                last = product(pe, ps[:, LIN + t, :], (oh[:, c, t * P:(t + 1) * P], ol[:, c, t * P:(t + 1) * P]),
                               (m.wh[:, u % RING_UNITS, :], m.wl[:, u % RING_UNITS, :]), c == 0, c == KC - 1)
                if c == KC - 1 and t < TT - 1:
                    last.then_inc(out_done, 1)
            last.then_inc(m.unit_done, 1)

    def scalar(act):
        load = lambda out, src: act.dma_start(out, src).then_inc(consts, 16)
        load(cos[:, :], m.d["rope_cos"])
        load(sin[:, :], m.d["rope_sin"])
        load(gx[:, :], m.d["gamma_x"])
        load(bx[:, :], m.d["beta_x"])
        load(gl[:, :], m.d["gamma_l"])
        load(bl[:, :], m.d["beta_l"])

        for n in range(2):
            act.wait_ge(lat_stats, n + 1)
            guess_rstd(act, rstd).then_inc(lat_guess, 1)
        act.wait_ge(consts, loaded + 6 * 16)
        for c in range(KC):
            act.wait_ge(xt_done, c + 1)
            if c >= 2:
                act.wait_ge(x_split, c - 1)
            act.activation(y[:, c % 2, :], ps[:, XT, :], ACT.Identity, scale=gl[:, c:c + 1], bias=bl[:, c:c + 1])\
               .then_inc(y_ready, 1)

        def guess(b):
            act.wait_ge(ctx_stats, b + 1)
            guess_rstd(act, rstd).then_inc(ctx_guess, 1)

        guess(0)
        def context_chunk(b, c):
            act.wait_ge(xt_done, KC * (b + 1) + c + 1)
            act.wait_ge(x_split, KC * (b + 1) + c - 1)
            act.activation(y[:, c % 2, :], ps[:, XT, :], ACT.Identity, scale=gx[:, c:c + 1], bias=bx[:, c:c + 1])\
               .then_inc(y_ready, 1)

        for n in range(KC):
            act.wait_ge(m.unit_done, first_unit + n + 1)
            act.activation(q[:, n, :, :].rearrange("p b l -> p (b l)"), ps[:, LIN + n, :], ACT.Copy, scale=SCALE)\
               .then_inc(lat_out, 1)
        context_chunk(0, 0)
        context_chunk(0, 1)
        for n in range(KC):
            act.wait_ge(lat_done, n + 1)
            act.copy(kl[:, n, :, :].rearrange("p b l -> p (b l)"), ps[:, LIN + n, :]).then_inc(lat_out, 1)
        context_chunk(0, 2)
        context_chunk(0, 3)
        for t in range(TT):
            act.wait_ge(lat_done, KC + t + 1)
            act.copy(vl[:, 2 * t, :], ps[0:L, LIN + t, :])
            act.copy(vl[:, 2 * t + 1, :], ps[L:P, LIN + t, :]).then_inc(lat_out, 1)

        def stage(b, par):
            if isinstance(b, int) and b == 0:
                act.wait_ge(q_zero, 1)
                act.wait_ge(lat_out, 3 * KC)
            for h in range(4):
                rows = slice(32 * h, 32 * h + 32)
                act.copy(q_pairs[rows, par, :, h // 2, h % 2, :], q[rows, :, bass.ds(b, 1), :].rearrange("p c o l -> p c (o l)"))
            act.copy(kl_batch[:, par, :, :], kl[:, :, bass.ds(b, 1), :].rearrange("p c o l -> p c (o l)"))\
               .then_inc(staged, 1)

        def stage_values(b):
            act.copy(vl_batch[:, :], vl[:, bass.ds(b, 1), :].rearrange("p o n -> p (o n)")).then_inc(values_staged, 1)

        def value_tile(b, par, t):
            act.wait_ge(lin_done, 8 * b + 5 + t)
            act.copy(v[:, par, t, :], ps[:, LB[4 + t], :]).then_inc(v_ready, 1)

        def exponentials(b, hp):
            act.wait_ge(nmax_ready, 4 * b + hp + 1)
            act.activation(p[:, hp % 2, :], sc_all, ACT.Exp, bias=nmax[:, hp % 2:hp % 2 + 1],
                           accum_out=rsum[:, hp % 2:hp % 2 + 1]).then_inc(exp_done, 1)

        def transposed(b, hp):
            act.wait_ge(pt_done, 4 * b + hp + 1)
            if not (first(b, 0) and hp == 0):
                act.wait_ge(pv_done, 4 * b + hp)
            act.copy(pt[:, 0:TT, :].rearrange("p t n -> p (t n)"), ps[:, PTB, :])
            act.copy(pt[0:L, TT, :], pt5).then_inc(pt_ready, 1)

        def output(b, hp):
            act.wait_ge(pv_done, 4 * b + hp + 1)
            for e in range(2):
                rows = slice(64 * e, 64 * e + 64)
                last = act.copy(o[rows, hp, bass.ds(b * L, L)], pv[rows, 64 * e:64 * e + 64])
            last.then_inc(o_ready, 1)

        def step(b, par, lin=True, att=True, rows=True, nxt=True, carry=True):
            for hp in range(PAIRS):
                behind = (b - 1, hp - 1) if hp else (b - 2, PAIRS - 1)
                follow = att and (hp or carry)
                if att:
                    exponentials(b - 1, hp)
                if follow:
                    transposed(*behind)
                if lin and hp >= 2:
                    value_tile(b, par, 2 * hp - 4)
                if follow:
                    output(*behind)
                if att and hp == 0:
                    stage_values(b - 1)
                if lin and hp == 0:
                    stage(b, par)
                if rows and hp == 1:
                    guess(b + 2)
                if lin and hp >= 2:
                    value_tile(b, par, 2 * hp - 3)
                if nxt:
                    context_chunk(b + 1, hp)
        guess(1)
        step(0, 0, att=False)
        step(1, 1, carry=False)
        with act.Fori(1, B // 2 - 1) as i:
            step(2 * i, 0)
            step(2 * i + 1, 1)
        step(B - 2, 0, rows=False)
        step(B - 1, 1, rows=False, nxt=False)
        step(B, 0, lin=False, rows=False, nxt=False)
        transposed(B - 1, PAIRS - 1)
        output(B - 1, PAIRS - 1)
        act.wait_ge(o_ready, 4 * B)
        for hp in range(PAIRS):
            act.copy(oh[:, hp, :], o[:, hp, :]).then_inc(o_high, 1)

    def vector(dve):
        steps = m.dve_steps
        dve.memset(q_pairs[:, :, :, :, :, :].rearrange("p s c r e l -> p (s c r e l)"), 0.0).then_inc(q_zero, 1)
        dve.wait_ge(x_loaded, 16)
        for n in range(2):
            rows = ctx[:, 1] if n else x
            row_stats(dve, steps, rows, stats, mv, ve[:, :], rstd).then_inc(lat_stats, 1)
            dve.wait_ge(lat_guess, n + 1)
            refine_rstd(dve, steps, ve[:, :], rstd[:, :], tmp[:, :])
            last = normalize_rows(dve, ctx[:, 1], rows, mv, rstd)
            if n:
                last.then_inc(lat_rows, 1)
            else:
                steps.done(last)

        def split(n, slot, c):
            dve.wait_ge(y_ready, n + 1)
            steps.done(dve.tensor_copy(xh[:, slot, c, :], y[:, c % 2, :]))
            dve.tensor_tensor(xl[:, slot, c, :], y[:, c % 2, :], f32(xh[:, slot, c, :]), ALU.subtract)\
               .then_inc(x_split, 1)

        def context_stats(b, par):
            dve.wait_ge(ctx_loaded[par], 8 * (b - par) + 16)
            row_stats(dve, steps, ctx[:, par], stats, mv, ve[:, :], rstd).then_inc(ctx_stats, 1)

        def normalize_context(b, par):
            dve.wait_ge(ctx_guess, b + 1)
            refine_rstd(dve, steps, ve[:, :], rstd[:, :], tmp[:, :])
            normalize_rows(dve, ctx[:, par], ctx[:, par], mv, rstd).then_inc(rows_ready, 1)

        def rotate(b, par, cc):
            dve.wait_ge(lin_done, 8 * b + 2 * cc + 2)
            if cc or not first(b, 0):
                dve.wait_ge(rotated, 2 * b + cc)
            k1, k2 = ps[:, LB[2 * cc], :], ps[:, LB[2 * cc + 1], :]
            steps.mark(dve.tensor_tensor(kt[:, par, cc, :], k1, cos[:, :], ALU.mult))
            steps.mark(dve.tensor_tensor(by_sin[:, 0, :], k2, sin[:, :], ALU.mult))
            steps.mark(dve.tensor_tensor(kt[:, par, cc + 2, :], k2, cos[:, :], ALU.mult))
            steps.mark(dve.tensor_tensor(by_sin[:, 1, :], k1, sin[:, :], ALU.mult))
            steps.wait()
            steps.mark(dve.tensor_tensor(kt[:, par, cc, :], kt[:, par, cc, :], by_sin[:, 0, :], ALU.subtract))
            dve.tensor_tensor(kt[:, par, cc + 2, :], kt[:, par, cc + 2, :], by_sin[:, 1, :], ALU.add)\
               .then_inc(rotated, 1)

        def softmax(b, hp):
            slot = slice(hp % 2, hp % 2 + 1)
            dve.wait_ge(scores, 4 * b + hp + 1)
            dve.tensor_reduce(nmax[:, slot], sc_all, AX.X, ALU.max, negate=True).then_inc(nmax_ready, 1)
            dve.wait_ge(exp_done, 4 * b + hp + 1)
            steps.done(dve.reciprocal(rinv[:, slot], rsum[:, slot]))
            dve.tensor_scalar(p[:, hp % 2, :], p[:, hp % 2, :], rinv[:, slot], None, ALU.mult).then_inc(p_ready, 1)

        def step(b, par, lin=True, att=True, rows=True, nxt=True):
            for hp in range(PAIRS):
                if att:
                    softmax(b - 1, hp)
                if rows and hp == 1:
                    context_stats(b + 2, par)
                if rows and hp == 2:
                    normalize_context(b + 2, par)
                if lin and hp < 2:
                    rotate(b, par, hp)
                if nxt:
                    split(KC * (b + 2) + hp, 1 - par, hp)

        for c in range(KC):
            split(c, 1, c)
        context_stats(0, 0)
        normalize_context(0, 0)
        dve.wait_ge(consts, loaded + 6 * 16)
        for c in range(KC):
            split(KC + c, 0, c)
        context_stats(1, 1)
        normalize_context(1, 1)
        step(0, 0, att=False)
        step(1, 1)
        with dve.Fori(1, B // 2 - 1) as i:
            steps.enter(i - 1, 66)
            step(2 * i, 0)
            step(2 * i + 1, 1)
            steps.leave(B // 2 - 2)
        step(B - 2, 0, rows=False)
        step(B - 1, 1, rows=False, nxt=False)
        step(B, 0, lin=False, rows=False, nxt=False)
        for hp in range(PAIRS):
            dve.wait_ge(o_high, halves + hp + 1)
            dve.tensor_tensor(ol[:, hp, :], o[:, hp, :], f32(oh[:, hp, :]), ALU.subtract).then_inc(o_split, 1)
        for t in range(TT):
            if t < TT - 1:
                dve.wait_ge(out_done, outs + t + 1)
            else:
                dve.wait_ge(m.unit_done, first_unit + 16)
            dve.tensor_tensor(x[:, t, :], x[:, t, :], ps[:, LIN + t, :], ALU.add).then_inc(m.x_ready, 1)

    def loads(sp):
        def load_context(b, par, trip):
            sp.dma_start(ctx[:, par, :, :], m.d["ctx_rows"][bass.ds(b, 1)].rearrange("o p t n -> (o p) t n"))\
              .then_inc(ctx_loaded[par], 16)

        load_context(0, 0, 0)
        sp.wait_ge(xt_done, KC)
        load_context(1, 1, 0)
        with sp.Fori(1, B // 2) as i:
            for par in range(2):
                b = 2 * i + par
                sp.wait_ge(xt_done, KC * b)
                load_context(b, par, i)

    return tensor, scalar, vector, loads


def oscillator(nc, m, first_unit, k):
    G, DI = 8, 1024
    NM = DI // P
    CONV = 4
    with ExitStack() as mem:
        sb = lambda name, shape, dt=F32: mem.enter_context(nc.sbuf_tensor("os_" + name, shape, dt))
        vh, vl = sb("vh", [P, NM, T], F32R), sb("vl", [P, NM, T], F32R)
        qs = sb("qs", [P, 2, 2, G, B, L + 1])
        aw = sb("aw", [P, 2, G, B, L])
        small = sb("small", [P, 128])
        scan = sb("scan", [P, 6 * G * B])
        with ExitStack() as early:
            sbe = lambda name, shape, dt=F32: early.enter_context(nc.sbuf_tensor("os_" + name, shape, dt))
            xh, xl = sbe("xh", [P, KC, T], F32R), sbe("xl", [P, KC, T], F32R)
            with ExitStack() as first:
                wph, wpl = (first.enter_context(nc.sbuf_tensor("os_" + n, [P, KC, P], F32R)) for n in ("wph", "wpl"))
            gate_out = sbe("gate_out", [P, 2, T])
        bc = sb("bc", [P, 4, T])
        sq = sb("sq", [P, 2, T])
        gt = sb("gt", [P, 2, 4, P])
        ur = sb("ur", [P, TT, P])
        vg = sb("vg", [P, T])
        pick = sb("pick", [P, 32])
    u3 = scan[:, :].rearrange("p (u r n) -> p u r n", u=3, r=2)
    mask, spread = scan[:, 0:P], scan[:, P:2 * P]
    norm = sq[:, 1, :]
    early_at = qs[:, :, :, :, :, :].rearrange("p r c g b t -> p (r c g b t)")
    take = lambda n, at: early_at[:, at * 512:(at + n) * 512]
    rows = take(4, 0).rearrange("p (t n) -> p t n", t=TT)
    conv_y, silu_y = take(2, 4).rearrange("p (s n) -> p s n", s=2), take(2, 6).rearrange("p (s n) -> p s n", s=2)
    select = take(4, 8).rearrange("p (g n) -> p g n", g=2 * G)
    compact, e_u, e_w, e_d, e_l = (take(1, 12 + n) for n in range(5))
    dt_rows = take(2, 17).rearrange("p (s n) -> p s n", s=2)
    wp_raw = take(1, 19).rearrange("p (c n) -> p c n", c=KC)
    slot = lambda n: aw[:, 0, n, :, :].rearrange("p b t -> p (b t)")
    g0, g1, e0, e1, v1, v2, ta, tb = (slot(n) for n in range(8))
    conv_w, conv_b, skip = small[:, 44:76].rearrange("p (m j) -> p m j", j=CONV), small[:, 76:84], small[:, 84:92]
    a_log, root_a, inv_root = small[:, 92:100], small[:, 100:108], small[:, 108:116]
    dt_bias = small[:, 116:117]
    gates = nc.dram_tensor("os_gates", (P, NM, T), F32, kind="Internal").ap()
    released = m.shared("out_split", 0)
    s = lambda name: m.sem("os_" + name)
    consts, loaded = m.shared("stage_consts", 7 * 16)
    ln = NormalizedColumns(m, k, rows, small, xh, xl, (1, 2, 3, 4))
    late_consts, wp_split, roots = s("late_consts"), s("wp_split"), s("roots")
    par_done, e_ready, w_ready, l_ready, k_ready, compact_ready = (
        s(n) for n in ("par_done", "e_ready", "w_ready", "l_ready", "k_ready", "compact_ready"))
    tap, conv_done, silu_done, v_split = s("tap"), s("conv_done"), s("silu_done"), s("v_split")
    sel_done, dt_copied, aw_ready = s("sel_done"), s("dt_copied"), s("aw_ready")
    gate_silu, gate_stored = s("gate_silu"), [s("gate_stored0"), s("gate_stored1")]
    squared, sums_done, rooted, bc_ready = s("squared"), s("sums_done"), s("rooted"), s("bc_ready")
    spread_copied = s("spread_copied")
    norm_ready, spread_done, scanned, scan_consts = s("norm_ready"), s("spread_done"), s("scanned"), s("scan_consts")
    vg_ready, ur_done, ur_ready = s("vg_ready"), s("ur_done"), s("ur_ready")
    w_used, gate_loaded = s("w_used"), s("gate_loaded")
    ge_ready, head_done, gt_ready, y_done, y_ready = (s(n) for n in ("ge_ready", "head_done", "gt_ready", "y_done", "y_ready"))
    (y_high, halves), (y_split, _) = m.shared("out_high", 8), m.shared("out_split", 8)
    out_done, outs = m.shared("out_done", TT - 1)
    LIN, PAR, SUM, GB, YB = 1, 5, 5, (0, 7), 6
    SEL, SEL_K = (6, 0), (7, 5)
    NB = (5, 0, 7, 5)
    ps = m.ps
    value_unit, gate_unit, bc_unit, out_unit = first_unit, first_unit + 8, first_unit + 16, first_unit + 80

    def pair_of(h, n, c):
        return h[:, n % RING_UNITS, c * P:(c + 1) * P]

    def tensor(pe):
        ln.tensor(pe)
        ln.wait_split(pe, KC)
        pe.wait_ge(wp_split, 1)
        for c in range(KC):
            last = product(pe, ps[:, PAR, :], (wph[:, c, :], wpl[:, c, :]), (xh[:, c, :], xl[:, c, :]), c == 0, c == KC - 1)
        last.then_inc(par_done, 1)

        def columns(n, bank, unit):
            pe.wait_ge(m.unit_ready, unit + 1)
            for c in range(KC):
                last = product(pe, ps[:, bank, :], (pair_of(m.wh, unit, c), pair_of(m.wl, unit, c)),
                               (xh[:, c, :], xl[:, c, :]), c == 0, c == KC - 1)
            last.then_inc(m.unit_done, 1)

        for n in range(NM):
            if n >= 4:
                pe.wait_ge(conv_done, n - 3)
            columns(n, LIN + n % 4, value_unit + n)
        pe.wait_ge(compact_ready, 1)
        for g in range(G):
            if g >= 2:
                pe.wait_ge(aw_ready, g - 1)
            pe.matmul(ps[:, SEL[g % 2], :], select[:, g, :], compact, start=True, stop=True)
            pe.matmul(ps[:, SEL_K[g % 2], :], select[:, G + g, :], compact, start=True, stop=True).then_inc(sel_done, 1)
        for n in range(NM):
            pe.wait_ge(conv_done, NM)
            if n >= 4:
                pe.wait_ge(gate_silu, n - 3)
            columns(n, LIN + n % 4, gate_unit + n)

        def bc_products(g, j):
            if isinstance(g, int) and g == 0:
                pe.wait_ge(v_split, NM)
                pe.wait_ge(gate_silu, 5 + j)
            else:
                pe.wait_ge(bc_ready, 4 * g + (j - 3))
            for half in range(2):
                at = 2 * j + half
                pe.wait_ge(m.unit_ready, bc_unit + 8 * g + (at + 1))
                for c in range(KC):
                    cc = KC * half + c
                    last = product(pe, ps[:, LIN + j, :], (pair_of(m.wh, bc_unit + at, c), pair_of(m.wl, bc_unit + at, c)),
                                   (vh[:, cc, :], vl[:, cc, :]), cc == 0, cc == NM - 1)
                last.then_inc(m.unit_done, 1)

        def sums(g, j):
            if isinstance(g, int) and g == 0:
                pe.wait_ge(late_consts, 16)
            elif j == 0:
                pe.wait_ge(spread_copied, 4 * g)
            pe.wait_ge(squared, 4 * g + j + 1)
            pe.matmul(ps[32 * j:32 * j + 32, SUM, :], pick[:, :], sq[:, j % 2, :], start=True, stop=True).then_inc(sums_done, 1)

        def spread_norms(g):
            pe.wait_ge(norm_ready, g + 1)
            if isinstance(g, int) and g == 0:
                pe.wait_ge(scan_consts, 2 * 16)
            for j in range(4):
                if j == 1 and not (isinstance(g, int) and g == 0):
                    pe.wait_ge(gt_ready, 4 * g)
                part = slice(32 * j, 32 * j + 32)
                if j == 3:
                    pe.wait_ge(spread_copied, 4 * g + 1)
                pe.matmul(ps[:, NB[j], :], spread[part, :], norm[part, :], start=True, stop=True).then_inc(spread_done, 1)

        def turn_values(g):
            pe.wait_ge(vg_ready, g + 1)
            if not (isinstance(g, int) and g == 0):
                pe.wait_ge(y_ready, g)
            for t in range(TT):
                last = pe.transpose(ps[:, YB, t * P:(t + 1) * P], vg[:, t * P:(t + 1) * P], m.ident[:, :])
            last.then_inc(ur_done, 1)

        def outputs(g):
            pe.wait_ge(ge_ready, g + 1)
            for half in range(2):
                pe.wait_ge(gt_ready, 4 * g + 2 * half)
                for h in range(4):
                    if h >= 2:
                        pe.wait_ge(head_done, 8 * g + 4 * half + h - 1)
                    hr = slice(32 * h, 32 * h + 32)
                    for q in range(2):
                        cols = slice((2 * half + q) * P, (2 * half + q + 1) * P)
                        at = ((h // 2) * 2 + q) * P
                        out = ps[:, GB[h % 2], at:at + P]
                        pe.matmul(out, g0[hr, cols], e0[hr, cols], start=True, stop=False)
                        last = pe.matmul(out, g1[hr, cols], e1[hr, cols], start=False, stop=True)
                    last.then_inc(head_done, 1)
                pe.wait_ge(ur_ready, g + 1)
                for h in range(4):
                    if h < 2:
                        pe.wait_ge(gt_ready, 4 * g + 2 * half + h + 1)
                    for q in range(2):
                        pr = 2 * half + q
                        last = pe.matmul(ps[32 * h:32 * h + 32, YB, pr * P:(pr + 1) * P], ur[:, pr, 32 * h:32 * h + 32],
                                         gt[:, h % 2, (h // 2) * 2 + q, :], start=True, stop=True)
                last.then_inc(y_done, 1)

        def group(g, products=True, out=True):
            if products:
                for j in range(4):
                    bc_products(g, j)
                    if j:
                        sums(g, j - 1)
            if out:
                turn_values(g - 1)
            if products:
                sums(g, 3)
            if out:
                outputs(g - 1)
            if products:
                spread_norms(g)

        pe.wait_ge(aw_ready, G)
        group(0, out=False)
        with pe.Fori(1, G) as g:
            group(g)
        group(G, products=False)
        for cc in range(NM):
            u = out_unit + cc
            pe.wait_ge(m.unit_ready, u + 1)
            pe.wait_ge(y_split, halves + cc + 1)
            for t in range(TT):
                last = product(pe, ps[:, LIN + t, :], (vh[:, cc, t * P:(t + 1) * P], vl[:, cc, t * P:(t + 1) * P]),
                               (m.wh[:, u % RING_UNITS, :], m.wl[:, u % RING_UNITS, :]), cc == 0, cc == NM - 1)
                if cc == NM - 1 and t < TT - 1:
                    last.then_inc(out_done, 1)
            last.then_inc(m.unit_done, 1)

    def scalar(act):
        if k:
            act.wait_ge(*released)
        for out, src in ((conv_w, m.d["conv_w"]), (conv_b, m.d["conv_b"]), (skip, m.d["skip"]), (a_log, m.d["a_log"]),
                         (dt_bias[0:32, :], m.d["dt_bias"]), (select, m.d["select"]), (wp_raw, m.d["w_params"])):
            act.dma_start(out, src).then_inc(consts, 16)
        ln.scalar_guess(act)
        act.wait_ge(consts, loaded + 7 * 16)
        act.activation(root_a, a_log, ACT.Exp, scale=0.5).then_inc(roots, 1)
        act.activation(inv_root, a_log, ACT.Exp, scale=-0.5).then_inc(roots, 1)
        ln.scalar_high(act)
        act.wait_ge(par_done, 1)
        act.activation(e_u[0:32, :], ps[0:32, PAR, :], ACT.Exp, bias=dt_bias[0:32, :]).then_inc(e_ready, 1)
        act.wait_ge(w_ready, 1)
        act.activation(e_l[0:32, :], e_w[0:32, :], ACT.Ln).then_inc(l_ready, 1)
        act.activation(e_l[32:64, :], ps[32:64, PAR, :], ACT.Sigmoid).then_inc(k_ready, 1)

        def first_tap(n):
            act.wait_ge(m.unit_done, value_unit + n + 1)
            if n >= 2:
                act.wait_ge(silu_done, n - 1)
            act.activation(conv_y[:, n % 2, :], ps[:, LIN + n % 4, :], ACT.Identity, scale=conv_w[:, n, 3:4],
                           bias=conv_b[:, n:n + 1]).then_inc(tap, 1)

        for n in range(NM + 1):
            if n < NM:
                first_tap(n)
            if n:
                act.wait_ge(conv_done, n)
                if n >= 3:
                    act.wait_ge(v_split, n - 2)
                act.activation(silu_y[:, (n - 1) % 2, :], conv_y[:, (n - 1) % 2, :], ACT.Silu).then_inc(silu_done, 1)
        for g in range(G):
            act.wait_ge(sel_done, g + 1)
            if g >= 2:
                act.wait_ge(aw_ready, g - 1)
            act.copy(dt_rows[:, g % 2, :], ps[:, SEL[g % 2], :]).then_inc(dt_copied, 1)
        for n in range(NM):
            act.wait_ge(m.unit_done, gate_unit + n + 1)
            if n >= 2:
                act.wait_ge(gate_stored[n % 2], 16 * (n // 2))
            act.activation(gate_out[:, n % 2, :], ps[:, LIN + n % 4, :], ACT.Silu).then_inc(gate_silu, 1)
            act.wait_ge(gate_silu, n + 1)
            act.dma_start(gates[:, n, :], gate_out[:, n % 2, :]).then_inc(gate_stored[n % 2], 16)
        act.dma_start(pick[:, :], m.d["pick"]).then_inc(late_consts, 16)
        for n in range(2):
            act.wait_ge(gate_stored[n], 16 * NM // 2)

        def squares(g, j):
            act.wait_ge(m.unit_done, bc_unit + 8 * g + (2 * j + 2))
            if not (isinstance(g, int) and g == 0 and j < 2):
                act.wait_ge(sums_done, 4 * g + (j - 1))
            if j == 1 and not (isinstance(g, int) and g == 0):
                act.wait_ge(spread_done, 4 * g)
            act.activation(sq[:, j % 2, :], ps[:, LIN + j, :], ACT.Square).then_inc(squared, 1)

        def value_rows(g):
            act.wait_ge(w_used, g + 1)
            act.dma_start(aw[:, 1, bass.ds(g, 1), :, :].rearrange("p o b t -> p (o b t)"),
                          gates[:, bass.ds(g, 1), :].rearrange("p o n -> p (o n)")).then_inc(gate_loaded, 16)
            act.wait_ge(ur_done, g + 1)
            act.copy(ur[:, :, :].rearrange("p t n -> p (t n)"), ps[:, YB, :]).then_inc(ur_ready, 1)

        def group(g, products=True, out=True):
            if products:
                for j in range(4):
                    squares(g, j)
            if out:
                value_rows(g - 1)
            if products:
                if isinstance(g, int) and g == 0:
                    act.wait_ge(scanned, 1)
                    act.dma_start(mask, m.d["causal"]).then_inc(scan_consts, 16)
                    act.dma_start(spread, m.d["spread"]).then_inc(scan_consts, 16)
                act.wait_ge(sums_done, 4 * g + 4)
                act.activation(norm[:, :], ps[:, SUM, :], ACT.Sqrt).then_inc(rooted, 1)
                for j in range(4):
                    act.wait_ge(spread_done, 4 * g + j + 1)
                    if j == 0 and not (isinstance(g, int) and g == 0):
                        act.wait_ge(ge_ready, g)
                    act.copy(bc[:, j, :], ps[:, NB[j], :]).then_inc(spread_copied, 1)

        group(0, out=False)
        with act.Fori(1, G) as g:
            group(g)
        group(G, products=False)
        act.wait_ge(y_ready, G)
        for cc in range(NM):
            act.copy(vh[:, cc, :], qs[:, 0, 0, cc, :, 1:L + 1].rearrange("p b t -> p b t")).then_inc(y_high, 1)

    def vector(dve):
        steps = m.dve_steps
        if k:
            dve.wait_ge(m.x_ready, TT * k)
        ln.vector_rows(dve, steps)
        dve.wait_ge(consts, loaded + 7 * 16)
        steps.done(dve.tensor_copy(wph[:, :, :], wp_raw))
        dve.tensor_tensor(wpl[:, :, :], wp_raw, f32(wph[:, :, :]), ALU.subtract).then_inc(wp_split, 1)
        steps.done(dve.memset(compact, 0.0))
        ln.vector_low(dve)
        dve.wait_ge(e_ready, 1)
        d32 = slice(0, 32)
        steps.done(dve.tensor_scalar(e_u[d32, :], e_u[d32, :], 1e4, None, ALU.min))
        steps.done(dve.tensor_scalar(e_w[d32, :], e_u[d32, :], 1.0, None, ALU.add))
        dve.tensor_scalar(e_d[d32, :], e_w[d32, :], -1.0, 1e-30, ALU.add, ALU.max).then_inc(w_ready, 1)
        dve.wait_ge(w_ready, 1)
        steps.done(dve.reciprocal(e_d[d32, :], e_d[d32, :]))
        steps.done(dve.tensor_tensor(e_u[d32, :], e_u[d32, :], e_d[d32, :], ALU.mult))
        dve.wait_ge(l_ready, 1)
        steps.done(dve.tensor_tensor(e_u[d32, :], e_u[d32, :], e_l[d32, :], ALU.mult))
        steps.mark(dve.tensor_scalar(compact[d32, :], e_u[d32, :], 1e-4, 0.1, ALU.max, ALU.min))
        dve.wait_ge(k_ready, 1)
        dve.tensor_scalar(compact[32:64, :], e_l[32:64, :], 0.5, None, ALU.mult).then_inc(compact_ready, 1)

        by_batch = lambda ap: ap.rearrange("p (b t) -> p b t", b=B)

        def convolve(n):
            dve.wait_ge(tap, n + 1)
            y, v = by_batch(conv_y[:, n % 2, :]), by_batch(ps[:, LIN + n % 4, :])
            for j in range(1, CONV):
                ins = dve.scalar_tensor_tensor(y[:, :, j:], v[:, :, 0:L - j], conv_w[:, n, 3 - j:4 - j], y[:, :, j:],
                                               ALU.mult, ALU.add)
                if j < CONV - 1:
                    steps.done(ins)
            ins.then_inc(conv_done, 1)

        def split_value(n):
            dve.wait_ge(silu_done, n + 1)
            steps.done(dve.tensor_copy(vh[:, n, :], silu_y[:, n % 2, :]))
            dve.tensor_tensor(vl[:, n, :], silu_y[:, n % 2, :], f32(vh[:, n, :]), ALU.subtract).then_inc(v_split, 1)

        for n in range(NM + 1):
            if n < NM:
                convolve(n)
            if n:
                split_value(n - 1)
        dve.wait_ge(roots, 2)
        for g in range(G):
            a_g, w_g = (aw[:, n, g, :, :].rearrange("p b t -> p (b t)") for n in range(2))
            dve.wait_ge(dt_copied, g + 1)
            steps.mark(dve.tensor_tensor(a_g, dt_rows[:, g % 2, :], ps[:, SEL_K[g % 2], :], ALU.mult))
            steps.done(dve.tensor_scalar(w_g, dt_rows[:, g % 2, :], root_a[:, g:g + 1], None, ALU.mult))
            dve.tensor_scalar(a_g, a_g, 1.0, None, ALU.add).then_inc(aw_ready, 1)
        dve.wait_ge(aw_ready, G)

        qt = qs[:, :, :, :, :, :].rearrange("p r c g b t -> p r c (g b) t")
        at = aw[:, :, :, :, :].rearrange("p c g b t -> p c (g b) t")
        for r in range(2):
            for c in range(2):
                steps.mark(dve.memset(qt[:, r, c, :, 0], 1.0 if r == c else 0.0))
        steps.wait()
        col = lambda ap: ap.rearrange("p r n o -> p r (n o)")
        UNROLL = 8
        with dve.Fori(0, L // UNROLL) as i:
            steps.enter(i, 4 * UNROLL)
            for n in range(UNROLL):
                t = i * UNROLL + n
                q_a, q_c = (col(qt[:, :, c, :, bass.ds(t, 1)]) for c in range(2))
                n_a, n_c = (col(qt[:, :, c, :, bass.ds(t + 1, 1)]) for c in range(2))
                a_w = col(at[:, :, :, bass.ds(t, 1)])
                steps.mark(dve.tensor_tensor(u3[:, 0:2, :, :], a_w.unsqueeze(2).to_broadcast([P, 2, 2, G * B]),
                                             q_a.unsqueeze(1).to_broadcast([P, 2, 2, G * B]), ALU.mult))
                steps.mark(dve.tensor_tensor(u3[:, 2, :, :], a_w[:, 1:2, :].to_broadcast([P, 2, G * B]), q_c, ALU.mult))
                steps.wait()
                steps.mark(dve.tensor_tensor(n_a, u3[:, 0, :, :], u3[:, 2, :, :], ALU.subtract))
                steps.mark(dve.tensor_tensor(n_c, u3[:, 1, :, :], q_c, ALU.add))
                steps.wait()
            steps.leave(L // UNROLL)

        def invert_norms(g):
            dve.wait_ge(rooted, g + 1)
            steps.done(dve.tensor_scalar(norm[:, :], norm[:, :], 1e-8, None, ALU.add))
            dve.reciprocal(norm[:, :], norm[:, :]).then_inc(norm_ready, 1)

        def normalize(g, j):
            dve.wait_ge(spread_copied, 4 * g + j + 1)
            dve.tensor_tensor(bc[:, j, :], ps[:, LIN + j, :], bc[:, j, :], ALU.mult).then_inc(bc_ready, 1)

        def inputs_and_outputs(g):
            at_g = lambda r, c, d: qs[:, r, c, bass.ds(g, 1), :, d:d + L].rearrange("p o b t -> p (o b) t")
            w_g = aw[:, 1, bass.ds(g, 1), :, :].rearrange("p o b t -> p (o b t)")
            ir = inv_root[:, bass.ds(g, 1)]
            mul = lambda out, x, y: steps.mark(dve.tensor_tensor(out, x, y, ALU.mult))
            sub = lambda out, x, y: steps.mark(dve.tensor_tensor(out, x, y, ALU.subtract))
            dve.wait_ge(bc_ready, 4 * g + 4)
            if not (isinstance(g, int) and g == 0):
                dve.wait_ge(y_done, 2 * g)
            dve.tensor_tensor(vg[:, :], f32(vh[:, bass.ds(g, 1), :]).rearrange("p o n -> p (o n)"),
                              f32(vl[:, bass.ds(g, 1), :]).rearrange("p o n -> p (o n)"), ALU.add).then_inc(vg_ready, 1)
            mul(v2, w_g, bc[:, 1, :])
            steps.wait()
            steps.done(dve.scalar_tensor_tensor(v1, bc[:, 0, :], ir, v2, ALU.mult, ALU.add))
            dve.tensor_tensor(v1, v1, w_g, ALU.mult).then_inc(w_used, 1)
            dve.wait_ge(w_used, g + 1)
            for r, out in ((0, g0), (1, g1)):
                mul(by_batch(ta), at_g(r, 0, 0), by_batch(v1))
                mul(by_batch(tb), at_g(r, 1, 0), by_batch(v2))
                steps.wait()
                steps.done(dve.tensor_tensor(out, ta, tb, ALU.add))
            mul(by_batch(ta), at_g(0, 0, 1), at_g(1, 1, 1))
            mul(by_batch(tb), at_g(1, 0, 1), at_g(0, 1, 1))
            steps.mark(dve.tensor_scalar(bc[:, 3, :], bc[:, 3, :], ir, None, ALU.mult))
            steps.wait()
            sub(v1, ta, tb)
            steps.wait()
            steps.mark(dve.reciprocal(v1, v1))
            for (ra, ca, xa), (rb, cb, xb), out in (((1, 1, 2), (1, 0, 3), e0), ((0, 0, 3), (0, 1, 2), e1)):
                mul(by_batch(ta), at_g(ra, ca, 1), by_batch(bc[:, xa, :]))
                mul(by_batch(tb), at_g(rb, cb, 1), by_batch(bc[:, xb, :]))
                steps.wait()
                sub(ta, ta, tb)
                steps.wait()
                last = dve.tensor_tensor(out, ta, v1, ALU.mult)
                if out is e0:
                    steps.done(last)
            last.then_inc(ge_ready, 1)
            dve.wait_ge(ge_ready, g + 1)

        def gated_output(g):
            for half in range(2):
                dve.wait_ge(head_done, 8 * g + 4 * half + 4)
                if half or not (isinstance(g, int) and g == 0):
                    dve.wait_ge(y_done, 2 * g + half)
                for n in range(2):
                    dve.tensor_tensor(gt[:, n, :, :], ps[:, GB[n], :].rearrange("p (a t) -> p a t", a=4),
                                      mask.unsqueeze(1).to_broadcast([P, 4, P]), ALU.mult).then_inc(gt_ready, 1)
            dve.wait_ge(y_done, 2 * g + 2)
            dve.wait_ge(gate_loaded, 16 * (g + 1))
            steps.done(dve.scalar_tensor_tensor(ta, vg[:, :], skip[:, bass.ds(g, 1)], ps[:, YB, :], ALU.mult, ALU.add))
            dve.tensor_tensor(qs[:, 0, 0, bass.ds(g, 1), :, 1:L + 1].rearrange("p o b t -> p (o b) t"), by_batch(ta),
                              aw[:, 1, bass.ds(g, 1), :, :].rearrange("p o b t -> p (o b) t"), ALU.mult).then_inc(y_ready, 1)
            dve.wait_ge(y_ready, g + 1)

        def group(g, products=True, out=True):
            if out:
                inputs_and_outputs(g - 1)
            if products:
                invert_norms(g)
            if out:
                gated_output(g - 1)
            if products:
                for j in range(4):
                    normalize(g, j)

        dve.sem_inc(scanned, 1)
        dve.wait_ge(scan_consts, 2 * 16)
        group(0, out=False)
        with dve.Fori(1, G) as g:
            steps.enter(g - 1, 22)
            group(g)
            steps.leave(G - 1)
        group(G, products=False)
        for cc in range(NM):
            dve.wait_ge(y_high, halves + cc + 1)
            dve.tensor_tensor(by_batch(vl[:, cc, :]), qs[:, 0, 0, cc, :, 1:L + 1], by_batch(f32(vh[:, cc, :])), ALU.subtract)\
               .then_inc(y_split, 1)
        for t in range(TT):
            if t < TT - 1:
                dve.wait_ge(out_done, outs + t + 1)
            else:
                dve.wait_ge(m.unit_done, out_unit + NM)
            dve.tensor_tensor(m.x[:, t, :], m.x[:, t, :], ps[:, LIN + t, :], ALU.add).then_inc(m.x_ready, 1)

    return tensor, scalar, vector, None


def bit_ffn(nc, m, first_unit, k):
    H = 2048
    NH = H // P
    HT = 4
    with ExitStack() as mem:
        sb = lambda name, shape, dt=F32: mem.enter_context(nc.sbuf_tensor("bf_" + name, shape, dt))
        w1q, w2q = sb("w1q", [P, KC, H], BF16), sb("w2q", [P, NH, D], BF16)
        w1, w2 = sb("w1", [P, KC, H]), sb("w2", [P, NH, D])
        rows = sb("rows", [P, TT, D])
        rq = sb("rq", [P, TT, D], BF16)
        xq = sb("xq", [P, KC, T], BF16)
        hid = sb("hid", [P, NH // 2, T])
        top = sb("top", [P, T])
        scaled, conv_y, magnitude = (sb(n, [P, 2, T]) for n in ("scaled", "conv_y", "magnitude"))
        inv_row = sb("inv_row", [P, T])
        diag = sb("diag", [P, TT, P])
        ones, ident16 = sb("ones", [P, P]), sb("ident16", [P, P], BF16)
        small = sb("small", [P, 256])
    stats = small[:, 0:24].rearrange("p (t n) -> p t n", n=6)
    mv = small[:, 24:32].rearrange("p (t n) -> p t n", n=2)
    ve, rstd, tmp = small[:, 32:36], small[:, 36:40], small[:, 40:44]
    row_max, row_scale, row_inv = small[:, 44:48], small[:, 48:52], small[:, 52:56]
    hid_max, hid_scale, hid_inv = small[:, 56:60], small[:, 60:64], small[:, 64:68]
    w_sums, w_sum, w_mean, w_scale = small[:, 72:104], small[:, 104:106], small[:, 106:108], small[:, 108:110]
    conv_w, conv_b = small[:, 112:160].rearrange("p (n j) -> p n j", j=3), small[:, 160:176]
    s = lambda name: m.sem("bf_" + name)
    released = m.shared("out_split", 0)
    consts, loaded = m.shared("stage_consts", 3 * 16)
    w_loaded = [s("w1_loaded"), s("w2_loaded")]
    summed, sum_ready, total_done, scale_ready = (s(n) for n in ("summed", "sum_ready", "total_done", "scale_ready"))
    shifted, w_ready = s("shifted"), s("w_ready")
    ln_stats, ln_guess, rq_ready, rows_turned, xq_ready = (s(n) for n in ("ln_stats", "ln_guess", "rq_ready", "rows_turned", "xq_ready"))
    diag_ready, spread_done, spread_ready = s("diag_ready"), s("spread_done"), s("spread_ready")
    h_done, scaled_ready, tap, conv_done, silu_done, mag_ready, top_ready = (
        s(n) for n in ("h_done", "scaled_ready", "tap", "conv_done", "silu_done", "mag_ready", "top_ready"))
    top_turned, diag2_ready, spread2_done, q_ready = (
        s(n) for n in ("top_turned", "diag2_ready", "spread2_done", "q_ready"))
    clipped, rounded = s("clipped"), s("rounded")
    out_done, outs = m.shared("out_done", TT)
    TURN, LIN, SPREAD, TOT = 0, 1, 5, 6
    ps = m.ps
    w1_flat = w1[:, :, :].rearrange("p c n -> p (c n)")
    w2_flat = w2[:, :, :].rearrange("p c n -> p (c n)")
    hidden = lambda n: hid[:, n, :] if n < NH // 2 else w1_flat[:, (n - NH // 2) * T:(n - NH // 2 + 1) * T]
    q2 = w2_flat.bitcast(BF16)[:, 0:NH * T].rearrange("p (n t) -> p n t", n=NH)

    def tensor(pe):
        def total(j):
            pe.wait_ge(sum_ready, j + 1)
            pe.matmul(ps[:, TOT, j:j + 1], ones[:, :], w_sum[:, j:j + 1], start=True, stop=True).then_inc(total_done, 1)

        pe.wait_ge(consts, loaded + 3 * 16)
        pe.wait_ge(m.consts, 16)
        total(0)
        turned = ps[:, TURN, :].bitcast(BF16)
        for c in range(KC):
            pe.wait_ge(rq_ready, 1)
            if c:
                pe.wait_ge(xq_ready, c)
            for t in range(TT):
                last = pe.transpose(turned[:, t * P:(t + 1) * P], rq[:, t, c * P:(c + 1) * P], ident16[:, :])
            last.then_inc(rows_turned, 1)
        pe.wait_ge(diag_ready, 1)
        for t in range(TT):
            last = pe.matmul(ps[:, SPREAD, t * P:(t + 1) * P], ones[:, :], diag[:, t, :], start=True, stop=True)
        last.then_inc(spread_done, 1)
        pe.wait_ge(xq_ready, KC)
        pe.wait_ge(w_ready, 4)
        for n in range(NH):
            if n >= 4:
                pe.wait_ge(scaled_ready, n - 3)
            for c in range(KC):
                last = pe.matmul(ps[:, LIN + n % 4, :], w1q[:, c, n * P:(n + 1) * P], xq[:, c, :], start=c == 0, stop=c == KC - 1)
            last.then_inc(h_done, 1)
            if n == 11:
                total(1)
        pe.wait_ge(top_ready, NH)
        for t in range(TT):
            last = pe.transpose(ps[:, TURN, t * P:(t + 1) * P], top[:, t * P:(t + 1) * P], m.ident[:, :])
        last.then_inc(top_turned, 1)
        pe.wait_ge(diag2_ready, 1)
        for t in range(TT):
            last = pe.matmul(ps[:, SPREAD, t * P:(t + 1) * P], ones[:, :], diag[:, t, :], start=True, stop=True)
        last.then_inc(spread2_done, 1)
        pe.wait_ge(w_ready, 8)
        for n in range(NH):
            pe.wait_ge(q_ready, n + 1)
            for t in range(TT):
                last = pe.matmul(ps[:, LIN + t, :], q2[:, n, t * P:(t + 1) * P], w2q[:, n, :], start=n == 0, stop=n == NH - 1)
                if n == NH - 1:
                    last.then_inc(out_done, 1)

    def scalar(act):
        act.wait_ge(m.x_loaded, 16)
        if k:
            act.wait_ge(*released)
        act.dma_start(w1_flat, m.d["ffn_w1"]).then_inc(w_loaded[0], 16)
        act.dma_start(w2_flat, m.d["ffn_w2"]).then_inc(w_loaded[1], 16)
        for out, src in ((conv_w, m.d["ffn_conv_w"]), (conv_b, m.d["ffn_conv_b"]), (ones[:, :], m.d["ones"])):
            act.dma_start(out, src).then_inc(consts, 16)
        act.wait_ge(ln_stats, 1)
        guess_rstd(act, rstd).then_inc(ln_guess, 1)
        def magnitudes(j, n):
            w, wq = ((w1_flat, w1q), (w2_flat, w2q))[j]
            act.wait_ge(w_loaded[j], 16)
            if j or n:
                act.wait_ge(summed, 4 * j + n)
            act.activation(wq[:, :, :].rearrange("p c n -> p (c n)")[:, n * H:(n + 1) * H], w[:, n * H:(n + 1) * H],
                           ACT.Abs, accum_out=w_sums[:, 4 * j + n:4 * j + n + 1]).then_inc(summed, 1)

        def scale_weights(j, n):
            cols = slice(n * H, (n + 1) * H)
            w = (w1_flat, w2_flat)[j][:, cols]
            act.wait_ge(scale_ready, j + 1)
            act.activation(w, w, ACT.Copy, scale=w_scale[:, j:j + 1]).then_inc(shifted, 1)

        def quantize_w2(n):
            if n < 8 and n % 2:
                magnitudes(1, n // 2)
            elif 8 <= n < 16 and n % 2:
                scale_weights(1, (n - 8) // 2)

        for n in range(4):
            magnitudes(0, n)
        for n in range(4):
            scale_weights(0, n)
        for c in range(KC):
            act.wait_ge(rows_turned, c + 1)
            act.copy(xq[:, c, :], ps[:, TURN, :].bitcast(BF16)[:, 0:T]).then_inc(xq_ready, 1)
        act.wait_ge(spread_done, 1)
        act.activation(inv_row[:, :], ps[:, SPREAD, :], ACT.Copy, scale=w_mean[:, 0:1]).then_inc(spread_ready, 1)
        for n in range(NH + 1):
            if n < NH:
                act.wait_ge(scaled_ready, n + 1)
                if n >= 2:
                    act.wait_ge(silu_done, n - 1)
                act.activation(conv_y[:, n % 2, :], scaled[:, n % 2, :], ACT.Identity, scale=conv_w[:, n, 1:2],
                               bias=conv_b[:, n:n + 1]).then_inc(tap, 1)
            if n:
                act.wait_ge(conv_done, n)
                act.activation(hidden(n - 1), conv_y[:, (n - 1) % 2, :], ACT.Silu).then_inc(silu_done, 1)
                act.wait_ge(silu_done, n)
                if n >= 3:
                    act.wait_ge(top_ready, n - 2)
                act.activation(magnitude[:, (n - 1) % 2, :], hidden(n - 1), ACT.Abs).then_inc(mag_ready, 1)
            quantize_w2(n)
        act.wait_ge(w_ready, 8)
        for n in range(NH):
            act.wait_ge(clipped, n + 1)
            act.activation(hidden(n), hidden(n), ACT.Copy, bias=MAGIC).then_inc(rounded, 1)
            act.wait_ge(rounded, n + 1)
            act.activation(q2[:, n, :], hidden(n), ACT.Copy, bias=-MAGIC).then_inc(q_ready, 1)

    def vector(dve):
        steps = m.dve_steps
        dve.wait_ge(m.x_loaded, 16)
        if k:
            dve.wait_ge(m.x_ready, TT * k)
        dve.wait_ge(m.consts, 16)
        steps.done(dve.tensor_copy(ident16[:, :], m.ident[:, :]))
        row_stats(dve, steps, m.x, stats, mv, ve, rstd).then_inc(ln_stats, 1)
        dve.wait_ge(ln_guess, 1)
        refine_rstd(dve, steps, ve, rstd, tmp)
        steps.done(normalize_rows(dve, rows, m.x, mv, rstd))

        def scales(top_values, scale, inverse):
            steps.done(dve.tensor_scalar(top_values, top_values, 1e-5, None, ALU.max))
            steps.done(dve.reciprocal(scale, top_values))
            steps.done(dve.tensor_scalar(scale, scale, 127.0, None, ALU.mult))
            steps.done(dve.reciprocal(inverse, scale))

        steps.done(dve.tensor_reduce(row_max, rows[:, :, :], AX.X, ALU.max, apply_absolute_value=True))
        scales(row_max, row_scale, row_inv)
        for t in range(TT):
            steps.mark(dve.tensor_scalar(rows[:, t, :], rows[:, t, :], row_scale[:, t:t + 1], 127.0, ALU.mult, ALU.min))
        steps.wait()
        steps.done(dve.tensor_scalar(rows[:, :, :], rows[:, :, :], -128.0, MAGIC, ALU.max, ALU.add))
        dve.tensor_scalar(rq[:, :, :], rows[:, :, :], -MAGIC, None, ALU.add).then_inc(rq_ready, 1)
        for t in range(TT):
            last = dve.tensor_scalar(diag[:, t, :], m.ident[:, :], row_inv[:, t:t + 1], None, ALU.mult)
        last.then_inc(diag_ready, 1)
        def weight_scale(j):
            dve.wait_ge(summed, 4 * j + 4)
            dve.tensor_reduce(w_sum[:, j:j + 1], w_sums[:, 4 * j:4 * j + 4], AX.X, ALU.add).then_inc(sum_ready, 1)
            dve.wait_ge(total_done, j + 1)
            steps.done(dve.tensor_scalar(w_mean[:, j:j + 1], ps[:, TOT, j:j + 1], 1.0 / (H * D), 1e-5, ALU.mult, ALU.max))
            dve.reciprocal(w_scale[:, j:j + 1], w_mean[:, j:j + 1]).then_inc(scale_ready, 1)

        def round_weights(j, n):
            w, wq = ((w1_flat, w1q), (w2_flat, w2q))[j]
            cols = slice(n * H, (n + 1) * H)
            dve.wait_ge(shifted, 4 * j + n + 1)
            steps.done(dve.tensor_scalar(w[:, cols], w[:, cols], 1.0, -1.0, ALU.min, ALU.max))
            dve.tensor_scalar(wq[:, :, :].rearrange("p c n -> p (c n)")[:, cols], w[:, cols], MAGIC, -MAGIC, ALU.add, ALU.add)\
               .then_inc(w_ready, 1)

        def quantize_w2(n):
            if n == 8:
                weight_scale(1)
            elif 10 <= n <= 16 and n % 2 == 0:
                round_weights(1, (n - 10) // 2)

        weight_scale(0)
        for n in range(4):
            round_weights(0, n)
        by_batch = lambda ap: ap.rearrange("p (b t) -> p b t", b=B)
        steps.done(dve.memset(top[:, :], 0.0))
        dve.wait_ge(spread_ready, 1)
        for n in range(NH + 2):
            if n < NH:
                dve.wait_ge(h_done, n + 1)
                if n >= 2:
                    dve.wait_ge(conv_done, n - 1)
                dve.tensor_tensor(scaled[:, n % 2, :], ps[:, LIN + n % 4, :], inv_row[:, :], ALU.mult).then_inc(scaled_ready, 1)
            if 1 <= n <= NH:
                c = n - 1
                dve.wait_ge(tap, c + 1)
                y, v = by_batch(conv_y[:, c % 2, :]), by_batch(scaled[:, c % 2, :])
                steps.done(dve.scalar_tensor_tensor(y[:, :, 1:], v[:, :, 0:L - 1], conv_w[:, c, 0:1], y[:, :, 1:],
                                                    ALU.mult, ALU.add))
                dve.scalar_tensor_tensor(y[:, :, 0:L - 1], v[:, :, 1:], conv_w[:, c, 2:3], y[:, :, 0:L - 1],
                                         ALU.mult, ALU.add).then_inc(conv_done, 1)
            if n >= 2:
                c = n - 2
                dve.wait_ge(mag_ready, c + 1)
                if c:
                    dve.wait_ge(top_ready, c)
                dve.tensor_tensor(top[:, :], top[:, :], magnitude[:, c % 2, :], ALU.max).then_inc(top_ready, 1)
            quantize_w2(n)
        dve.wait_ge(top_turned, 1)
        steps.done(dve.tensor_reduce(hid_max, ps[:, TURN, :].rearrange("p (t n) -> p t n", t=TT), AX.X, ALU.max))
        scales(hid_max, hid_scale, hid_inv)
        for t in range(TT):
            last = dve.tensor_scalar(diag[:, t, :], m.ident[:, :], hid_scale[:, t:t + 1], None, ALU.mult)
        last.then_inc(diag2_ready, 1)
        steps.done(dve.tensor_scalar(hid_inv, hid_inv, w_mean[:, 1:2], None, ALU.mult))
        dve.wait_ge(spread2_done, 1)
        for n in range(NH):
            steps.done(dve.tensor_tensor(hidden(n), hidden(n), ps[:, SPREAD, :], ALU.mult))
            dve.tensor_scalar(hidden(n), hidden(n), 127.0, -128.0, ALU.min, ALU.max).then_inc(clipped, 1)
        for t in range(TT):
            dve.wait_ge(out_done, outs + t + 1)
            dve.scalar_tensor_tensor(m.x[:, t, :], ps[:, LIN + t, :], hid_inv[:, t:t + 1], m.x[:, t, :], ALU.mult, ALU.add)\
               .then_inc(m.x_ready, 1)

    return tensor, scalar, vector, None


def context_attention(nc, m, first_unit, k):
    SCALE = 32 ** -0.5
    PAIRS = 8
    with ExitStack() as mem:
        sb = lambda name, shape, dt=F32: mem.enter_context(nc.sbuf_tensor("ca_" + name, shape, dt))
        ctx = sb("ctx", [P, 2, KC, KEYS])
        kt = sb("kt", [P, 2, KC, KEYS])
        xh, xl = sb("xh", [P, 2, KC, T], F32R), sb("xl", [P, 2, KC, T], F32R)
        rows = sb("rows", [P, TT, D])
        q = sb("q", [P, KC, B, L])
        q_pairs = sb("q_pairs", [P, 2, KC, 2, 2, L])
        v = sb("v", [P, 2, TT, D])
        p, pt = sb("p", [P, 2, KEYS]), sb("pt", [P, TT, P])
        o = sb("o", [P, KC, T])
        bias = sb("bias", [P, D])
        small = sb("small", [P, 56])
    nmax, rsum, rinv = small[:, 44:46], small[:, 46:48], small[:, 48:50]
    oh, ol = xh[:, 0], xl[:, 0]
    latents = NormalizedColumns(m, k, rows, small, xh[:, 1], xl[:, 1], (5, 6, 7, 0))
    s = lambda name: m.sem("ca_" + name)
    (ctx_loaded0, loads0), (ctx_loaded1, _) = (m.shared(f"ctx_loaded{n}", 16 * B // 2) for n in range(2))
    ctx_loaded = (ctx_loaded0, ctx_loaded1)
    bias_loaded, q_zero, q_ready, staged = s("bias_loaded"), s("q_zero"), s("q_ready"), s("staged")
    ctx_high, ctx_split, kt_ready = s("ctx_high"), s("ctx_split"), s("kt_ready")
    (lin_done, lins), (v_ready, vals) = m.shared("lin_done", 8 * B), m.shared("v_ready", 4 * B)
    (scores, before), (nmax_ready, _), (exp_done, _), (p_ready, _), (pt_done, _), (pt_ready, _), (pv_done, _), (o_ready, _) = (
        m.shared(n, PAIRS * B) for n in ("scores", "nmax_ready", "exp_done", "p_ready", "pt_done", "pt_ready", "pv_done", "o_ready"))
    (o_high, halves), (o_split, _) = m.shared("out_high", 4), m.shared("out_split", 4)
    out_done, outs = m.shared("out_done", TT - 1)
    SC, LIN, PTB, PV = (0, 5), 1, 6, 7
    QB = (5, 6, 7, 0)
    ps = m.ps
    first = lambda b, value: isinstance(b, int) and b == value

    def lhs(h, n, c):
        return h[:, n % RING_UNITS, c * P:(c + 1) * P]

    def tensor(pe):
        def queries(n):
            u = first_unit + n
            pe.wait_ge(m.unit_ready, u + 1)
            latents.wait_split(pe, KC)
            for c in range(KC):
                last = product(pe, ps[:, QB[n], :], (lhs(m.wh, u, c), lhs(m.wl, u, c)),
                               (xh[:, 1, c, :], xl[:, 1, c, :]), c == 0, c == KC - 1)
            last.then_inc(m.unit_done, 1)

        def linear(b, par, l, chunks):
            bank = ps[:, LIN + l % 4, :]
            if chunks[0] == 0 and l < 4 and not first(b, 0):
                pe.wait_ge(v_ready, vals + 4 * b + l - 3)
            elif chunks[0] == 0 and l >= 4:
                pe.wait_ge(kt_ready, 4 * b + l - 3)
            for c in chunks:
                if l == 0:
                    pe.wait_ge(ctx_split, KC * b + c + 1)
                x_c = (xh[:, par, c, :], xl[:, par, c, :])
                if l < 4:
                    u = first_unit + 4 + l
                    pe.wait_ge(m.unit_ready, u + 1)
                    last = product(pe, bank, (lhs(m.wh, u, c), lhs(m.wl, u, c)), x_c, c == 0, c == KC - 1)
                else:
                    u = first_unit + 8 + c
                    pe.wait_ge(m.unit_ready, u + 1)
                    t = slice((l - 4) * P, (l - 3) * P)
                    last = product(pe, bank, (x_c[0][:, t], x_c[1][:, t]),
                                   (m.wh[:, u % RING_UNITS, :], m.wl[:, u % RING_UNITS, :]), c == 0, c == KC - 1)
            if chunks[-1] == KC - 1:
                last.then_inc(lin_done, 1)

        def attention_scores(b, par, hp):
            if hp == 0:
                pe.wait_ge(staged, b + 1)
                pe.wait_ge(kt_ready, 4 * b + 4)
            if not (first(b, 0) and hp < 2):
                pe.wait_ge(exp_done, before + PAIRS * b + hp - 1)
            pe.matmul(ps[:, SC[hp % 2], :], q_pairs[:, par, hp // 2, hp % 2, :, :].rearrange("p e l -> p (e l)"),
                      kt[:, par, hp // 2, :], start=True, stop=True).then_inc(scores, 1)

        def probability_transposes(b, hp):
            pe.wait_ge(p_ready, before + PAIRS * b + hp + 1)
            if not (first(b, 0) and hp == 0):
                pe.wait_ge(pt_ready, before + PAIRS * b + hp)
            for t in range(TT):
                last = pe.transpose(ps[:, PTB, t * P:(t + 1) * P], p[:, hp % 2, t * P:(t + 1) * P], m.ident[:, :])
            last.then_inc(pt_done, 1)

        def values(b, par, hp):
            pe.wait_ge(pt_ready, before + PAIRS * b + hp + 1)
            pe.wait_ge(v_ready, vals + 4 * b + 4)
            if not (first(b, 0) and hp == 0):
                pe.wait_ge(o_ready, before + PAIRS * b + hp)
            for t in range(TT):
                last = pe.matmul(ps[:, PV, 0:P], v[:, par, t, (hp // 2) * P:(hp // 2 + 1) * P], pt[:, t, :],
                                 start=t == 0, stop=t == TT - 1)
            last.then_inc(pv_done, 1)

        def step(b, par, lin=True, att=True, carry=True):
            for hp in range(PAIRS):
                behind = (b - 1, 1 - par, hp - 1) if hp else (b - 2, par, PAIRS - 1)
                follow = att and (hp or carry)
                if att:
                    attention_scores(b - 1, 1 - par, hp)
                if lin:
                    linear(b, par, hp, range(0, 2))
                if follow:
                    probability_transposes(behind[0], behind[2])
                if lin:
                    linear(b, par, hp, range(2, 4))
                if follow:
                    values(*behind)

        for l in range(KC):
            linear(0, 0, l, range(KC))
        latents.tensor(pe)
        for n in range(KC):
            queries(n)
        for l in range(KC, 2 * KC):
            linear(0, 0, l, range(KC))
        pe.wait_ge(q_ready, KC)
        step(1, 1, carry=False)
        with pe.Fori(1, B // 2) as i:
            step(2 * i, 0)
            step(2 * i + 1, 1)
        pe.wait_ge(lin_done, lins + 8 * B)
        pe.sem_inc(m.unit_done, 8)
        step(B, 0, lin=False)
        probability_transposes(B - 1, PAIRS - 1)
        values(B - 1, 1, PAIRS - 1)

        for c in range(KC):
            u = first_unit + 12 + c
            pe.wait_ge(m.unit_ready, u + 1)
            pe.wait_ge(o_split, halves + c + 1)
            for t in range(TT):
                last = product(pe, ps[:, LIN + t, :], (oh[:, c, t * P:(t + 1) * P], ol[:, c, t * P:(t + 1) * P]),
                               (m.wh[:, u % RING_UNITS, :], m.wl[:, u % RING_UNITS, :]), c == 0, c == KC - 1)
                if c == KC - 1 and t < TT - 1:
                    last.then_inc(out_done, 1)
            last.then_inc(m.unit_done, 1)

    def scalar(act):
        act.wait_ge(m.x_loaded, 16)
        for b in range(2):
            act.dma_start(ctx[:, b, :, :], m.d["ctx_columns"][b]).then_inc(ctx_loaded[b], 16)
        act.dma_start(bias[:, :], m.d["ca_bias"]).then_inc(bias_loaded, 16)

        def high(b, par, c):
            if c == 0:
                act.wait_ge(ctx_loaded[par], loads0 + 8 * (b - par) + 16)
                if not first(b, 0):
                    act.wait_ge(lin_done, lins + 8 * (b - 1))
            act.copy(xh[:, par, c, :], ctx[:, par, c, :]).then_inc(ctx_high, 1)

        def stage_queries(b, par):
            if first(b, 0):
                act.wait_ge(q_zero, 1)
                act.wait_ge(q_ready, KC)
            for h in range(4):
                part = slice(32 * h, 32 * h + 32)
                last = act.copy(q_pairs[part, par, :, h // 2, h % 2, :],
                                q[part, :, bass.ds(b, 1), :].rearrange("p c o l -> p c (o l)"))
            last.then_inc(staged, 1)

        def exponentials(b, hp):
            act.wait_ge(nmax_ready, before + PAIRS * b + hp + 1)
            act.activation(p[:, hp % 2, :], ps[:, SC[hp % 2], :], ACT.Exp, bias=nmax[:, hp % 2:hp % 2 + 1],
                           accum_out=rsum[:, hp % 2:hp % 2 + 1]).then_inc(exp_done, 1)

        def transposed(b, hp):
            act.wait_ge(pt_done, before + PAIRS * b + hp + 1)
            if not (first(b, 0) and hp == 0):
                act.wait_ge(pv_done, before + PAIRS * b + hp)
            act.copy(pt[:, :, :].rearrange("p t n -> p (t n)"), ps[:, PTB, :]).then_inc(pt_ready, 1)

        def output(b, hp):
            act.wait_ge(pv_done, before + PAIRS * b + hp + 1)
            for e in range(2):
                part = slice(64 * (hp % 2) + 32 * e, 64 * (hp % 2) + 32 * e + 32)
                last = act.copy(o[part, hp // 2, bass.ds(b * L, L)], ps[part, PV, 64 * e:64 * e + 64])
            last.then_inc(o_ready, 1)

        def step(b, par, lin=True, att=True, carry=True, nxt=True):
            for hp in range(PAIRS):
                behind = (b - 1, hp - 1) if hp else (b - 2, PAIRS - 1)
                follow = att and (hp or carry)
                if att:
                    exponentials(b - 1, hp)
                if follow:
                    transposed(*behind)
                if lin and hp >= 4:
                    t = hp - 4
                    act.wait_ge(lin_done, lins + 8 * b + 5 + t)
                    act.copy(v[:, par, t, :], ps[:, LIN + t, :]).then_inc(v_ready, 1)
                if follow:
                    output(*behind)
                if lin and hp == 2:
                    stage_queries(b, par)
                if nxt and hp % 2:
                    high(b + 1, 1 - par, hp // 2)

        for c in range(KC):
            high(0, 0, c)
        latents.scalar_guess(act)
        latents.scalar_high(act)
        for n in range(KC):
            act.wait_ge(m.unit_done, first_unit + n + 1)
            act.activation(q[:, n, :, :].rearrange("p b l -> p (b l)"), ps[:, QB[n], :], ACT.Copy, scale=SCALE)\
               .then_inc(q_ready, 1)
        step(0, 0, att=False)
        step(1, 1, carry=False)
        with act.Fori(1, B // 2 - 1) as i:
            step(2 * i, 0)
            step(2 * i + 1, 1)
        step(B - 2, 0)
        step(B - 1, 1, nxt=False)
        step(B, 0, lin=False, nxt=False)
        transposed(B - 1, PAIRS - 1)
        output(B - 1, PAIRS - 1)
        act.wait_ge(o_ready, before + PAIRS * B)
        for c in range(KC):
            act.copy(oh[:, c, :], o[:, c, :]).then_inc(o_high, 1)

    def vector(dve):
        steps = m.dve_steps

        def low(b, par, c):
            dve.wait_ge(ctx_high, KC * b + c + 1)
            dve.tensor_tensor(xl[:, par, c, :], ctx[:, par, c, :], f32(xh[:, par, c, :]), ALU.subtract)\
               .then_inc(ctx_split, 1)

        def softmax(b, hp):
            slot = slice(hp % 2, hp % 2 + 1)
            dve.wait_ge(scores, before + PAIRS * b + hp + 1)
            dve.tensor_reduce(nmax[:, slot], ps[:, SC[hp % 2], :], AX.X, ALU.max, negate=True).then_inc(nmax_ready, 1)
            dve.wait_ge(exp_done, before + PAIRS * b + hp + 1)
            steps.done(dve.reciprocal(rinv[:, slot], rsum[:, slot]))
            dve.tensor_scalar(p[:, hp % 2, :], p[:, hp % 2, :], rinv[:, slot], None, ALU.mult).then_inc(p_ready, 1)

        def step(b, par, lin=True, att=True, nxt=True):
            for hp in range(PAIRS):
                if att:
                    softmax(b - 1, hp)
                if lin and hp < 4:
                    keys(b, par, hp)
                if nxt and hp % 2:
                    low(b + 1, 1 - par, hp // 2)

        def keys(b, par, l):
            dve.wait_ge(lin_done, lins + 8 * b + l + 1)
            dve.tensor_copy(kt[:, par, l, :], ps[:, LIN + l, :]).then_inc(kt_ready, 1)

        for c in range(KC):
            low(0, 0, c)
        latents.vector_rows(dve, steps)
        dve.memset(q_pairs[:, :, :, :, :, :].rearrange("p s c r e l -> p (s c r e l)"), 0.0).then_inc(q_zero, 1)
        for l in range(KC):
            keys(0, 0, l)
        latents.vector_low(dve)
        dve.wait_ge(bias_loaded, 16)
        latents.wait_rows(dve)
        for t in range(TT):
            steps.mark(dve.tensor_tensor(m.x[:, t, :], m.x[:, t, :], bias[:, :], ALU.add))
        steps.wait()
        for c in range(KC):
            low(1, 1, c)
        step(1, 1)
        with dve.Fori(1, B // 2 - 1) as i:
            steps.enter(i - 1, 16)
            step(2 * i, 0)
            step(2 * i + 1, 1)
            steps.leave(B // 2 - 2)
        step(B - 2, 0)
        step(B - 1, 1, nxt=False)
        step(B, 0, lin=False, nxt=False)
        for c in range(KC):
            dve.wait_ge(o_high, halves + c + 1)
            dve.tensor_tensor(ol[:, c, :], o[:, c, :], f32(oh[:, c, :]), ALU.subtract).then_inc(o_split, 1)
        for t in range(TT):
            if t < TT - 1:
                dve.wait_ge(out_done, outs + t + 1)
            else:
                dve.wait_ge(m.unit_done, first_unit + 16)
            dve.tensor_tensor(m.x[:, t, :], m.x[:, t, :], ps[:, LIN + t, :], ALU.add).then_inc(m.x_ready, 1)

    def loads(sp):
        with sp.Fori(1, B // 2) as i:
            for par in range(2):
                b = 2 * i + par
                sp.wait_ge(ctx_split, KC * (b - 1))
                sp.dma_start(ctx[:, par, :, :], m.d["ctx_columns"][bass.ds(b, 1)].rearrange("o p c n -> (o p) c n"))\
                  .then_inc(ctx_loaded[par], 16)

    return tensor, scalar, vector, loads


def linear_attention(nc, m, first_unit, k):
    HEADS, HD, FEATURES = 16, 32, 64
    PAIRS = HEADS // 2
    GROUP = 3
    GROUPS = (HEADS + GROUP - 1) // GROUP
    with ExitStack() as mem:
        sb = lambda name, shape, dt=F32: mem.enter_context(nc.sbuf_tensor("li_" + name, shape, dt))
        rows = sb("rows", [P, TT, D])
        xh, xl = sb("xh", [P, KC, T], F32R), sb("xl", [P, KC, T], F32R)
        qk = sb("qk", [P, 2, KC, T])
        feat = sb("feat", [P, 2, PAIRS, T])
        v = sb("v", [P, TT, HEADS, HD + 1])
        masked = sb("masked", [P, 2, TT, P])
        proj = sb("proj", [P, KC, 2, P])
        causal = sb("causal", [P, P])
        v_bias, out_bias = sb("v_bias", [P, D]), sb("out_bias", [P, D])
        small = sb("small", [P, 80])
    qk_bias = small[:, 44:52]
    inv = small[:, 52:52 + GROUP * TT].rearrange("p (h t) -> p h t", t=TT)
    latents = NormalizedColumns(m, k, rows, small, xh, xl, (0, 1, 2, 3))
    released = m.shared("out_split", 0)
    s = lambda name: m.sem("li_" + name)
    consts, loaded = m.shared("stage_consts", 4 * 16)
    proj_zero, proj_loaded, ones_ready = s("proj_zero"), s("proj_loaded"), s("ones_ready")
    q_ready, k_ready, v_done, v_ready = s("q_ready"), s("k_ready"), s("v_done"), s("v_ready")
    feat_done, fq_ready, fk_ready = s("feat_done"), s("fq_ready"), s("fk_ready")
    scores, mask_done, group_done, rows_out = s("scores"), s("mask_done"), s("group_done"), s("rows_out")
    o_turned = s("o_turned")
    (o_high, halves), (o_split, _) = m.shared("out_high", 4), m.shared("out_split", 4)
    out_done, outs = m.shared("out_done", TT - 1)
    QB, KB, VB, FB, SB, CB, OT, OB = 4, 0, 4, 0, 0, 2, 0, 4
    ps = m.ps

    def tensor(pe):
        latents.tensor(pe)
        for j, bank in enumerate((QB, KB)):
            for n in range(KC):
                u = first_unit + 4 * j + n
                pe.wait_ge(m.unit_ready, u + 1)
                at = u % RING_UNITS
                for c in range(KC):
                    latents.wait_split(pe, c + 1)
                    last = product(pe, ps[:, bank + n, :], (m.wh[:, at, c * P:(c + 1) * P], m.wl[:, at, c * P:(c + 1) * P]),
                                   (xh[:, c, :], xl[:, c, :]), c == 0, c == KC - 1)
                last.then_inc(m.unit_done, 1)
        for c in range(KC):
            u = first_unit + 8 + c
            pe.wait_ge(m.unit_ready, u + 1)
            for t in range(TT):
                if c == 0:
                    pe.wait_ge(q_ready, t + 1)
                last = product(pe, ps[:, VB + t, :], (xh[:, c, t * P:(t + 1) * P], xl[:, c, t * P:(t + 1) * P]),
                               (m.wh[:, u % RING_UNITS, :], m.wl[:, u % RING_UNITS, :]), c == 0, c == KC - 1)
            last.then_inc(m.unit_done, 1)
        pe.wait_ge(proj_loaded, 4 * 16)
        pe.wait_ge(q_ready, KC)
        pe.wait_ge(k_ready, KC)
        for pair in range(PAIRS):
            if pair >= 2:
                pe.wait_ge(fq_ready, pair - 1)
                pe.wait_ge(fk_ready, pair - 1)
            for j in range(2):
                pe.matmul(ps[:, FB + 2 * (pair % 2) + j, :], proj[:, pair // 2, pair % 2, :], qk[:, j, pair // 2, :],
                          start=True, stop=True).then_inc(feat_done, 1)
        pe.wait_ge(fq_ready, PAIRS)
        pe.wait_ge(fk_ready, PAIRS)
        pe.wait_ge(v_ready, TT)
        pe.wait_ge(ones_ready, 1)

        def context(h):
            pe.wait_ge(mask_done, h + 1)
            for t in range(TT):
                at = ((h % GROUP) * TT + t) * (HD + 1)
                last = pe.matmul(ps[:, CB + h // GROUP, at:at + HD + 1], masked[:, h % 2, t, :], v[:, t, h, :],
                                 start=True, stop=True)
            last.then_inc(group_done, 1)

        for h in range(HEADS):
            part = slice(FEATURES * (h % 2), FEATURES * (h % 2) + FEATURES)
            if h >= 2:
                pe.wait_ge(mask_done, h - 1)
            for t in range(TT):
                tok = slice(t * P, (t + 1) * P)
                last = pe.matmul(ps[:, SB + h % 2, tok], feat[part, 1, h // 2, tok], feat[part, 0, h // 2, tok],
                                 start=True, stop=True)
            last.then_inc(scores, 1)
            if h:
                context(h - 1)
        context(HEADS - 1)
        pe.wait_ge(rows_out, GROUPS)
        for c in range(KC):
            for t in range(TT):
                last = pe.transpose(ps[:, OT + c, t * P:(t + 1) * P], rows[:, t, c * P:(c + 1) * P], m.ident[:, :])
            last.then_inc(o_turned, 1)
        for c in range(KC):
            u = first_unit + 12 + c
            pe.wait_ge(m.unit_ready, u + 1)
            pe.wait_ge(o_split, halves + c + 1)
            for t in range(TT):
                last = product(pe, ps[:, OB + t, :], (xh[:, c, t * P:(t + 1) * P], xl[:, c, t * P:(t + 1) * P]),
                               (m.wh[:, u % RING_UNITS, :], m.wl[:, u % RING_UNITS, :]), c == 0, c == KC - 1)
                if c == KC - 1 and t < TT - 1:
                    last.then_inc(out_done, 1)
            last.then_inc(m.unit_done, 1)

    def scalar(act):
        act.wait_ge(m.x_loaded, 16)
        if k:
            act.wait_ge(*released)
        for out, src in ((causal[:, :], m.d["causal"]), (v_bias[:, :], m.d["v_bias"]), (out_bias[:, :], m.d["li_bias"]),
                         (qk_bias, m.d["qk_bias"])):
            act.dma_start(out, src).then_inc(consts, 16)
        act.wait_ge(proj_zero, 1)
        for h in range(4):
            act.dma_start(proj[32 * h:32 * h + 32, :, h // 2, 64 * (h % 2):64 * (h % 2) + 64], m.d["proj"][h])\
               .then_inc(proj_loaded, 16)
        latents.scalar_guess(act)
        latents.scalar_high(act)
        act.wait_ge(consts, loaded + 4 * 16)
        for n in range(KC):
            act.wait_ge(m.unit_done, first_unit + n + 1)
            act.activation(qk[:, 0, n, :], ps[:, QB + n, :], ACT.Identity, bias=qk_bias[:, n:n + 1]).then_inc(q_ready, 1)
        for pair in range(PAIRS):
            act.wait_ge(feat_done, 2 * pair + 1)
            act.activation(feat[:, 0, pair, :], ps[:, FB + 2 * (pair % 2), :], ACT.Relu).then_inc(fq_ready, 1)
        for c in range(KC):
            act.wait_ge(o_turned, c + 1)
            act.copy(xh[:, c, :], ps[:, OT + c, :]).then_inc(o_high, 1)

    def vector(dve):
        steps = m.dve_steps
        dve.wait_ge(m.x_loaded, 16)
        if k:
            dve.wait_ge(m.x_ready, TT * k)
        dve.memset(proj[:, :, :, :].rearrange("p c r n -> p (c r n)"), 0.0).then_inc(proj_zero, 1)
        latents.vector_rows(dve, steps)
        dve.memset(v[:, :, :, HD:HD + 1], 1.0).then_inc(ones_ready, 1)
        latents.vector_low(dve)
        dve.wait_ge(consts, loaded + 4 * 16)
        latents.wait_rows(dve)
        for t in range(TT):
            steps.mark(dve.tensor_tensor(m.x[:, t, :], m.x[:, t, :], out_bias[:, :], ALU.add))
        steps.wait()
        for n in range(KC):
            dve.wait_ge(m.unit_done, first_unit + 4 + n + 1)
            dve.tensor_scalar(qk[:, 1, n, :], ps[:, KB + n, :], qk_bias[:, 4 + n:5 + n], None, ALU.add).then_inc(k_ready, 1)
        dve.wait_ge(m.unit_done, first_unit + 12)
        by_head = lambda ap: ap.rearrange("p (h d) -> p h d", d=HD)
        for t in range(TT):
            dve.tensor_tensor(v[:, t, :, 0:HD], by_head(ps[:, VB + t, :]), by_head(v_bias[:, :]), ALU.add).then_inc(v_ready, 1)
        for pair in range(PAIRS):
            dve.wait_ge(feat_done, 2 * pair + 2)
            dve.tensor_scalar(feat[:, 1, pair, :], ps[:, FB + 2 * (pair % 2) + 1, :], 0.0, None, ALU.max).then_inc(fk_ready, 1)

        def divide(g):
            h0, h1 = g * GROUP, min((g + 1) * GROUP, HEADS)
            n = h1 - h0
            dve.wait_ge(group_done, h1)
            if g:
                dve.wait_ge(rows_out, g)
            out = ps[:, CB + g, 0:n * TT * (HD + 1)].rearrange("p (h t d) -> p h t d", h=n, t=TT)
            steps.done(dve.tensor_scalar(inv[:, 0:n, :], out[:, :, :, HD], 1e-6, None, ALU.add))
            steps.done(dve.reciprocal(inv[:, 0:n, :], inv[:, 0:n, :]))
            for t in range(TT):
                last = dve.tensor_tensor(by_head(rows[:, t, h0 * HD:h1 * HD]), out[:, :, t, 0:HD],
                                         inv[:, 0:n, t:t + 1].to_broadcast([P, n, HD]), ALU.mult)
            last.then_inc(rows_out, 1)

        for h in range(HEADS):
            dve.wait_ge(scores, h + 1)
            if h >= 2:
                dve.wait_ge(group_done, h - 1)
            dve.tensor_tensor(masked[:, h % 2, :, :], ps[:, SB + h % 2, :].rearrange("p (t n) -> p t n", t=TT),
                              causal[:, :].rearrange("p (o n) -> p o n", o=1).to_broadcast([P, TT, P]), ALU.mult)\
               .then_inc(mask_done, 1)
            if h % GROUP == 1 and h > GROUP:
                divide(h // GROUP - 1)
        for g in range((HEADS - 1) // GROUP - 1, GROUPS):
            divide(g)
        for c in range(KC):
            dve.wait_ge(o_high, halves + c + 1)
            dve.tensor_tensor(xl[:, c, :], ps[:, OT + c, :], f32(xh[:, c, :]), ALU.subtract).then_inc(o_split, 1)
        for t in range(TT):
            if t < TT - 1:
                dve.wait_ge(out_done, outs + t + 1)
            else:
                dve.wait_ge(m.unit_done, first_unit + 16)
            dve.tensor_tensor(m.x[:, t, :], m.x[:, t, :], ps[:, OB + t, :], ALU.add).then_inc(m.x_ready, 1)

    return tensor, scalar, vector, None


def experts(nc, m, first_unit, k):
    E, F = 8, 1024
    NF = F // P
    LIMIT, ALPHA = 9.0, 1.702
    with ExitStack() as mem:
        sb = lambda name, shape, dt=F32: mem.enter_context(nc.sbuf_tensor("ex_" + name, shape, dt))
        xh, xl = sb("xh", [P, KC, T], F32R), sb("xl", [P, KC, T], F32R)
        hh, hl = sb("hh", [P, NF, T], F32R), sb("hl", [P, NF, T], F32R)
        rows = sb("rows", [P, TT, D])
        g, u, sg, h = sb("g", [P, 2, T]), sb("u", [P, 2, T]), sb("sg", [P, 2, T]), sb("h", [P, 2, T])
        b1 = sb("b1", [P, E, NF, 2])
        b2 = sb("b2", [E, D])
        gw_raw = sb("gw_raw", [P, KC, E])
        gwh, gwl = sb("gwh", [P, KC, E], F32R), sb("gwl", [P, KC, E], F32R)
        before = sb("before", [P, E, E])
        small = sb("small", [P, 44])
        gates, rank, best, second, coef = (sb(n, [P, TT, E]) for n in ("gates", "rank", "best", "second", "coef"))
        greater, equal = sb("greater", [P, TT, E, E]), sb("equal", [P, TT, E, E])
        v1, v2, w1, w2 = (sb(n, [P, TT]) for n in ("v1", "v2", "w1", "w2"))
        coef_t = sb("coef_t", [E, T])
    UNITS = 3 * NF
    m.scalar_from = first_unit + RING_UNITS
    released = m.shared("out_split", 0)
    s = lambda name: m.sem("ex_" + name)
    consts, loaded = m.shared("stage_consts", 4 * 16)
    ln = NormalizedColumns(m, k, rows, small, xh, xl, (1, 2, 3, 4))
    gw_split, gates_done, diff_ready, diff_exp = (s(n) for n in ("gw_split", "gates_done", "diff_ready", "diff_exp"))
    coef_ready, coef_turned, coef_t_ready, bias_done, bias_added = (
        s(n) for n in ("coef_ready", "coef_turned", "coef_t_ready", "bias_done", "bias_added"))
    g_ready, u_ready, sg_ready, h_ready, h_high, h_split = (
        s(n) for n in ("g_ready", "u_ready", "sg_ready", "h_ready", "h_high", "h_split"))
    tile_done, added = s("tile_done"), s("added")
    LIN, OUT, GATE = 1, (0, 5, 6, 7), 5
    ps = m.ps

    def tensor(pe):
        ln.tensor(pe)
        ln.wait_split(pe, KC)
        pe.wait_ge(gw_split, 1)
        for t in range(TT):
            for c in range(KC):
                cols = slice(t * P, (t + 1) * P)
                last = product(pe, ps[:, GATE, t * E:(t + 1) * E], (xh[:, c, cols], xl[:, c, cols]),
                               (gwh[:, c, :], gwl[:, c, :]), c == 0, c == KC - 1)
        last.then_inc(gates_done, 1)

        def turn_weights():
            pe.wait_ge(coef_ready, 1)
            for t in range(TT):
                last = pe.transpose(ps[0:E, 6, t * P:(t + 1) * P], coef[:, t, :], m.ident[:, :])
            last.then_inc(coef_turned, 1)

        def output_biases():
            pe.wait_ge(coef_t_ready, 1)
            for t in range(TT):
                pe.matmul(ps[:, OUT[t], :], coef_t[:, t * P:(t + 1) * P], b2[:, :], start=True, stop=True).then_inc(bias_done, 1)

        def expert(e, is_first):
            for n in range(2 * NF):
                u0 = first_unit + n
                bank = LIN + n % 4
                pe.wait_ge(m.unit_ready, first_unit + 24 * e + (n + 1))
                if n >= 4 or not is_first:
                    pe.wait_ge((g_ready, u_ready)[n % 2], 8 * e + (n // 2 - 1))
                for c in range(KC):
                    w = (m.wh[:, u0 % RING_UNITS, c * P:(c + 1) * P], m.wl[:, u0 % RING_UNITS, c * P:(c + 1) * P])
                    last = product(pe, ps[:, bank, :], w, (xh[:, c, :], xl[:, c, :]), c == 0, c == KC - 1)
                last.then_inc(m.unit_done, 1)
                if is_first and n == 5:
                    turn_weights()
                if is_first and n == 8:
                    output_biases()
            for n in range(NF):
                at = 2 * NF + n
                slot = (first_unit + at) % RING_UNITS
                pe.wait_ge(m.unit_ready, first_unit + 24 * e + (at + 1))
                pe.wait_ge(h_split, 8 * e + (n + 1))
                for t in range(TT):
                    if n == 0:
                        if is_first:
                            pe.wait_ge(bias_added, t + 1)
                        else:
                            pe.wait_ge(added, 4 * e + (t - 3))
                    cols = slice(t * P, (t + 1) * P)
                    last = product(pe, ps[:, OUT[t], :], (hh[:, n, cols], hl[:, n, cols]),
                                   (m.wh[:, slot, :], m.wl[:, slot, :]), n == 0, n == NF - 1)
                    if n == NF - 1 and t < TT - 1:
                        last.then_inc(tile_done, 1)
                last.then_inc(m.unit_done, 1)

        expert(0, True)
        with pe.Fori(1, E) as e:
            expert(e, False)

    def scalar(act):
        act.wait_ge(m.x_loaded, 16)
        if k:
            act.wait_ge(*released)
        for out, src in ((b1[:, :, :, :], m.d["expert_b1"]), (b2[:, :], m.d["expert_b2"]), (gw_raw[:, :, :], m.d["gate_w"]),
                         (before[:, :, :], m.d["before"])):
            act.dma_start(out, src).then_inc(consts, 16)
        ln.scalar_guess(act)
        ln.scalar_high(act)
        act.wait_ge(diff_ready, 1)
        act.activation(w2[:, :], v2[:, :], ACT.Exp).then_inc(diff_exp, 1)

        def high_part(e, n):
            m.high_part(act, (first_unit // 8) + 3 * e + (n // 8 + 1), n % 8)

        def expert(e, is_first=False, is_last=False):
            for n in range(NF + 1):
                if is_first and n == 3:
                    act.wait_ge(coef_turned, 1)
                    act.copy(coef_t[:, :], ps[0:E, 6, :]).then_inc(coef_t_ready, 1)
                if n < NF:
                    act.wait_ge(m.unit_done, first_unit + UNITS * e + (2 * n + 2))
                    if n >= 2 or not is_first:
                        act.wait_ge(h_ready, 8 * e + (n - 1))
                    act.activation(u[:, n % 2, :], ps[:, LIN + (2 * n + 1) % 4, :], ACT.Identity,
                                   bias=b1[:, bass.ds(e, 1), n, 1:2].rearrange("p o n -> p (o n)")).then_inc(u_ready, 1)
                    high_part(e, 2 * n)
                    high_part(e, 2 * n + 1)
                    act.wait_ge(g_ready, 8 * e + (n + 1))
                    act.activation(sg[:, n % 2, :], g[:, n % 2, :], ACT.Sigmoid, scale=ALPHA).then_inc(sg_ready, 1)
                if n:
                    act.wait_ge(h_ready, 8 * e + n)
                    act.copy(hh[:, n - 1, :], h[:, (n - 1) % 2, :]).then_inc(h_high, 1)
            if not is_last:
                for n in range(2 * NF, UNITS):
                    high_part(e, n)

        expert(0, is_first=True)
        with act.Fori(1, E - 1) as e:
            expert(e)
        expert(E - 1, is_last=True)

    def vector(dve):
        steps = m.dve_steps
        if k:
            dve.wait_ge(m.x_ready, TT * k)
        ln.vector_rows(dve, steps)
        dve.wait_ge(consts, loaded + 4 * 16)
        steps.done(dve.tensor_copy(gwh[:, :, :], gw_raw[:, :, :]))
        dve.tensor_tensor(gwl[:, :, :], gw_raw[:, :, :], f32(gwh[:, :, :]), ALU.subtract).then_inc(gw_split, 1)
        ln.vector_low(dve)
        dve.wait_ge(gates_done, 1)
        steps.done(dve.tensor_copy(gates[:, :, :].rearrange("p t e -> p (t e)"), ps[:, GATE, 0:TT * E]))
        of_e = gates[:, :, :].unsqueeze(3).to_broadcast([P, TT, E, E])
        of_f = gates[:, :, :].unsqueeze(2).to_broadcast([P, TT, E, E])
        steps.mark(dve.tensor_tensor(greater[:, :, :, :], of_f, of_e, ALU.is_gt))
        steps.done(dve.tensor_tensor(equal[:, :, :, :], of_f, of_e, ALU.is_equal))
        flat = lambda ap: ap.rearrange("p t e f -> p t (e f)")
        steps.done(dve.tensor_tensor(flat(equal[:, :, :, :]), flat(equal[:, :, :, :]),
                                     before[:, :, :].rearrange("p e f -> p (e f)").unsqueeze(1).to_broadcast([P, TT, E * E]), ALU.mult))
        steps.done(dve.tensor_tensor(flat(greater[:, :, :, :]), flat(greater[:, :, :, :]), flat(equal[:, :, :, :]), ALU.add))
        steps.done(dve.tensor_reduce(rank[:, :, :], greater[:, :, :, :], AX.X, ALU.add))
        steps.mark(dve.tensor_scalar(best[:, :, :], rank[:, :, :], 0.0, None, ALU.is_equal))
        steps.mark(dve.tensor_scalar(second[:, :, :], rank[:, :, :], 1.0, None, ALU.is_equal))
        steps.mark(dve.tensor_reduce(v1[:, :], gates[:, :, :], AX.X, ALU.max))
        steps.wait()
        steps.done(dve.tensor_tensor(coef[:, :, :], gates[:, :, :], second[:, :, :], ALU.mult))
        steps.done(dve.tensor_reduce(v2[:, :], coef[:, :, :], AX.X, ALU.add))
        dve.tensor_tensor(v2[:, :], v2[:, :], v1[:, :], ALU.subtract).then_inc(diff_ready, 1)
        dve.wait_ge(diff_exp, 1)
        steps.done(dve.tensor_scalar(w1[:, :], w2[:, :], 1.0, None, ALU.add))
        steps.done(dve.reciprocal(w1[:, :], w1[:, :]))
        steps.mark(dve.tensor_tensor(w2[:, :], w2[:, :], w1[:, :], ALU.mult))
        spread = lambda ap: ap.unsqueeze(2).to_broadcast([P, TT, E])
        steps.done(dve.tensor_tensor(best[:, :, :], best[:, :, :], spread(w1[:, :]), ALU.mult))
        steps.done(dve.tensor_tensor(second[:, :, :], second[:, :, :], spread(w2[:, :]), ALU.mult))
        dve.tensor_tensor(coef[:, :, :], best[:, :, :], second[:, :, :], ALU.add).then_inc(coef_ready, 1)

        def expert(e, is_first):
            for n in range(NF + 1):
                if is_first and n == 5:
                    for t in range(TT):
                        dve.wait_ge(bias_done, t + 1)
                        dve.tensor_tensor(m.x[:, t, :], m.x[:, t, :], ps[:, OUT[t], :], ALU.add).then_inc(bias_added, 1)
                if n < NF:
                    s0 = n % 2
                    dve.wait_ge(m.unit_done, first_unit + 24 * e + (2 * n + 1))
                    if n or not is_first:
                        steps.wait()
                    dve.tensor_scalar(g[:, s0, :], ps[:, LIN + (2 * n) % 4, :], b1[:, bass.ds(e, 1), n, 0:1].rearrange("p o n -> p (o n)"),
                                      LIMIT, ALU.add, ALU.min).then_inc(g_ready, 1)
                    dve.wait_ge(u_ready, 8 * e + (n + 1))
                    steps.mark(dve.tensor_scalar(u[:, s0, :], u[:, s0, :], LIMIT, -LIMIT, ALU.min, ALU.max))
                    dve.wait_ge(sg_ready, 8 * e + (n + 1))
                    steps.done(dve.tensor_tensor(g[:, s0, :], g[:, s0, :], sg[:, s0, :], ALU.mult))
                    if n >= 2 or not is_first:
                        dve.wait_ge(h_split, 8 * e + (n - 1))
                    dve.scalar_tensor_tensor(h[:, s0, :], u[:, s0, :], 1.0, g[:, s0, :], ALU.add, ALU.mult).then_inc(h_ready, 1)
                if n:
                    dve.wait_ge(h_high, 8 * e + n)
                    dve.tensor_tensor(hl[:, n - 1, :], h[:, (n - 1) % 2, :], f32(hh[:, n - 1, :]), ALU.subtract).then_inc(h_split, 1)
            for t in range(TT):
                if t < TT - 1:
                    dve.wait_ge(tile_done, 3 * e + (t + 1))
                else:
                    dve.wait_ge(m.unit_done, first_unit + 24 * e + 24)
                dve.scalar_tensor_tensor(m.x[:, t, :], ps[:, OUT[t], :], coef[:, t, bass.ds(e, 1)], m.x[:, t, :], ALU.mult, ALU.add)\
                   .then_inc(added, 1)

        expert(0, True)
        with dve.Fori(1, E) as e:
            steps.enter(e - 1, 16)
            expert(e, False)
            steps.leave(E - 1)
        dve.wait_ge(added, TT * E)
        dve.sem_inc(m.x_ready, TT)

    return tensor, scalar, vector, None


class Memory:

    def __init__(self):
        self.sems = {}

    def shared(self, name, raised):
        if name not in self.sems:
            self.sems[name] = [self.sem(name), 0]
        sem, before = self.sems[name]
        self.sems[name][1] += raised
        return sem, before


def program(nc, d, out, stages):
    m = Memory()
    m.d = d
    n_blocks = sum(STAGE_BLOCKS[name] for name, _ in stages)
    with ExitStack() as whole:
        sb = lambda name, shape, dt=F32: whole.enter_context(nc.sbuf_tensor(name, shape, dt))
        m.sem = lambda name: whole.enter_context(nc.semaphore(name))
        m.x = sb("x_rows", [P, TT, D])
        m.ident = sb("ident", [P, P])
        m.wh, m.wl = sb("w_high", [P, RING_UNITS, 512], F32R), sb("w_low", [P, RING_UNITS, 512], F32R)
        w_raw = sb("w_raw", [P, 2, 4, 512])
        one, one_ready = sb("one", [P, 1]), m.sem("one_ready")
        m.ps = whole.enter_context(nc.psum_tensor("ps", [P, 8, 512], F32))
        m.consts, m.x_loaded, m.x_ready = m.sem("consts"), m.sem("x_loaded"), m.sem("x_ready")
        raw_loaded = [m.sem("raw_loaded0"), m.sem("raw_loaded1")]
        unit_high, m.unit_ready, m.unit_done = m.sem("unit_high"), m.sem("unit_ready"), m.sem("unit_done")
        stored = m.sem("stored")
        dve_steps = m.sem("dve_steps")
        scalar_high = m.sem("scalar_high")
        m.scalar_from = None

        def high_part(act, pair, at):
            n = 8 * pair + at
            act.wait_ge(raw_loaded[at // 4], 16 * (pair + 1))
            act.wait_ge(m.unit_done, n - 7)
            act.copy(m.wh[:, at, :], w_raw[:, at // 4, at % 4, :]).then_inc(scalar_high, 1)

        m.high_part = high_part
        first, made = 0, []
        for k, (name, stage) in enumerate(stages):
            made.append((first, STAGE_BLOCKS[name], stage(nc, m, 4 * first, k)))
            first += STAGE_BLOCKS[name]
        block = whole.enter_context(nc.Block())

        @block.sync
        def _(sp):
            def load_block(n, slot):
                if not isinstance(n, int) or n >= 2:
                    sp.wait_ge(m.unit_ready, 4 * (n - 1))
                sp.dma_start(w_raw[:, slot, :, :], d["weights"][bass.ds(n, 1)].rearrange("o p u n -> (o p) u n"))\
                  .then_inc(raw_loaded[slot], 16)

            sp.dma_start(m.x[:, :, :], d["x"]).then_inc(m.x_loaded, 16)
            sp.dma_start(m.ident[:, :], d["ident"]).then_inc(m.consts, 16)
            done = 0
            for first, count, (_, _, _, loads) in made:
                last = min(first + count + (1 if count else 0), n_blocks)
                while done < min(2, last):
                    load_block(done, done)
                    done += 1
                if last - done > 4:
                    if done % 2:
                        load_block(done, 1)
                        done += 1
                    with sp.Fori(done // 2, last // 2) as i:
                        load_block(2 * i, 0)
                        load_block(2 * i + 1, 1)
                    done = last // 2 * 2
                for n in range(done, last):
                    load_block(n, n % 2)
                done = max(done, last)
                if loads:
                    loads(sp)
            sp.wait_ge(m.x_ready, TT * len(stages))
            sp.dma_start(out, m.x[:, :, :]).then_inc(stored, 16)
            sp.wait_ge(stored, 16)

        @block.gpsimd
        def _(pool):
            def split(pair, first_pair=False, high=True):
                for slot in range(2):
                    if high:
                        pool.wait_ge(raw_loaded[slot], 16 * (pair + 1))
                    for u in range(4):
                        n, at = 8 * pair + 4 * slot + u, 4 * slot + u
                        if high:
                            if not first_pair:
                                pool.wait_ge(m.unit_done, n - 7)
                            pool.tensor_tensor(m.wh[:, at, :], w_raw[:, slot, u, :], one[:, :].to_broadcast([P, 512]), ALU.mult)\
                                .then_inc(unit_high, 1)
                            pool.wait_ge(unit_high, n + 1)
                        else:
                            pool.wait_ge(scalar_high, n + 1 - m.scalar_from)
                        pool.tensor_tensor(m.wl[:, at, :], w_raw[:, slot, u, :], f32(m.wh[:, at, :]), ALU.subtract)\
                            .then_inc(m.unit_ready, 1)

            pool.memset(one[:, :], 1.0).then_inc(one_ready, 1)
            pool.wait_ge(one_ready, 1)
            pairs = n_blocks // 2
            own = pairs if m.scalar_from is None else m.scalar_from // 8
            if own:
                split(0, first_pair=True)
            if own > 1:
                with pool.Fori(1, own) as i:
                    split(i)
            if pairs > own:
                with pool.Fori(own, pairs) as i:
                    split(i, high=False)

        @block.scalar
        def _(act):
            for _, _, (_, scalar, _, _) in made:
                scalar(act)

        @block.vector
        def _(dve):
            m.dve_steps = Steps(dve, dve_steps)
            for _, _, (_, _, vector, _) in made:
                vector(dve)

        @block.tensor
        def _(pe):
            for _, _, (tensor, _, _, _) in made:
                tensor(pe)


STAGES = (("latent_attention", latent_attention), ("oscillator", oscillator), ("bit_ffn", bit_ffn),
          ("context_attention", context_attention), ("linear_attention", linear_attention), ("experts", experts))


def columns_unit(w):
    k, n = w.shape
    return w.reshape(k // 128, 128, n // 512, 4, 128).transpose(2, 1, 3, 0, 4).reshape(n // 512, 128, 4, k)


def rows_unit(w):
    return w.reshape(-1, 4, 128, 512).transpose(0, 2, 1, 3)


def per_partition(v):
    return np.ascontiguousarray(v.reshape(-1, 128).T)


def lay_out(i):
    i = {k: np.asarray(v) for k, v in i.items()}
    d = {"x": i["x"].reshape(4, 128, 512).transpose(1, 0, 2), "ident": np.eye(128, dtype=np.float32)}
    blocks = []
    at = np.arange(128)
    halves = np.arange(512).reshape(2, 4, 2, 32).transpose(2, 0, 1, 3).reshape(512)
    wkv = i["L0_xattn_Wkv"]
    blocks += [columns_unit(i["L0_xattn_Wq"][:, halves]), columns_unit(wkv[:, :512][:, halves]),
               rows_unit(wkv[:, 512:]), rows_unit(i["L0_xattn_Wo"])]
    d["ctx_rows"] = i["ctx_1024"].reshape(8, 4, 128, 512).transpose(0, 2, 1, 3)
    for name in ("gamma_x", "beta_x", "gamma_l", "beta_l"):
        d[name] = per_partition(i["L0_xattn_" + name])
    freq = (1.0 / np.float32(10000.0) ** (np.arange(0, 64, 2, dtype=np.float32) / np.float32(64))).astype(np.float32)
    angle = np.tile(freq[:, None] * np.arange(512, dtype=np.float32)[None, :], (4, 1))
    d["rope_cos"], d["rope_sin"] = np.cos(angle), np.sin(angle)
    w_in, w_bc = i["L0_attn_W_in"], i["L0_attn_W_bc"]
    bc = w_bc.reshape(8, 4, 4, 32, 8, 128).transpose(0, 5, 2, 4, 1, 3).reshape(8, 128, 2, 4, 512)
    blocks += [columns_unit(w_in[1024:2048].T), columns_unit(w_in[:1024].T),
               bc.transpose(0, 2, 1, 3, 4).reshape(16, 128, 4, 512), rows_unit(i["L0_attn_W_out"].T)]
    params = w_in[2048:].reshape(32, 2, 512).transpose(1, 0, 2).reshape(64, 512)
    d["w_params"] = np.concatenate([params, params]).T.reshape(4, 128, 128).transpose(1, 0, 2)
    d["conv_w"] = i["L0_attn_dw_weight"].reshape(8, 128, 4).transpose(1, 0, 2)
    d["conv_b"], d["skip"] = per_partition(i["L0_attn_dw_bias"]), per_partition(i["L0_attn_skip"])
    d["a_log"] = i["L0_attn_A_log"].reshape(8, 4, 32).transpose(1, 2, 0).reshape(128, 8)
    d["dt_bias"] = i["L0_attn_dt_bias"][:, None]
    select = np.zeros((128, 16, 128), np.float32)
    for n in range(16):
        for p in range(128):
            select[32 * (n // 8) + 4 * (n % 8) + p // 32, n, p] = 1
    d["select"] = select
    d["causal"] = ((at[:, None] // 64 == at[None, :] // 64) & (at[:, None] <= at[None, :])).astype(np.float32)
    pick = (at[:, None] // 32 == np.arange(32)[None, :]).astype(np.float32)
    d["pick"], d["spread"] = pick, (at[None, :] // 32 == at[:, None] % 32).astype(np.float32)
    d["ffn_w1"] = i["L0_ffn_w1"].T.reshape(4, 128, 2048).transpose(1, 0, 2).reshape(128, 8192)
    d["ffn_w2"] = i["L0_ffn_w2"].T.reshape(16, 128, 512).transpose(1, 0, 2).reshape(128, 8192)
    d["ffn_conv_w"] = i["L0_ffn_conv_w"].reshape(16, 128, 3).transpose(1, 0, 2)
    d["ffn_conv_b"] = per_partition(i["L0_ffn_conv_b"])
    d["ones"] = np.ones((128, 128), np.float32)
    wkv = i["L1_xattn_Wkv"]
    blocks += [columns_unit(i["L1_xattn_Wq"].T), columns_unit(wkv[:512].T), rows_unit(wkv[512:].T),
               rows_unit(i["L1_xattn_Wout"].T)]
    d["ctx_columns"] = i["ctx_1024"].reshape(8, 512, 4, 128).transpose(0, 3, 2, 1)
    d["ca_bias"] = np.broadcast_to(i["L1_xattn_bout"], (128, 512))
    w, b = i["L1_attn_qkv_w"], i["L1_attn_qkv_b"]
    blocks += [columns_unit(w[:, :512]), columns_unit(w[:, 512:1024]), rows_unit(w[:, 1024:]), rows_unit(i["L1_attn_out_w"])]
    d["qk_bias"] = per_partition(b[:1024])
    d["v_bias"], d["li_bias"] = np.broadcast_to(b[1024:], (128, 512)), np.broadcast_to(i["L1_attn_out_b"], (128, 512))
    d["proj"] = i["L1_attn_proj"].reshape(4, 4, 32, 64).transpose(1, 2, 0, 3)
    w1 = i["L1_ffn_dense_1_w"].reshape(8, 4, 2, 128, 2, 4, 128).transpose(0, 1, 6, 2, 4, 5, 3).reshape(8, 4, 128, 4, 512)
    w2 = i["L1_ffn_dense_2_w"].transpose(0, 2, 1).reshape(8, 2, 4, 128, 512).transpose(0, 1, 3, 2, 4)
    blocks.append(np.concatenate([w1, w2], axis=1).reshape(48, 128, 4, 512))
    d["expert_b1"] = i["L1_ffn_dense_1_b"].reshape(8, 8, 128, 2).transpose(2, 0, 1, 3)
    d["expert_b2"] = i["L1_ffn_dense_2_b"]
    d["gate_w"] = i["L1_ffn_gate_w"].reshape(4, 128, 8).transpose(1, 0, 2)
    e = np.arange(8)
    d["before"] = np.broadcast_to((e[None, :] < e[:, None]).astype(np.float32), (128, 8, 8))
    d["weights"] = np.concatenate(blocks)
    return {k: np.ascontiguousarray(v) for k, v in d.items()}


def kernel(**inputs):
    import concourse.bacc as _bacc
    from concourse.bass_utils import run_bass_kernel_spmd as _run

    nc = _bacc.Bacc("TRN2", target_bir_lowering=False, num_devices=1)
    arrays = lay_out(inputs)
    d = {name: nc.dram_tensor("in_" + name, a.shape, mybir.dt.from_np(a.dtype), kind="ExternalInput").ap()
         for name, a in arrays.items()}
    out = nc.dram_tensor("out_x", (P, TT, D), F32, kind="ExternalOutput").ap()
    program(nc, d, out, STAGES)
    r = _run(nc, [{"in_" + name: a for name, a in arrays.items()}], core_ids=[0])
    return np.ascontiguousarray(r.results[0]["out_x"].transpose(1, 0, 2).reshape(B, L, D))
```

```python
from contextlib import ExitStack

import concourse.bass as bass
from concourse import mybir
import numpy as np

P = 128
T = 512
D = 512
B = 8
L = 64
KEYS = 512
KC = D // P
TT = T // P
EPS = 1e-5
MAGIC = 12582912.0

F32 = mybir.dt.float32
F32R = mybir.dt.float32r
BF16 = mybir.dt.bfloat16
ALU = mybir.AluOpType
ACT = mybir.ActivationFunctionType
AX = mybir.AxisListType

STAGE_BLOCKS = {"latent_attention": 4, "oscillator": 22, "bit_ffn": 0, "context_attention": 4,
                "linear_attention": 4, "experts": 48}
RING_UNITS = 8


class Steps:

    def __init__(self, eng, sem):
        self.eng, self.sem, self.base, self.n = eng, sem, 0, 0

    def mark(self, ins):
        ins.then_inc(self.sem, 1)
        self.n += 1

    def wait(self):
        self.eng.wait_ge(self.sem, self.base + self.n)

    def done(self, ins):
        self.mark(ins)
        self.wait()

    def enter(self, i, per_trip):
        self.before, self.per_trip = self.base + self.n, per_trip
        self.base, self.n = self.before + i * per_trip, 0

    def leave(self, trips):
        assert self.n == self.per_trip, f"{self.n} steps a trip"
        self.base, self.n = self.before + trips * self.per_trip, 0


def product(pe, out, lhs, rhs, start, stop):
    (lh, ll), (rh, rl) = lhs, rhs
    pe.matmul(out, lh, rh, start=start, stop=False)
    pe.matmul(out, lh, rl, start=False, stop=False)
    return pe.matmul(out, ll, rh, start=False, stop=stop)


def f32(ap):
    return ap.bitcast(F32)


def tile_stats(dve, steps, rows, stats, t):
    steps.mark(dve.bn_stats(stats[:, t, :], rows[:, t, :]))


def join_stats(dve, steps, stats, mean_var, var_eps, rstd):
    steps.wait()
    mean, half_gap = mean_var[:, :, 0], mean_var[:, :, 1]
    steps.mark(dve.tensor_tensor(mean, stats[:, :, 1], stats[:, :, 4], ALU.add))
    steps.mark(dve.tensor_tensor(half_gap, stats[:, :, 1], stats[:, :, 4], ALU.subtract))
    steps.mark(dve.tensor_tensor(var_eps, stats[:, :, 2], stats[:, :, 5], ALU.add))
    steps.wait()
    steps.mark(dve.tensor_scalar(mean, mean, 0.5, None, ALU.mult))
    steps.mark(dve.tensor_tensor(half_gap, half_gap, half_gap, ALU.mult))
    steps.mark(dve.tensor_scalar(var_eps, var_eps, 1.0 / D, EPS, ALU.mult, ALU.add))
    steps.wait()
    steps.done(dve.scalar_tensor_tensor(var_eps, half_gap, 0.25, var_eps, ALU.mult, ALU.add))
    return dve.reciprocal(rstd, var_eps)


def row_stats(dve, steps, rows, stats, mean_var, var_eps, rstd):
    for t in range(TT):
        tile_stats(dve, steps, rows, stats, t)
    return join_stats(dve, steps, stats, mean_var, var_eps, rstd)


def tile_added(dve, m, k, t, add):
    add.then_inc(m.x_ready, 1)
    dve.wait_ge(m.x_ready, TT * k + t + 1)
    tile_stats(dve, m.dve_steps, m.x, m.norm.stats, t)


def guess_rstd(act, rstd):
    return act.activation(rstd, rstd, ACT.Sqrt)


def refine_rstd(dve, steps, var_eps, rstd, tmp):
    steps.done(dve.tensor_tensor(tmp, rstd, rstd, ALU.mult))
    steps.done(dve.tensor_tensor(tmp, tmp, var_eps, ALU.mult))
    steps.done(dve.tensor_scalar(tmp, tmp, -0.5, 1.5, ALU.mult, ALU.add))
    steps.done(dve.tensor_tensor(rstd, rstd, tmp, ALU.mult))


def normalize_rows(dve, out, rows, mean_var, rstd):
    for t in range(TT):
        last = dve.tensor_scalar(out[:, t, :], rows[:, t, :], mean_var[:, t, 0:1], rstd[:, t:t + 1],
                                 ALU.subtract, ALU.mult)
    return last


class NormMemory:

    def __init__(self, sb):
        small = sb("norm_small", [P, 48])
        self.stats = small[:, 0:24].rearrange("p (t n) -> p t n", n=6)
        self.mv = small[:, 24:32].rearrange("p (t n) -> p t n", n=2)
        self.ve, self.rstd, self.tmp, self.unused = small[:, 32:36], small[:, 36:40], small[:, 40:44], small[:, 44:45]


def x_stats(dve, m, k):
    n = m.norm
    if k:
        dve.wait_ge(m.x_ready, TT * k)
    else:
        dve.wait_ge(m.x_loaded, 16)
        for t in range(TT):
            tile_stats(dve, m.dve_steps, m.x, n.stats, t)
    return join_stats(dve, m.dve_steps, n.stats, n.mv, n.ve, n.rstd)


def x_guess(act, m, stats_ready, before):
    act.wait_ge(m.consts, 16)
    act.activation(m.norm.unused, m.ident[:, 0:1], ACT.Sqrt)
    act.wait_ge(stats_ready, before + 1)
    return guess_rstd(act, m.norm.rstd)


class NormalizedColumns:

    def __init__(self, m, k, rows, high, low, banks):
        self.m, self.k, self.rows, self.high, self.low, self.banks = m, k, rows, high, low, banks
        (self.stats_ready, self.uses), (self.guessed, _), (self.rows_ready, self.rows_before) = (
            m.shared("norm_" + n, 1) for n in ("stats", "guess", "rows"))
        (self.turned, self.chunks), (self.high_ready, _), (self.split, _) = (
            m.shared("norm_" + n, KC) for n in ("turned", "high", "split"))

    def wait_rows(self, eng):
        eng.wait_ge(self.rows_ready, self.rows_before + 1)

    def wait_split(self, eng, chunks):
        eng.wait_ge(self.split, self.chunks + chunks)

    def vector_rows(self, dve, steps):
        x_stats(dve, self.m, self.k).then_inc(self.stats_ready, 1)
        dve.wait_ge(self.guessed, self.uses + 1)
        n = self.m.norm
        refine_rstd(dve, steps, n.ve, n.rstd, n.tmp)
        normalize_rows(dve, self.rows, self.m.x, n.mv, n.rstd).then_inc(self.rows_ready, 1)

    def vector_low(self, dve):
        for c in range(KC):
            dve.wait_ge(self.high_ready, self.chunks + c + 1)
            dve.tensor_tensor(self.low[:, c, :], self.m.ps[:, self.banks[c], :], f32(self.high[:, c, :]), ALU.subtract)\
               .then_inc(self.split, 1)

    def scalar_guess(self, act):
        x_guess(act, self.m, self.stats_ready, self.uses).then_inc(self.guessed, 1)

    def scalar_high(self, act):
        for c in range(KC):
            act.wait_ge(self.turned, self.chunks + c + 1)
            act.copy(self.high[:, c, :], self.m.ps[:, self.banks[c], :]).then_inc(self.high_ready, 1)

    def tensor(self, pe):
        pe.wait_ge(self.m.consts, 16)
        self.wait_rows(pe)
        for c in range(KC):
            for t in range(TT):
                last = pe.transpose(self.m.ps[:, self.banks[c], t * P:(t + 1) * P], self.rows[:, t, c * P:(c + 1) * P],
                                    self.m.ident[:, :])
            last.then_inc(self.turned, 1)


def latent_attention(nc, m, first_unit, k):
    SCALE = 64 ** -0.5
    PAIRS = 4
    NK = KEYS + L
    with ExitStack() as mem:
        sb = lambda name, shape, dt=F32: mem.enter_context(nc.sbuf_tensor("la_" + name, shape, dt))
        ctx = sb("ctx", [P, 2, TT, D])
        xh, xl = sb("xh", [P, 2, KC, T], F32R), sb("xl", [P, 2, KC, T], F32R)
        y = sb("y", [P, 2, T])
        q = sb("q", [P, KC, B, L])
        q_pairs = sb("q_pairs", [P, 2, PAIRS, 2, L])
        kl = sb("kl", [P, PAIRS, B, L])
        kl_batch = sb("kl_batch", [P, 2, PAIRS, L])
        vl = sb("vl", [P, TT * D])
        vl_batch = sb("vl_batch", [P, D])
        kt = sb("kt", [P, KC, KEYS])
        kt_pairs = sb("kt_pairs", [P, 2, PAIRS, KEYS])
        v = sb("v", [P, 2, TT, D])
        cos, sin = sb("cos", [P, KEYS]), sb("sin", [P, KEYS])
        by_sin = sb("by_sin", [P, 2, KEYS])
        p = sb("p", [P, 2, NK])
        pt = sb("pt", [P, TT + 1, P])
        o = sb("o", [P, PAIRS, T])
        small = sb("small", [P, 72])
    gx, bx, gl, bl = (small[:, KC * n:KC * n + KC] for n in range(4))
    stats, mv = small[:, 16:40].rearrange("p (t n) -> p t n", n=6), small[:, 40:48].rearrange("p (t n) -> p t n", n=2)
    ve, rstd, tmp = small[:, 48:52], small[:, 52:56], small[:, 56:60]
    nmax, rsum, rinv = small[:, 60:62], small[:, 62:64], small[:, 64:66]
    oh, ol = xh[:, 0], xl[:, 0]
    x = m.x
    s = lambda name: m.sem("la_" + name)
    consts, loaded = m.shared("stage_consts", 6 * 16)
    x_loaded = m.x_loaded
    (ctx_loaded0, _), (ctx_loaded1, _) = (m.shared(f"ctx_loaded{n}", 16 * B // 2) for n in range(2))
    ctx_loaded = (ctx_loaded0, ctx_loaded1)
    (norm_stats, norms), (norm_guess, _) = m.shared("norm_stats", 2 + B), m.shared("norm_guess", 2 + B)
    lat_rows, rows_ready, values_staged = s("lat_rows"), s("rows_ready"), s("values_staged")
    (q_zero, _), (staged, _) = m.shared("q_zero", 1), m.shared("queries_staged", B)
    lat_done, lat_out = s("lat_done"), s("lat_out")
    xt_done, y_ready, x_split = s("xt_done"), s("y_ready"), s("x_split")
    (lin_done, _), (v_ready, _) = m.shared("lin_done", 8 * B), m.shared("v_ready", 4 * B)
    rotated, kl_merged, merged = s("rotated"), s("kl_merged"), (s("merged0"), s("merged1"))
    (scores, _), (nmax_ready, _), (exp_done, _), (p_ready, _), (pt_done, _), (pt_ready, _), (pv_done, _), (o_ready, _) = (
        m.shared(n, PAIRS * B) for n in ("scores", "nmax_ready", "exp_done", "p_ready", "pt_done", "pt_ready", "pv_done", "o_ready"))
    (o_high, halves), (o_split, _) = m.shared("out_high", 4), m.shared("out_split", 4)
    out_done, outs = m.shared("out_done", TT - 1)
    XT, LIN, PVB, SC, PTB = 0, 1, 4, 5, 7
    LB = [1, 2, 3, 1, 2, 3, 1, 2]
    OUT = [1, 2, 3, 0]
    ps = m.ps
    sc_all = ps[:, SC:SC + 2, :].rearrange("p a n -> p (a n)")[:, 0:NK]
    of_batch = lambda par: slice(L * par, L * par + L)
    pt5 = lambda par: ps[of_batch(par), PVB, 0:128]
    pv = ps[:, PVB, 128:256]
    first = lambda b, value: isinstance(b, int) and b == value
    CHUNK = [0, 2, 1, 3]

    def lhs(h, n, c):
        return h[:, n % RING_UNITS, c * P:(c + 1) * P]

    def tensor(pe):
        def transposes(b, par, c):
            for t in range(TT):
                last = pe.transpose(ps[:, XT, t * P:(t + 1) * P], ctx[:, par, t, c * P:(c + 1) * P], m.ident[:, :])
            last.then_inc(xt_done, 1)

        def context_transposes(b, par, c):
            if c == 0:
                pe.wait_ge(rows_ready, b + 1)
            pe.wait_ge(y_ready, KC * (b + 1) + c)
            transposes(b, par, c)

        pe.wait_ge(m.consts, 16)
        pe.wait_ge(lat_rows, 1)
        for c in range(KC):
            if c:
                pe.wait_ge(y_ready, c)
            transposes(0, 1, c)
        for j in range(2):
            for n in range(KC):
                u = first_unit + 4 * j + n
                pe.wait_ge(m.unit_ready, u + 1)
                pe.wait_ge(x_split, KC)
                if j:
                    pe.wait_ge(lat_out, n + 1)
                for c in range(KC):
                    last = product(pe, ps[:, LIN + n, :], (lhs(m.wh, u, c), lhs(m.wl, u, c)),
                                   (xh[:, 1, c, :], xl[:, 1, c, :]), c == 0, c == KC - 1)
                last.then_inc(lat_done if j else m.unit_done, 1)
            for c in (2 * j, 2 * j + 1):
                context_transposes(0, 0, c)
        for t in range(TT):
            pe.wait_ge(lat_out, KC + t + 1)
            for c in range(KC):
                u = first_unit + 8 + c
                pe.wait_ge(m.unit_ready, u + 1)
                last = product(pe, ps[:, LIN + t, :],
                               (xh[:, 1, c, t * P:(t + 1) * P], xl[:, 1, c, t * P:(t + 1) * P]),
                               (m.wh[:, u % RING_UNITS, :], m.wl[:, u % RING_UNITS, :]), c == 0, c == KC - 1)
            last.then_inc(lat_done, 1)

        def linear(b, par, l, chunks=range(KC)):
            if l == 0:
                pe.wait_ge(x_split, KC * (b + 2))
            bank = ps[:, LB[l], :]
            if chunks[0] == 0 and l < 3:
                if not first(b, 0):
                    pe.wait_ge(v_ready, 4 * b + (-1, 0, -2)[l])
            elif chunks[0] == 0 and l < 7:
                pe.wait_ge(rotated, 2 * b + (1 if l < 5 else 2))
            elif chunks[0] == 0:
                pe.wait_ge(v_ready, 4 * b + 1)
            for c in chunks:
                x_c = (xh[:, par, c, :], xl[:, par, c, :])
                if l < 4:
                    u = first_unit + 4 + CHUNK[l]
                    last = product(pe, bank, (lhs(m.wh, u, c), lhs(m.wl, u, c)), x_c, c == 0, c == KC - 1)
                else:
                    u = first_unit + 8 + c
                    t = slice((l - 4) * P, (l - 3) * P)
                    last = product(pe, bank, (x_c[0][:, t], x_c[1][:, t]),
                                   (m.wh[:, u % RING_UNITS, :], m.wl[:, u % RING_UNITS, :]), c == 0, c == KC - 1)
            if chunks[-1] == KC - 1:
                last.then_inc(lin_done, 1)

        def attention_scores(b, par, hp):
            if hp == 0:
                pe.wait_ge(merged[par], 64 * (b - par) + 128)
                pe.wait_ge(staged, b + 1)
            if not (first(b, 0) and hp == 0):
                pe.wait_ge(exp_done, 4 * b + hp)
            pair = q_pairs[:, par, hp, :, :].rearrange("p e l -> p (e l)")
            pe.matmul(sc_all[:, 0:KEYS], pair, kt_pairs[:, par, hp, :], start=True, stop=True)
            pe.matmul(sc_all[:, KEYS:NK], pair, kl_batch[:, par, hp, :], start=True, stop=True).then_inc(scores, 1)

        def probability_transposes(b, par, hp):
            pe.wait_ge(p_ready, 4 * b + hp + 1)
            if not (first(b, 0) and hp == 0):
                pe.wait_ge(pt_ready, 4 * b + hp)
                pe.wait_ge(o_ready, 4 * b + hp)
            for t in range(TT):
                pe.transpose(ps[:, PTB, t * P:(t + 1) * P], p[:, hp % 2, t * P:(t + 1) * P], m.ident[:, :])
            pe.matmul(pt5(par), p[:, hp % 2, KEYS:NK], m.ident[:, :], start=True, stop=True).then_inc(pt_done, 1)

        def values(b, par, hp):
            pe.wait_ge(pt_ready, 4 * b + hp + 1)
            pe.wait_ge(v_ready, 4 * b + 4)
            pe.wait_ge(values_staged, b + 1)
            cols = slice(hp * P, (hp + 1) * P)
            for t in range(TT):
                pe.matmul(pv, v[:, par, t, cols], pt[:, t, :], start=t == 0, stop=False)
            pe.matmul(pv, vl_batch[of_batch(par), cols], pt[of_batch(par), TT, :],
                      start=False, stop=True).then_inc(pv_done, 1)

        def project(t, chunks):
            pe.wait_ge(o_split, halves + t + 1)
            for c in chunks:
                u = first_unit + 12 + c
                pe.wait_ge(m.unit_ready, u + 1)
                last = product(pe, ps[:, OUT[t], :], (oh[:, c, t * P:(t + 1) * P], ol[:, c, t * P:(t + 1) * P]),
                               (m.wh[:, u % RING_UNITS, :], m.wl[:, u % RING_UNITS, :]), c == 0, c == KC - 1)
                if t == TT - 1:
                    last.then_inc(m.unit_done, 1)
                elif c == KC - 1:
                    last.then_inc(out_done, 1)

        def step(b, par, lin=True, att=True, nxt=True, carry=True, release=False, out=False):
            for hp in range(PAIRS):
                behind = (b - 1, 1 - par, hp - 1) if hp else (b - 2, par, PAIRS - 1)
                follow = att and (hp or carry)
                if att:
                    attention_scores(b - 1, 1 - par, hp)
                if lin:
                    linear(b, par, 2 * hp)
                if out and hp < TT - 1:
                    project(hp, range(0, 2))
                if follow:
                    probability_transposes(*behind)
                if out and hp < TT - 1:
                    project(hp, range(2, 4))
                if lin:
                    linear(b, par, 2 * hp + 1, range(0, 2))
                if follow:
                    values(*behind)
                if lin:
                    linear(b, par, 2 * hp + 1, range(2, 4))
                if nxt:
                    context_transposes(b + 1, 1 - par, hp)
                if release and hp == 2:
                    pe.wait_ge(lin_done, 8 * b + 4)
                    pe.sem_inc(m.unit_done, 4)

        pe.wait_ge(lat_out, 3 * KC)
        step(0, 0, att=False)
        step(1, 1, carry=False)
        with pe.Fori(1, B // 2 - 1) as i:
            step(2 * i, 0)
            step(2 * i + 1, 1)
        step(B - 2, 0)
        step(B - 1, 1, nxt=False, release=True)
        pe.wait_ge(lin_done, 8 * B)
        pe.sem_inc(m.unit_done, 4)
        step(B, 0, lin=False, nxt=False, out=True)
        probability_transposes(B - 1, 1, PAIRS - 1)
        values(B - 1, 1, PAIRS - 1)

        project(TT - 1, range(KC))

    def scalar(act):
        load = lambda out, src: act.dma_start(out, src).then_inc(consts, 16)
        load(cos[:, :], m.d["rope_cos"])
        load(sin[:, :], m.d["rope_sin"])
        load(gx[:, :], m.d["gamma_x"])
        load(bx[:, :], m.d["beta_x"])
        load(gl[:, :], m.d["gamma_l"])
        load(bl[:, :], m.d["beta_l"])

        act.dma_start(ctx[:, 0, :, :], m.d["ctx_rows"][0]).then_inc(ctx_loaded[0], 16)
        for n in range(2):
            act.wait_ge(norm_stats, norms + n + 1)
            guess_rstd(act, rstd).then_inc(norm_guess, 1)
        act.wait_ge(consts, loaded + 6 * 16)
        for c in range(KC):
            act.wait_ge(xt_done, c + 1)
            if c >= 2:
                act.wait_ge(x_split, c - 1)
            act.activation(y[:, c % 2, :], ps[:, XT, :], ACT.Identity, scale=gl[:, c:c + 1], bias=bl[:, c:c + 1])\
               .then_inc(y_ready, 1)

        def guess(b):
            act.wait_ge(norm_stats, norms + 2 + b + 1)
            guess_rstd(act, rstd).then_inc(norm_guess, 1)

        guess(0)
        act.wait_ge(xt_done, KC)
        act.dma_start(ctx[:, 1, :, :], m.d["ctx_rows"][1]).then_inc(ctx_loaded[1], 16)

        def context_chunk(b, c):
            act.wait_ge(xt_done, KC * (b + 1) + c + 1)
            act.wait_ge(x_split, KC * (b + 1) + c - 1)
            act.activation(y[:, c % 2, :], ps[:, XT, :], ACT.Identity, scale=gx[:, c:c + 1], bias=bx[:, c:c + 1])\
               .then_inc(y_ready, 1)

        for n in range(KC):
            act.wait_ge(m.unit_done, first_unit + n + 1)
            act.activation(q[:, n, :, :].rearrange("p b l -> p (b l)"), ps[:, LIN + n, :], ACT.Copy, scale=SCALE)\
               .then_inc(lat_out, 1)
        context_chunk(0, 0)
        context_chunk(0, 1)
        for n in range(KC):
            act.wait_ge(lat_done, n + 1)
            act.copy(kt[:, n, :], ps[:, LIN + n, :]).then_inc(lat_out, 1)
        context_chunk(0, 2)
        context_chunk(0, 3)
        for t in range(TT):
            act.wait_ge(lat_done, KC + t + 1)
            act.copy(vl[:, t * D:(t + 1) * D], ps[:, LIN + t, :]).then_inc(lat_out, 1)

        def stage(b, par):
            if isinstance(b, int) and b == 0:
                act.wait_ge(q_zero, 1)
                act.wait_ge(lat_out, 3 * KC)
                act.wait_ge(kl_merged, 8 * 16)
            for e in range(2):
                rows = slice(64 * e, 64 * e + 64)
                act.copy(q_pairs[rows, par, :, e, :], q[rows, :, bass.ds(b, 1), :].rearrange("p c o l -> p c (o l)"))
            act.copy(kl_batch[:, par, :, :], kl[:, :, bass.ds(b, 1), :].rearrange("p c o l -> p c (o l)"))\
               .then_inc(staged, 1)

        def stage_values(b, par):
            act.copy(vl_batch[of_batch(par), :], vl[of_batch(par), bass.ds((b - par) * (D // 2), D)]).then_inc(values_staged, 1)

        def value_tile(b, par, t):
            act.wait_ge(lin_done, 8 * b + 5 + t)
            act.copy(v[:, par, t, :], ps[:, LB[4 + t], :]).then_inc(v_ready, 1)

        def exponentials(b, hp):
            act.wait_ge(nmax_ready, 4 * b + hp + 1)
            act.activation(p[:, hp % 2, :], sc_all, ACT.Exp, bias=nmax[:, hp % 2:hp % 2 + 1],
                           accum_out=rsum[:, hp % 2:hp % 2 + 1]).then_inc(exp_done, 1)

        def transposed(b, par, hp):
            act.wait_ge(pt_done, 4 * b + hp + 1)
            if not (first(b, 0) and hp == 0):
                act.wait_ge(pv_done, 4 * b + hp)
            act.copy(pt[:, 0:TT, :].rearrange("p t n -> p (t n)"), ps[:, PTB, :])
            act.copy(pt[of_batch(par), TT, :], pt5(par)).then_inc(pt_ready, 1)

        def output(b, hp):
            act.wait_ge(pv_done, 4 * b + hp + 1)
            for e in range(2):
                rows = slice(64 * e, 64 * e + 64)
                last = act.copy(o[rows, hp, bass.ds(b * L, L)], pv[rows, 64 * e:64 * e + 64])
            last.then_inc(o_ready, 1)

        def output_high(t):
            act.copy(oh[:, :, t * P:(t + 1) * P], o[:, :, t * P:(t + 1) * P]).then_inc(o_high, 1)

        def step(b, par, lin=True, att=True, rows=True, nxt=True, carry=True, out=False):
            for hp in range(PAIRS):
                behind = (b - 1, 1 - par, hp - 1) if hp else (b - 2, par, PAIRS - 1)
                follow = att and (hp or carry)
                if out and hp < TT - 1:
                    output_high(hp)
                if follow:
                    transposed(*behind)
                if att:
                    exponentials(b - 1, hp)
                if lin and hp >= 2:
                    value_tile(b, par, 2 * hp - 4)
                if follow:
                    output(behind[0], behind[2])
                if att and hp == 0:
                    stage_values(b - 1, 1 - par)
                if lin and hp == 0:
                    stage(b, par)
                if rows and hp == 2:
                    guess(b + 2)
                if lin and hp >= 2:
                    value_tile(b, par, 2 * hp - 3)
                if nxt:
                    context_chunk(b + 1, hp)
        guess(1)
        step(0, 0, att=False)
        step(1, 1, carry=False)
        with act.Fori(1, B // 2 - 1) as i:
            step(2 * i, 0)
            step(2 * i + 1, 1)
        step(B - 2, 0, rows=False)
        step(B - 1, 1, rows=False, nxt=False)
        step(B, 0, lin=False, rows=False, nxt=False, out=True)
        transposed(B - 1, 1, PAIRS - 1)
        output(B - 1, PAIRS - 1)
        act.wait_ge(o_ready, 4 * B)
        output_high(TT - 1)

    def vector(dve):
        steps = m.dve_steps
        dve.memset(q_pairs[:, :, :, :, :].rearrange("p s c e l -> p (s c e l)"), 0.0).then_inc(q_zero, 1)
        dve.wait_ge(x_loaded, 16)
        for n in range(2):
            rows = ctx[:, 1] if n else x
            row_stats(dve, steps, rows, stats, mv, ve[:, :], rstd).then_inc(norm_stats, 1)
            dve.wait_ge(norm_guess, norms + n + 1)
            refine_rstd(dve, steps, ve[:, :], rstd[:, :], tmp[:, :])
            last = normalize_rows(dve, ctx[:, 1], rows, mv, rstd)
            if n:
                last.then_inc(lat_rows, 1)
            else:
                steps.done(last)

        def split(n, slot, c):
            dve.wait_ge(y_ready, n + 1)
            steps.done(dve.tensor_copy(xh[:, slot, c, :], y[:, c % 2, :]))
            dve.tensor_tensor(xl[:, slot, c, :], y[:, c % 2, :], f32(xh[:, slot, c, :]), ALU.subtract)\
               .then_inc(x_split, 1)

        def context_stats(b, par):
            dve.wait_ge(ctx_loaded[par], 8 * (b - par) + 16)
            row_stats(dve, steps, ctx[:, par], stats, mv, ve[:, :], rstd).then_inc(norm_stats, 1)

        def normalize_context(b, par):
            dve.wait_ge(norm_guess, norms + 2 + b + 1)
            refine_rstd(dve, steps, ve[:, :], rstd[:, :], tmp[:, :])
            normalize_rows(dve, ctx[:, par], ctx[:, par], mv, rstd).then_inc(rows_ready, 1)

        def rotate(b, par, cc):
            dve.wait_ge(lin_done, 8 * b + 2 * cc + 2)
            if first(b, 0):
                dve.wait_ge(kl_merged, 8 * 16)
            elif cc == 0:
                dve.wait_ge(merged[1 - par], 64 * (b + par))
            if cc or not first(b, 0):
                dve.wait_ge(rotated, 2 * b + cc)
            k1, k2 = ps[:, LB[2 * cc], :], ps[:, LB[2 * cc + 1], :]
            steps.mark(dve.tensor_tensor(kt[:, cc, :], k1, cos[:, :], ALU.mult))
            steps.mark(dve.tensor_tensor(by_sin[:, 0, :], k2, sin[:, :], ALU.mult))
            steps.mark(dve.tensor_tensor(kt[:, cc + 2, :], k2, cos[:, :], ALU.mult))
            steps.mark(dve.tensor_tensor(by_sin[:, 1, :], k1, sin[:, :], ALU.mult))
            steps.wait()
            steps.mark(dve.tensor_tensor(kt[:, cc, :], kt[:, cc, :], by_sin[:, 0, :], ALU.subtract))
            dve.tensor_tensor(kt[:, cc + 2, :], kt[:, cc + 2, :], by_sin[:, 1, :], ALU.add)\
               .then_inc(rotated, 1)

        def softmax(b, hp):
            slot = slice(hp % 2, hp % 2 + 1)
            dve.wait_ge(scores, 4 * b + hp + 1)
            dve.tensor_reduce(nmax[:, slot], sc_all, AX.X, ALU.max, negate=True).then_inc(nmax_ready, 1)
            dve.wait_ge(exp_done, 4 * b + hp + 1)
            steps.done(dve.reciprocal(rinv[:, slot], rsum[:, slot]))
            dve.tensor_scalar(p[:, hp % 2, :], p[:, hp % 2, :], rinv[:, slot], None, ALU.mult).then_inc(p_ready, 1)

        def output_low(t):
            dve.wait_ge(o_high, halves + t + 1)
            tile = (slice(None), slice(None), slice(t * P, (t + 1) * P))
            dve.tensor_tensor(ol[tile], o[tile], f32(oh[tile]), ALU.subtract).then_inc(o_split, 1)

        def add_output(t):
            if t < TT - 1:
                dve.wait_ge(out_done, outs + t + 1)
            else:
                dve.wait_ge(m.unit_done, first_unit + 16)
            tile_added(dve, m, k, t, dve.tensor_tensor(x[:, t, :], x[:, t, :], ps[:, OUT[t], :], ALU.add))

        def step(b, par, lin=True, att=True, rows=True, nxt=True, out=False):
            for hp in range(PAIRS):
                if out and hp < TT - 1:
                    output_low(hp)
                if att:
                    softmax(b - 1, hp)
                if out and hp:
                    add_output(hp - 1)
                if rows and hp == 2:
                    context_stats(b + 2, par)
                if rows and hp == 3:
                    normalize_context(b + 2, par)
                if lin and hp < 2:
                    rotate(b, par, hp)
                if nxt:
                    split(KC * (b + 2) + hp, 1 - par, hp)

        for c in range(KC):
            split(c, 1, c)
        context_stats(0, 0)
        normalize_context(0, 0)
        dve.wait_ge(consts, loaded + 6 * 16)
        for c in range(KC):
            split(KC + c, 0, c)
        context_stats(1, 1)
        normalize_context(1, 1)
        step(0, 0, att=False)
        step(1, 1)
        with dve.Fori(1, B // 2 - 1) as i:
            steps.enter(i - 1, 66)
            step(2 * i, 0)
            step(2 * i + 1, 1)
            steps.leave(B // 2 - 2)
        step(B - 2, 0, rows=False)
        step(B - 1, 1, rows=False, nxt=False)
        step(B, 0, lin=False, rows=False, nxt=False, out=True)
        output_low(TT - 1)
        add_output(TT - 1)

    def loads(sp):
        def load_context(b, par):
            sp.wait_ge(xt_done, KC * b)
            sp.dma_start(ctx[:, par, :, :], m.d["ctx_rows"][bass.ds(b, 1)].rearrange("o p t n -> (o p) t n"))\
              .then_inc(ctx_loaded[par], 16)

        def merge(out, keys, done):
            for j in range(4):
                for half in range(2):
                    at = 64 * (j % 2) + 32 * half
                    sp.dma_start(out[at:at + 32].rearrange("p (c r) n -> p c r n", r=2)[:, :, j // 2, :],
                                 keys[32 * j:32 * j + 32, 2 * half:2 * half + 2, :]).then_inc(done, 16)

        def merge_keys(b, par):
            sp.wait_ge(rotated, 2 * b + 2)
            merge(kt_pairs[:, par], kt, merged[par])

        sp.wait_ge(lat_out, 2 * KC)
        merge(kl[:, :, :, :].rearrange("p c b l -> p c (b l)"), kt, kl_merged)
        for b in range(2):
            load_context(b + 2, b)
            merge_keys(b, b)
        with sp.Fori(2, B // 2) as i:
            for par in range(2):
                load_context(2 * i + par, par)
                merge_keys(2 * i + (par - 2), par)
        for b in range(B - 2, B):
            merge_keys(b, b % 2)

    return tensor, scalar, vector, loads


def oscillator(nc, m, first_unit, k):
    G, DI = 8, 1024
    NM = DI // P
    CONV = 4
    with ExitStack() as mem:
        sb = lambda name, shape, dt=F32: mem.enter_context(nc.sbuf_tensor("os_" + name, shape, dt))
        vh, vl = sb("vh", [P, NM, T], F32R), sb("vl", [P, NM, T], F32R)
        qs = sb("qs", [P, 2, 2, G, B, L + 1])
        aw = sb("aw", [P, 2, G, B, L])
        small = sb("small", [P, 76])
        scan = sb("scan", [P, 6 * G * B])
        with ExitStack() as early:
            sbe = lambda name, shape, dt=F32: early.enter_context(nc.sbuf_tensor("os_" + name, shape, dt))
            xh, xl = sbe("xh", [P, KC, T], F32R), sbe("xl", [P, KC, T], F32R)
            with ExitStack() as first:
                wph, wpl = (first.enter_context(nc.sbuf_tensor("os_" + n, [P, KC, P], F32R)) for n in ("wph", "wpl"))
            gate_out = sbe("gate_out", [P, 2, T])
        bc = sb("bc", [P, 4, T])
        sq = sb("sq", [P, 2, T])
        gt = sb("gt", [P, 2, 4, P])
        ur = sb("ur", [P, TT, P])
        vg = sb("vg", [P, T])
        pick = sb("pick", [P, 32])
    u3 = scan[:, :].rearrange("p (u r n) -> p u r n", u=3, r=2)
    mask, spread = scan[:, 0:P], scan[:, P:2 * P]
    norm = sq[:, 1, :]
    early_at = qs[:, :, :, :, :, :].rearrange("p r c g b t -> p (r c g b t)")
    take = lambda n, at: early_at[:, at * 512:(at + n) * 512]
    rows = take(4, 0).rearrange("p (t n) -> p t n", t=TT)
    conv_y, silu_y = take(2, 4).rearrange("p (s n) -> p s n", s=2), take(2, 6).rearrange("p (s n) -> p s n", s=2)
    select = take(4, 8).rearrange("p (g n) -> p g n", g=2 * G)
    compact, e_u, e_w, e_d, e_l = (take(1, 12 + n) for n in range(5))
    dt_rows = take(2, 17).rearrange("p (s n) -> p s n", s=2)
    wp_raw = take(1, 19).rearrange("p (c n) -> p c n", c=KC)
    slot = lambda n: aw[:, 0, n, :, :].rearrange("p b t -> p (b t)")
    g0, g1, e0, e1, v1, v2, ta, tb = (slot(n) for n in range(8))
    conv_w, conv_b, skip = small[:, 0:32].rearrange("p (m j) -> p m j", j=CONV), small[:, 32:40], small[:, 40:48]
    a_log, root_a, inv_root = small[:, 48:56], small[:, 56:64], small[:, 64:72]
    dt_bias = small[:, 72:73]
    gates = nc.dram_tensor("os_gates", (P, NM, T), F32, kind="Internal").ap()
    released = m.shared("out_split", 0)
    s = lambda name: m.sem("os_" + name)
    consts, loaded = m.shared("stage_consts", 7 * 16)
    ln = NormalizedColumns(m, k, rows, xh, xl, (1, 2, 3, 4))
    late_consts, wp_split, roots = s("late_consts"), s("wp_split"), s("roots")
    par_done, e_ready, w_ready, l_ready, k_ready, compact_ready = (
        s(n) for n in ("par_done", "e_ready", "w_ready", "l_ready", "k_ready", "compact_ready"))
    tap, conv_done, silu_done, v_high, v_split = (s(n) for n in ("tap", "conv_done", "silu_done", "v_high", "v_split"))
    sel_done, dt_copied, w_made, aw_ready = s("sel_done"), s("dt_copied"), s("w_made"), s("aw_ready")
    gate_silu, gate_stored = s("gate_silu"), [s("gate_stored0"), s("gate_stored1")]
    squared, sums_done, rooted, bc_ready = s("squared"), s("sums_done"), s("rooted"), s("bc_ready")
    spread_copied = s("spread_copied")
    norm_ready, spread_done, scanned, scan_consts = s("norm_ready"), s("spread_done"), s("scanned"), s("scan_consts")
    vg_ready, ur_done, ur_ready = s("vg_ready"), s("ur_done"), s("ur_ready")
    w_used, gate_loaded = s("w_used"), s("gate_loaded")
    ge_ready, head_done, gt_ready, y_done, y_ready = (s(n) for n in ("ge_ready", "head_done", "gt_ready", "y_done", "y_ready"))
    (y_high, halves), (y_split, _) = m.shared("out_high", 8), m.shared("out_split", 8)
    out_done, outs = m.shared("out_done", TT - 1)
    LIN, PAR, SUM, GB, YB = 1, 5, 5, (0, 7), 6
    SEL, SEL_K = (6, 0), (7, 5)
    NB = (5, 0, 7, 5)
    ps = m.ps
    value_unit, gate_unit, bc_unit, out_unit = first_unit, first_unit + 8, first_unit + 16, first_unit + 80

    def pair_of(h, n, c):
        return h[:, n % RING_UNITS, c * P:(c + 1) * P]

    def tensor(pe):
        ln.tensor(pe)
        ln.wait_split(pe, KC)
        pe.wait_ge(wp_split, 1)
        for c in range(KC):
            last = product(pe, ps[:, PAR, :], (wph[:, c, :], wpl[:, c, :]), (xh[:, c, :], xl[:, c, :]), c == 0, c == KC - 1)
        last.then_inc(par_done, 1)

        def columns(n, bank, unit):
            pe.wait_ge(m.unit_ready, unit + 1)
            for c in range(KC):
                last = product(pe, ps[:, bank, :], (pair_of(m.wh, unit, c), pair_of(m.wl, unit, c)),
                               (xh[:, c, :], xl[:, c, :]), c == 0, c == KC - 1)
            last.then_inc(m.unit_done, 1)

        for n in range(NM):
            if n >= 4:
                pe.wait_ge(conv_done, n - 3)
            columns(n, LIN + n % 4, value_unit + n)
        pe.wait_ge(compact_ready, 1)
        for g in range(G):
            if g >= 2:
                pe.wait_ge(aw_ready, g - 1)
                pe.wait_ge(w_made, g - 1)
            pe.matmul(ps[:, SEL[g % 2], :], select[:, g, :], compact, start=True, stop=True)
            pe.matmul(ps[:, SEL_K[g % 2], :], select[:, G + g, :], compact, start=True, stop=True).then_inc(sel_done, 1)
        for n in range(NM):
            pe.wait_ge(conv_done, NM)
            if n >= 4:
                pe.wait_ge(gate_silu, n - 3)
            columns(n, LIN + n % 4, gate_unit + n)

        def bc_products(g, j):
            if isinstance(g, int) and g == 0:
                pe.wait_ge(v_split, NM)
                pe.wait_ge(gate_silu, 5 + j)
            else:
                pe.wait_ge(bc_ready, 4 * g + (j - 3))
            for half in range(2):
                at = 2 * j + half
                pe.wait_ge(m.unit_ready, bc_unit + 8 * g + (at + 1))
                for c in range(KC):
                    cc = KC * half + c
                    last = product(pe, ps[:, LIN + j, :], (pair_of(m.wh, bc_unit + at, c), pair_of(m.wl, bc_unit + at, c)),
                                   (vh[:, cc, :], vl[:, cc, :]), cc == 0, cc == NM - 1)
                last.then_inc(m.unit_done, 1)

        def sums(g, j):
            if isinstance(g, int) and g == 0:
                pe.wait_ge(late_consts, 16)
            elif j == 0:
                pe.wait_ge(spread_copied, 4 * g)
            pe.wait_ge(squared, 4 * g + j + 1)
            pe.matmul(ps[32 * j:32 * j + 32, SUM, :], pick[:, :], sq[:, j % 2, :], start=True, stop=True).then_inc(sums_done, 1)

        def spread_norms(g):
            pe.wait_ge(norm_ready, g + 1)
            if isinstance(g, int) and g == 0:
                pe.wait_ge(scan_consts, 2 * 16)
            for j in range(4):
                if j == 1 and not (isinstance(g, int) and g == 0):
                    pe.wait_ge(gt_ready, 4 * g)
                part = slice(32 * j, 32 * j + 32)
                if j == 3:
                    pe.wait_ge(spread_copied, 4 * g + 1)
                pe.matmul(ps[:, NB[j], :], spread[part, :], norm[part, :], start=True, stop=True).then_inc(spread_done, 1)

        def turn_values(g):
            pe.wait_ge(vg_ready, g + 1)
            if not (isinstance(g, int) and g == 0):
                pe.wait_ge(y_ready, g)
            for t in range(TT):
                last = pe.transpose(ps[:, YB, t * P:(t + 1) * P], vg[:, t * P:(t + 1) * P], m.ident[:, :])
            last.then_inc(ur_done, 1)

        def outputs(g):
            pe.wait_ge(ge_ready, g + 1)
            for half in range(2):
                pe.wait_ge(gt_ready, 4 * g + 2 * half)
                for h in range(4):
                    if h >= 2:
                        pe.wait_ge(head_done, 8 * g + 4 * half + h - 1)
                    hr = slice(32 * h, 32 * h + 32)
                    for q in range(2):
                        cols = slice((2 * half + q) * P, (2 * half + q + 1) * P)
                        at = ((h // 2) * 2 + q) * P
                        out = ps[:, GB[h % 2], at:at + P]
                        pe.matmul(out, g0[hr, cols], e0[hr, cols], start=True, stop=False)
                        last = pe.matmul(out, g1[hr, cols], e1[hr, cols], start=False, stop=True)
                    last.then_inc(head_done, 1)
                pe.wait_ge(ur_ready, g + 1)
                for h in range(4):
                    if h < 2:
                        pe.wait_ge(gt_ready, 4 * g + 2 * half + h + 1)
                    for q in range(2):
                        pr = 2 * half + q
                        last = pe.matmul(ps[32 * h:32 * h + 32, YB, pr * P:(pr + 1) * P], ur[:, pr, 32 * h:32 * h + 32],
                                         gt[:, h % 2, (h // 2) * 2 + q, :], start=True, stop=True)
                last.then_inc(y_done, 1)

        def project(chunks):
            for cc in chunks:
                u = out_unit + cc
                pe.wait_ge(m.unit_ready, u + 1)
                pe.wait_ge(y_split, halves + cc + 1)
                for t in range(TT):
                    last = product(pe, ps[:, LIN + t, :], (vh[:, cc, t * P:(t + 1) * P], vl[:, cc, t * P:(t + 1) * P]),
                                   (m.wh[:, u % RING_UNITS, :], m.wl[:, u % RING_UNITS, :]), cc == 0, cc == NM - 1)
                    if cc == NM - 1 and t < TT - 1:
                        last.then_inc(out_done, 1)
                last.then_inc(m.unit_done, 1)

        def group(g, products=True, out=True):
            if products:
                for j in range(4):
                    bc_products(g, j)
                    if j:
                        sums(g, j - 1)
            if out:
                turn_values(g - 1)
            if products:
                sums(g, 3)
            if out:
                outputs(g - 1)
            if products:
                spread_norms(g)

        pe.wait_ge(aw_ready, G)
        pe.wait_ge(w_made, G)
        group(0, out=False)
        with pe.Fori(1, G) as g:
            group(g)
        project(range(0, NM - 1))
        group(G, products=False)
        project(range(NM - 1, NM))

    def scalar(act):
        if k:
            act.wait_ge(*released)
        for out, src in ((conv_w, m.d["conv_w"]), (conv_b, m.d["conv_b"]), (skip, m.d["skip"]), (a_log, m.d["a_log"]),
                         (dt_bias[0:32, :], m.d["dt_bias"]), (select, m.d["select"]), (wp_raw, m.d["w_params"])):
            act.dma_start(out, src).then_inc(consts, 16)
        ln.scalar_guess(act)
        act.wait_ge(consts, loaded + 7 * 16)
        act.activation(root_a, a_log, ACT.Exp, scale=0.5).then_inc(roots, 1)
        act.activation(inv_root, a_log, ACT.Exp, scale=-0.5).then_inc(roots, 1)
        ln.scalar_high(act)
        act.wait_ge(par_done, 1)
        act.activation(e_u[0:32, :], ps[0:32, PAR, :], ACT.Exp, bias=dt_bias[0:32, :]).then_inc(e_ready, 1)
        act.wait_ge(w_ready, 1)
        act.activation(e_l[0:32, :], e_w[0:32, :], ACT.Ln).then_inc(l_ready, 1)
        act.activation(e_l[32:64, :], ps[32:64, PAR, :], ACT.Sigmoid).then_inc(k_ready, 1)

        def first_tap(n):
            act.wait_ge(m.unit_done, value_unit + n + 1)
            if n >= 2:
                act.wait_ge(silu_done, n - 1)
            act.activation(conv_y[:, n % 2, :], ps[:, LIN + n % 4, :], ACT.Identity, scale=conv_w[:, n, 3:4],
                           bias=conv_b[:, n:n + 1]).then_inc(tap, 1)

        for n in range(NM + 1):
            if n < NM:
                first_tap(n)
            if n:
                act.wait_ge(conv_done, n)
                if n >= 3:
                    act.wait_ge(v_split, n - 2)
                act.activation(silu_y[:, (n - 1) % 2, :], conv_y[:, (n - 1) % 2, :], ACT.Silu).then_inc(silu_done, 1)
                act.wait_ge(silu_done, n)
                act.copy(vh[:, n - 1, :], silu_y[:, (n - 1) % 2, :]).then_inc(v_high, 1)
        act.wait_ge(roots, 2)
        for g in range(G):
            act.wait_ge(sel_done, g + 1)
            if g >= 2:
                act.wait_ge(aw_ready, g - 1)
            act.copy(dt_rows[:, g % 2, :], ps[:, SEL[g % 2], :]).then_inc(dt_copied, 1)
            act.activation(aw[:, 1, g, :, :].rearrange("p b t -> p (b t)"), ps[:, SEL[g % 2], :], ACT.Copy,
                           scale=root_a[:, g:g + 1]).then_inc(w_made, 1)
        for n in range(NM):
            act.wait_ge(m.unit_done, gate_unit + n + 1)
            if n >= 2:
                act.wait_ge(gate_stored[n % 2], 16 * (n // 2))
            act.activation(gate_out[:, n % 2, :], ps[:, LIN + n % 4, :], ACT.Silu).then_inc(gate_silu, 1)
            act.wait_ge(gate_silu, n + 1)
            act.dma_start(gates[:, n, :], gate_out[:, n % 2, :]).then_inc(gate_stored[n % 2], 16)
        act.dma_start(pick[:, :], m.d["pick"]).then_inc(late_consts, 16)
        for n in range(2):
            act.wait_ge(gate_stored[n], 16 * NM // 2)

        def squares(g, j):
            act.wait_ge(m.unit_done, bc_unit + 8 * g + (2 * j + 2))
            if not (isinstance(g, int) and g == 0 and j < 2):
                act.wait_ge(sums_done, 4 * g + (j - 1))
            if j == 1 and not (isinstance(g, int) and g == 0):
                act.wait_ge(spread_done, 4 * g)
            act.activation(sq[:, j % 2, :], ps[:, LIN + j, :], ACT.Square).then_inc(squared, 1)

        def value_rows(g):
            act.wait_ge(w_used, g + 1)
            act.dma_start(aw[:, 1, bass.ds(g, 1), :, :].rearrange("p o b t -> p (o b t)"),
                          gates[:, bass.ds(g, 1), :].rearrange("p o n -> p (o n)")).then_inc(gate_loaded, 16)
            act.wait_ge(ur_done, g + 1)
            act.copy(ur[:, :, :].rearrange("p t n -> p (t n)"), ps[:, YB, :]).then_inc(ur_ready, 1)

        def group(g, products=True, out=True):
            if products:
                for j in range(4):
                    squares(g, j)
            if out:
                value_rows(g - 1)
            if products:
                if isinstance(g, int) and g == 0:
                    act.wait_ge(scanned, 1)
                    act.dma_start(mask, m.d["causal"]).then_inc(scan_consts, 16)
                    act.dma_start(spread, m.d["spread"]).then_inc(scan_consts, 16)
                act.wait_ge(sums_done, 4 * g + 4)
                act.activation(norm[:, :], ps[:, SUM, :], ACT.Sqrt).then_inc(rooted, 1)
                for j in range(4):
                    act.wait_ge(spread_done, 4 * g + j + 1)
                    if j == 0 and not (isinstance(g, int) and g == 0):
                        act.wait_ge(ge_ready, g)
                    act.copy(bc[:, j, :], ps[:, NB[j], :]).then_inc(spread_copied, 1)

        group(0, out=False)
        with act.Fori(1, G) as g:
            group(g)

        def output_high(cc):
            act.wait_ge(y_ready, cc + 1)
            act.copy(vh[:, cc, :], qs[:, 0, 0, cc, :, 1:L + 1].rearrange("p b t -> p b t")).then_inc(y_high, 1)

        for cc in range(NM - 1):
            output_high(cc)
        group(G, products=False)
        output_high(NM - 1)

    def vector(dve):
        steps = m.dve_steps
        if k:
            dve.wait_ge(m.x_ready, TT * k)
        ln.vector_rows(dve, steps)
        dve.wait_ge(consts, loaded + 7 * 16)
        steps.done(dve.tensor_copy(wph[:, :, :], wp_raw))
        dve.tensor_tensor(wpl[:, :, :], wp_raw, f32(wph[:, :, :]), ALU.subtract).then_inc(wp_split, 1)
        steps.done(dve.memset(compact, 0.0))
        ln.vector_low(dve)
        dve.wait_ge(e_ready, 1)
        d32 = slice(0, 32)
        steps.done(dve.tensor_scalar(e_u[d32, :], e_u[d32, :], 1e4, None, ALU.min))
        steps.done(dve.tensor_scalar(e_w[d32, :], e_u[d32, :], 1.0, None, ALU.add))
        dve.tensor_scalar(e_d[d32, :], e_w[d32, :], -1.0, 1e-30, ALU.add, ALU.max).then_inc(w_ready, 1)
        dve.wait_ge(w_ready, 1)
        steps.done(dve.reciprocal(e_d[d32, :], e_d[d32, :]))
        steps.done(dve.tensor_tensor(e_u[d32, :], e_u[d32, :], e_d[d32, :], ALU.mult))
        dve.wait_ge(l_ready, 1)
        steps.done(dve.tensor_tensor(e_u[d32, :], e_u[d32, :], e_l[d32, :], ALU.mult))
        steps.mark(dve.tensor_scalar(compact[d32, :], e_u[d32, :], 1e-4, 0.1, ALU.max, ALU.min))
        dve.wait_ge(k_ready, 1)
        dve.tensor_scalar(compact[32:64, :], e_l[32:64, :], 0.5, None, ALU.mult).then_inc(compact_ready, 1)

        by_batch = lambda ap: ap.rearrange("p (b t) -> p b t", b=B)

        def convolve(n):
            dve.wait_ge(tap, n + 1)
            y, v = by_batch(conv_y[:, n % 2, :]), by_batch(ps[:, LIN + n % 4, :])
            for j in range(1, CONV):
                ins = dve.scalar_tensor_tensor(y[:, :, j:], v[:, :, 0:L - j], conv_w[:, n, 3 - j:4 - j], y[:, :, j:],
                                               ALU.mult, ALU.add)
                if j < CONV - 1:
                    steps.done(ins)
            ins.then_inc(conv_done, 1)

        def split_value(n):
            dve.wait_ge(v_high, n + 1)
            dve.tensor_tensor(vl[:, n, :], silu_y[:, n % 2, :], f32(vh[:, n, :]), ALU.subtract).then_inc(v_split, 1)

        for n in range(NM + 1):
            if n < NM:
                convolve(n)
            if n:
                split_value(n - 1)
        dve.wait_ge(roots, 2)
        for g in range(G):
            a_g = aw[:, 0, g, :, :].rearrange("p b t -> p (b t)")
            dve.wait_ge(dt_copied, g + 1)
            steps.done(dve.tensor_tensor(a_g, dt_rows[:, g % 2, :], ps[:, SEL_K[g % 2], :], ALU.mult))
            dve.tensor_scalar(a_g, a_g, 1.0, None, ALU.add).then_inc(aw_ready, 1)
        dve.wait_ge(aw_ready, G)
        dve.wait_ge(w_made, G)

        qt = qs[:, :, :, :, :, :].rearrange("p r c g b t -> p r c (g b) t")
        at = aw[:, :, :, :, :].rearrange("p c g b t -> p c (g b) t")
        for r in range(2):
            for c in range(2):
                steps.mark(dve.memset(qt[:, r, c, :, 0], 1.0 if r == c else 0.0))
        steps.wait()
        col = lambda ap: ap.rearrange("p r n o -> p r (n o)")
        UNROLL = 8
        with dve.Fori(0, L // UNROLL) as i:
            steps.enter(i, 4 * UNROLL)
            for n in range(UNROLL):
                t = i * UNROLL + n
                q_a, q_c = (col(qt[:, :, c, :, bass.ds(t, 1)]) for c in range(2))
                n_a, n_c = (col(qt[:, :, c, :, bass.ds(t + 1, 1)]) for c in range(2))
                a_w = col(at[:, :, :, bass.ds(t, 1)])
                steps.mark(dve.tensor_tensor(u3[:, 0:2, :, :], a_w.unsqueeze(2).to_broadcast([P, 2, 2, G * B]),
                                             q_a.unsqueeze(1).to_broadcast([P, 2, 2, G * B]), ALU.mult))
                steps.mark(dve.tensor_tensor(u3[:, 2, :, :], a_w[:, 1:2, :].to_broadcast([P, 2, G * B]), q_c, ALU.mult))
                steps.wait()
                steps.mark(dve.tensor_tensor(n_a, u3[:, 0, :, :], u3[:, 2, :, :], ALU.subtract))
                steps.mark(dve.tensor_tensor(n_c, u3[:, 1, :, :], q_c, ALU.add))
                steps.wait()
            steps.leave(L // UNROLL)

        def invert_norms(g):
            dve.wait_ge(rooted, g + 1)
            steps.done(dve.tensor_scalar(norm[:, :], norm[:, :], 1e-8, None, ALU.add))
            dve.reciprocal(norm[:, :], norm[:, :]).then_inc(norm_ready, 1)

        def normalize(g, j):
            dve.wait_ge(spread_copied, 4 * g + j + 1)
            dve.tensor_tensor(bc[:, j, :], ps[:, LIN + j, :], bc[:, j, :], ALU.mult).then_inc(bc_ready, 1)

        def inputs_and_outputs(g):
            at_g = lambda r, c, d: qs[:, r, c, bass.ds(g, 1), :, d:d + L].rearrange("p o b t -> p (o b) t")
            w_g = aw[:, 1, bass.ds(g, 1), :, :].rearrange("p o b t -> p (o b t)")
            ir = inv_root[:, bass.ds(g, 1)]
            mul = lambda out, x, y: steps.mark(dve.tensor_tensor(out, x, y, ALU.mult))
            sub = lambda out, x, y: steps.mark(dve.tensor_tensor(out, x, y, ALU.subtract))
            dve.wait_ge(bc_ready, 4 * g + 4)
            if not (isinstance(g, int) and g == 0):
                dve.wait_ge(y_done, 2 * g)
            dve.tensor_tensor(vg[:, :], f32(vh[:, bass.ds(g, 1), :]).rearrange("p o n -> p (o n)"),
                              f32(vl[:, bass.ds(g, 1), :]).rearrange("p o n -> p (o n)"), ALU.add).then_inc(vg_ready, 1)
            mul(v2, w_g, bc[:, 1, :])
            steps.wait()
            steps.done(dve.scalar_tensor_tensor(v1, bc[:, 0, :], ir, v2, ALU.mult, ALU.add))
            dve.tensor_tensor(v1, v1, w_g, ALU.mult).then_inc(w_used, 1)
            dve.wait_ge(w_used, g + 1)
            for r, out in ((0, g0), (1, g1)):
                mul(by_batch(ta), at_g(r, 0, 0), by_batch(v1))
                mul(by_batch(tb), at_g(r, 1, 0), by_batch(v2))
                steps.wait()
                steps.done(dve.tensor_tensor(out, ta, tb, ALU.add))
            mul(by_batch(ta), at_g(0, 0, 1), at_g(1, 1, 1))
            mul(by_batch(tb), at_g(1, 0, 1), at_g(0, 1, 1))
            steps.mark(dve.tensor_scalar(bc[:, 3, :], bc[:, 3, :], ir, None, ALU.mult))
            steps.wait()
            sub(v1, ta, tb)
            steps.wait()
            steps.mark(dve.reciprocal(v1, v1))
            for (ra, ca, xa), (rb, cb, xb), out in (((1, 1, 2), (1, 0, 3), e0), ((0, 0, 3), (0, 1, 2), e1)):
                mul(by_batch(ta), at_g(ra, ca, 1), by_batch(bc[:, xa, :]))
                mul(by_batch(tb), at_g(rb, cb, 1), by_batch(bc[:, xb, :]))
                steps.wait()
                sub(ta, ta, tb)
                steps.wait()
                last = dve.tensor_tensor(out, ta, v1, ALU.mult)
                if out is e0:
                    steps.done(last)
            last.then_inc(ge_ready, 1)
            dve.wait_ge(ge_ready, g + 1)

        def gated_output(g):
            for half in range(2):
                dve.wait_ge(head_done, 8 * g + 4 * half + 4)
                if half or not (isinstance(g, int) and g == 0):
                    dve.wait_ge(y_done, 2 * g + half)
                for n in range(2):
                    dve.tensor_tensor(gt[:, n, :, :], ps[:, GB[n], :].rearrange("p (a t) -> p a t", a=4),
                                      mask.unsqueeze(1).to_broadcast([P, 4, P]), ALU.mult).then_inc(gt_ready, 1)
            dve.wait_ge(y_done, 2 * g + 2)
            dve.wait_ge(gate_loaded, 16 * (g + 1))
            steps.done(dve.scalar_tensor_tensor(ta, vg[:, :], skip[:, bass.ds(g, 1)], ps[:, YB, :], ALU.mult, ALU.add))
            dve.tensor_tensor(qs[:, 0, 0, bass.ds(g, 1), :, 1:L + 1].rearrange("p o b t -> p (o b) t"), by_batch(ta),
                              aw[:, 1, bass.ds(g, 1), :, :].rearrange("p o b t -> p (o b) t"), ALU.mult).then_inc(y_ready, 1)
            dve.wait_ge(y_ready, g + 1)

        def group(g, products=True, out=True):
            if out:
                inputs_and_outputs(g - 1)
            if products:
                invert_norms(g)
            if out:
                gated_output(g - 1)
            if products:
                for j in range(4):
                    normalize(g, j)

        dve.sem_inc(scanned, 1)
        dve.wait_ge(scan_consts, 2 * 16)
        group(0, out=False)
        with dve.Fori(1, G) as g:
            steps.enter(g - 1, 22)
            group(g)
            steps.leave(G - 1)

        def output_low(cc):
            dve.wait_ge(y_high, halves + cc + 1)
            dve.tensor_tensor(by_batch(vl[:, cc, :]), qs[:, 0, 0, cc, :, 1:L + 1], by_batch(f32(vh[:, cc, :])), ALU.subtract)\
               .then_inc(y_split, 1)

        for cc in range(NM - 1):
            output_low(cc)
        group(G, products=False)
        output_low(NM - 1)
        for t in range(TT):
            if t < TT - 1:
                dve.wait_ge(out_done, outs + t + 1)
            else:
                dve.wait_ge(m.unit_done, out_unit + NM)
            tile_added(dve, m, k, t, dve.tensor_tensor(m.x[:, t, :], m.x[:, t, :], ps[:, LIN + t, :], ALU.add))

    return tensor, scalar, vector, None


def bit_ffn(nc, m, first_unit, k):
    H = 2048
    NH = H // P
    with ExitStack() as mem:
        sb = lambda name, shape, dt=F32: mem.enter_context(nc.sbuf_tensor("bf_" + name, shape, dt))
        w1q, w2q = sb("w1q", [P, KC, H], BF16), sb("w2q", [P, NH, D], BF16)
        w1, w2 = sb("w1", [P, KC, H]), sb("w2", [P, NH, D])
        rows = sb("rows", [P, TT, D])
        rq = sb("rq", [P, TT, D], BF16)
        xq = sb("xq", [P, KC, T], BF16)
        hid = sb("hid", [P, NH // 2, T])
        top = sb("top", [P, T])
        scaled, conv_y, magnitude = (sb(n, [P, 2, T]) for n in ("scaled", "conv_y", "magnitude"))
        inv_row = sb("inv_row", [P, T])
        diag = sb("diag", [P, TT, P])
        ones, ident16 = sb("ones", [P, P]), sb("ident16", [P, P], BF16)
        small = sb("small", [P, 256])
    mv, ve, rstd, tmp = m.norm.mv, m.norm.ve, m.norm.rstd, m.norm.tmp
    row_max, row_scale, row_inv = small[:, 44:48], small[:, 48:52], small[:, 52:56]
    hid_max, hid_scale, hid_inv = small[:, 56:60], small[:, 60:64], small[:, 64:68]
    w_sums, w_sum, w_mean, w_scale = small[:, 72:104], small[:, 104:106], small[:, 106:108], small[:, 108:110]
    conv_w, conv_b = small[:, 112:160].rearrange("p (n j) -> p n j", j=3), small[:, 160:176]
    s = lambda name: m.sem("bf_" + name)
    released = m.shared("out_split", 0)
    consts, loaded = m.shared("stage_consts", 3 * 16)
    w2_loaded = s("w2_loaded")
    w_loaded = ((s("w1_low_loaded"), s("w1_high_loaded")), (w2_loaded, w2_loaded))
    summed, sum_ready, total_done, scale_ready = (s(n) for n in ("summed", "sum_ready", "total_done", "scale_ready"))
    shifted, w_ready = s("shifted"), s("w_ready")
    (ln_stats, norms), (ln_guess, _) = m.shared("norm_stats", 1), m.shared("norm_guess", 1)
    rq_ready, rows_turned, xq_ready = (s(n) for n in ("rq_ready", "rows_turned", "xq_ready"))
    diag_ready, spread_done, spread_ready = s("diag_ready"), s("spread_done"), s("spread_ready")
    h_done, scaled_ready, tap, conv_done, silu_done, mag_ready, top_ready = (
        s(n) for n in ("h_done", "scaled_ready", "tap", "conv_done", "silu_done", "mag_ready", "top_ready"))
    top_turned, diag2_ready, spread2_done, q_ready = (
        s(n) for n in ("top_turned", "diag2_ready", "spread2_done", "q_ready"))
    clipped, rounded = s("clipped"), s("rounded")
    out_done, outs = m.shared("out_done", TT)
    TURN, LIN, SPREAD, TOT = 0, 1, 5, 6
    ps = m.ps
    w1_flat = w1[:, :, :].rearrange("p c n -> p (c n)")
    w2_flat = w2[:, :, :].rearrange("p c n -> p (c n)")
    hidden = lambda n: hid[:, n, :] if n < NH // 2 else w1_flat[:, (n - NH // 2) * T:(n - NH // 2 + 1) * T]
    q2 = w2_flat.bitcast(BF16)[:, 0:NH * T].rearrange("p (n t) -> p n t", n=NH)

    def tensor(pe):
        def total(j):
            pe.wait_ge(sum_ready, j + 1)
            pe.matmul(ps[:, TOT, j:j + 1], ones[:, :], w_sum[:, j:j + 1], start=True, stop=True).then_inc(total_done, 1)

        pe.wait_ge(consts, loaded + 3 * 16)
        pe.wait_ge(m.consts, 16)
        total(0)
        turned = ps[:, TURN, :].bitcast(BF16)
        for c in range(KC):
            pe.wait_ge(rq_ready, 1)
            if c:
                pe.wait_ge(xq_ready, c)
            for t in range(TT):
                last = pe.transpose(turned[:, t * P:(t + 1) * P], rq[:, t, c * P:(c + 1) * P], ident16[:, :])
            last.then_inc(rows_turned, 1)
        pe.wait_ge(diag_ready, 1)
        for t in range(TT):
            last = pe.matmul(ps[:, SPREAD, t * P:(t + 1) * P], ones[:, :], diag[:, t, :], start=True, stop=True)
        last.then_inc(spread_done, 1)
        pe.wait_ge(xq_ready, KC)
        pe.wait_ge(w_ready, 4)
        for n in range(NH):
            if n >= 4:
                pe.wait_ge(scaled_ready, n - 3)
            for c in range(KC):
                last = pe.matmul(ps[:, LIN + n % 4, :], w1q[:, c, n * P:(n + 1) * P], xq[:, c, :], start=c == 0, stop=c == KC - 1)
            last.then_inc(h_done, 1)
            if n == 11:
                total(1)
        pe.wait_ge(top_ready, NH)
        for t in range(TT):
            last = pe.transpose(ps[:, TURN, t * P:(t + 1) * P], top[:, t * P:(t + 1) * P], m.ident[:, :])
        last.then_inc(top_turned, 1)
        pe.wait_ge(diag2_ready, 1)
        for t in range(TT):
            last = pe.matmul(ps[:, SPREAD, t * P:(t + 1) * P], ones[:, :], diag[:, t, :], start=True, stop=True)
        last.then_inc(spread2_done, 1)
        pe.wait_ge(w_ready, 8)
        for n in range(NH):
            pe.wait_ge(q_ready, n + 1)
            for t in range(TT):
                last = pe.matmul(ps[:, LIN + t, :], q2[:, n, t * P:(t + 1) * P], w2q[:, n, :], start=n == 0, stop=n == NH - 1)
                if n == NH - 1:
                    last.then_inc(out_done, 1)

    def scalar(act):
        act.wait_ge(m.x_loaded, 16)
        if k:
            act.wait_ge(*released)
        for half in range(2):
            cols = slice(half * 2 * H, (half + 1) * 2 * H)
            act.dma_start(w1_flat[:, cols], m.d["ffn_w1"][:, cols]).then_inc(w_loaded[0][half], 16)
        for out, src in ((conv_w, m.d["ffn_conv_w"]), (conv_b, m.d["ffn_conv_b"]), (ones[:, :], m.d["ones"])):
            act.dma_start(out, src).then_inc(consts, 16)
        act.dma_start(w2_flat, m.d["ffn_w2"]).then_inc(w_loaded[1][0], 16)
        x_guess(act, m, ln_stats, norms).then_inc(ln_guess, 1)

        def magnitudes(j, n):
            w, wq = ((w1_flat, w1q), (w2_flat, w2q))[j]
            act.wait_ge(w_loaded[j][n // 2], 16)
            if j or n:
                act.wait_ge(summed, 4 * j + n)
            act.activation(wq[:, :, :].rearrange("p c n -> p (c n)")[:, n * H:(n + 1) * H], w[:, n * H:(n + 1) * H],
                           ACT.Abs, accum_out=w_sums[:, 4 * j + n:4 * j + n + 1]).then_inc(summed, 1)

        def scale_weights(j, n):
            cols = slice(n * H, (n + 1) * H)
            w = (w1_flat, w2_flat)[j][:, cols]
            act.wait_ge(scale_ready, j + 1)
            act.activation(w, w, ACT.Copy, scale=w_scale[:, j:j + 1]).then_inc(shifted, 1)

        def quantize_w2(n):
            if n < 8 and n % 2:
                magnitudes(1, n // 2)
            elif 8 <= n < 16 and n % 2:
                scale_weights(1, (n - 8) // 2)

        for n in range(4):
            magnitudes(0, n)
        for c in range(KC):
            scale_weights(0, c)
            act.wait_ge(rows_turned, c + 1)
            act.copy(xq[:, c, :], ps[:, TURN, :].bitcast(BF16)[:, 0:T]).then_inc(xq_ready, 1)
        act.wait_ge(spread_done, 1)
        act.activation(inv_row[:, :], ps[:, SPREAD, :], ACT.Copy, scale=w_mean[:, 0:1]).then_inc(spread_ready, 1)
        for n in range(NH + 1):
            if n < NH:
                act.wait_ge(scaled_ready, n + 1)
                if n >= 2:
                    act.wait_ge(silu_done, n - 1)
                act.activation(conv_y[:, n % 2, :], scaled[:, n % 2, :], ACT.Identity, scale=conv_w[:, n, 1:2],
                               bias=conv_b[:, n:n + 1]).then_inc(tap, 1)
            if n:
                act.wait_ge(conv_done, n)
                act.activation(hidden(n - 1), conv_y[:, (n - 1) % 2, :], ACT.Silu).then_inc(silu_done, 1)
                act.wait_ge(silu_done, n)
                if n >= 3:
                    act.wait_ge(top_ready, n - 2)
                act.activation(magnitude[:, (n - 1) % 2, :], hidden(n - 1), ACT.Abs).then_inc(mag_ready, 1)
            quantize_w2(n)
        act.wait_ge(w_ready, 8)
        for n in range(NH):
            act.wait_ge(clipped, n + 1)
            act.activation(hidden(n), hidden(n), ACT.Copy, bias=MAGIC).then_inc(rounded, 1)
            act.wait_ge(rounded, n + 1)
            act.activation(q2[:, n, :], hidden(n), ACT.Copy, bias=-MAGIC).then_inc(q_ready, 1)

    def vector(dve):
        steps = m.dve_steps
        x_stats(dve, m, k).then_inc(ln_stats, 1)
        dve.wait_ge(m.consts, 16)
        steps.done(dve.tensor_copy(ident16[:, :], m.ident[:, :]))
        dve.wait_ge(ln_guess, norms + 1)
        refine_rstd(dve, steps, ve, rstd, tmp)
        steps.done(normalize_rows(dve, rows, m.x, mv, rstd))

        def scales(top_values, scale, inverse):
            steps.done(dve.tensor_scalar(top_values, top_values, 1e-5, None, ALU.max))
            steps.done(dve.reciprocal(scale, top_values))
            steps.done(dve.tensor_scalar(scale, scale, 127.0, None, ALU.mult))
            steps.done(dve.reciprocal(inverse, scale))

        steps.done(dve.tensor_reduce(row_max, rows[:, :, :], AX.X, ALU.max, apply_absolute_value=True))
        scales(row_max, row_scale, row_inv)
        for t in range(TT):
            steps.mark(dve.tensor_scalar(rows[:, t, :], rows[:, t, :], row_scale[:, t:t + 1], 127.0, ALU.mult, ALU.min))
        steps.wait()
        steps.done(dve.tensor_scalar(rows[:, :, :], rows[:, :, :], -128.0, MAGIC, ALU.max, ALU.add))
        dve.tensor_scalar(rq[:, :, :], rows[:, :, :], -MAGIC, None, ALU.add).then_inc(rq_ready, 1)
        for t in range(TT):
            last = dve.tensor_scalar(diag[:, t, :], m.ident[:, :], row_inv[:, t:t + 1], None, ALU.mult)
        last.then_inc(diag_ready, 1)
        def weight_scale(j):
            dve.wait_ge(summed, 4 * j + 4)
            dve.tensor_reduce(w_sum[:, j:j + 1], w_sums[:, 4 * j:4 * j + 4], AX.X, ALU.add).then_inc(sum_ready, 1)
            dve.wait_ge(total_done, j + 1)
            steps.done(dve.tensor_scalar(w_mean[:, j:j + 1], ps[:, TOT, j:j + 1], 1.0 / (H * D), 1e-5, ALU.mult, ALU.max))
            dve.reciprocal(w_scale[:, j:j + 1], w_mean[:, j:j + 1]).then_inc(scale_ready, 1)

        def round_weights(j, n):
            w, wq = ((w1_flat, w1q), (w2_flat, w2q))[j]
            cols = slice(n * H, (n + 1) * H)
            dve.wait_ge(shifted, 4 * j + n + 1)
            steps.done(dve.tensor_scalar(w[:, cols], w[:, cols], 1.0, -1.0, ALU.min, ALU.max))
            dve.tensor_scalar(wq[:, :, :].rearrange("p c n -> p (c n)")[:, cols], w[:, cols], MAGIC, -MAGIC, ALU.add, ALU.add)\
               .then_inc(w_ready, 1)

        def quantize_w2(n):
            if n == 8:
                weight_scale(1)
            elif 10 <= n <= 16 and n % 2 == 0:
                round_weights(1, (n - 10) // 2)

        weight_scale(0)
        for n in range(4):
            round_weights(0, n)
        by_batch = lambda ap: ap.rearrange("p (b t) -> p b t", b=B)
        steps.done(dve.memset(top[:, :], 0.0))
        dve.wait_ge(spread_ready, 1)
        for n in range(NH + 2):
            if n < NH:
                dve.wait_ge(h_done, n + 1)
                if n >= 2:
                    dve.wait_ge(conv_done, n - 1)
                dve.tensor_tensor(scaled[:, n % 2, :], ps[:, LIN + n % 4, :], inv_row[:, :], ALU.mult).then_inc(scaled_ready, 1)
            if 1 <= n <= NH:
                c = n - 1
                dve.wait_ge(tap, c + 1)
                y, v = by_batch(conv_y[:, c % 2, :]), by_batch(scaled[:, c % 2, :])
                steps.done(dve.scalar_tensor_tensor(y[:, :, 1:], v[:, :, 0:L - 1], conv_w[:, c, 0:1], y[:, :, 1:],
                                                    ALU.mult, ALU.add))
                dve.scalar_tensor_tensor(y[:, :, 0:L - 1], v[:, :, 1:], conv_w[:, c, 2:3], y[:, :, 0:L - 1],
                                         ALU.mult, ALU.add).then_inc(conv_done, 1)
            if n >= 2:
                c = n - 2
                dve.wait_ge(mag_ready, c + 1)
                if c:
                    dve.wait_ge(top_ready, c)
                dve.tensor_tensor(top[:, :], top[:, :], magnitude[:, c % 2, :], ALU.max).then_inc(top_ready, 1)
            quantize_w2(n)
        dve.wait_ge(top_turned, 1)
        steps.done(dve.tensor_reduce(hid_max, ps[:, TURN, :].rearrange("p (t n) -> p t n", t=TT), AX.X, ALU.max))
        scales(hid_max, hid_scale, hid_inv)
        for t in range(TT):
            last = dve.tensor_scalar(diag[:, t, :], m.ident[:, :], hid_scale[:, t:t + 1], None, ALU.mult)
        last.then_inc(diag2_ready, 1)
        steps.done(dve.tensor_scalar(hid_inv, hid_inv, w_mean[:, 1:2], None, ALU.mult))
        dve.wait_ge(spread2_done, 1)
        for n in range(NH):
            steps.done(dve.tensor_tensor(hidden(n), hidden(n), ps[:, SPREAD, :], ALU.mult))
            dve.tensor_scalar(hidden(n), hidden(n), 127.0, -128.0, ALU.min, ALU.max).then_inc(clipped, 1)
        for t in range(TT):
            dve.wait_ge(out_done, outs + t + 1)
            tile_added(dve, m, k, t, dve.scalar_tensor_tensor(m.x[:, t, :], ps[:, LIN + t, :], hid_inv[:, t:t + 1], m.x[:, t, :],
                                                             ALU.mult, ALU.add))

    return tensor, scalar, vector, None


def context_attention(nc, m, first_unit, k):
    SCALE = 32 ** -0.5
    PAIRS = 8
    with ExitStack() as mem:
        sb = lambda name, shape, dt=F32: mem.enter_context(nc.sbuf_tensor("ca_" + name, shape, dt))
        ctx = sb("ctx", [P, 2, KC, KEYS])
        kt = sb("kt", [P, 2, KC, KEYS])
        xh, xl = sb("xh", [P, 2, KC, T], F32R), sb("xl", [P, 2, KC, T], F32R)
        rows = sb("rows", [P, TT, D])
        q = sb("q", [P, KC, B, L])
        q_pairs = sb("q_pairs", [P, 2, KC, 2, 2, L])
        v = sb("v", [P, 2, TT, D])
        p, pt = sb("p", [P, 2, KEYS]), sb("pt", [P, TT, P])
        o = sb("o", [P, KC, T])
        bias = sb("bias", [P, D])
        small = sb("small", [P, 8])
    nmax, rsum, rinv = small[:, 0:2], small[:, 2:4], small[:, 4:6]
    oh, ol = xh[:, 0], xl[:, 0]
    latents = NormalizedColumns(m, k, rows, xh[:, 1], xl[:, 1], (5, 6, 7, 0))
    s = lambda name: m.sem("ca_" + name)
    (ctx_loaded0, loads0), (ctx_loaded1, _) = (m.shared(f"ctx_loaded{n}", 16 * B // 2) for n in range(2))
    ctx_loaded = (ctx_loaded0, ctx_loaded1)
    bias_loaded, q_ready = s("bias_loaded"), s("q_ready")
    (q_zero, zeros), (staged, stages) = m.shared("q_zero", 1), m.shared("queries_staged", B)
    ctx_high, ctx_split, kt_ready = s("ctx_high"), s("ctx_split"), s("kt_ready")
    (lin_done, lins), (v_ready, vals) = m.shared("lin_done", 8 * B), m.shared("v_ready", 4 * B)
    (scores, before), (nmax_ready, _), (exp_done, _), (p_ready, _), (pt_done, _), (pt_ready, _), (pv_done, _), (o_ready, _) = (
        m.shared(n, PAIRS * B) for n in ("scores", "nmax_ready", "exp_done", "p_ready", "pt_done", "pt_ready", "pv_done", "o_ready"))
    (o_high, halves), (o_split, _) = m.shared("out_high", 4), m.shared("out_split", 4)
    out_done, outs = m.shared("out_done", TT - 1)
    SC, LIN, PTB, PV = (0, 5), 1, 6, 7
    QB = (5, 6, 7, 0)
    ps = m.ps
    first = lambda b, value: isinstance(b, int) and b == value

    def lhs(h, n, c):
        return h[:, n % RING_UNITS, c * P:(c + 1) * P]

    def tensor(pe):
        def queries(n):
            u = first_unit + n
            pe.wait_ge(m.unit_ready, u + 1)
            latents.wait_split(pe, KC)
            for c in range(KC):
                last = product(pe, ps[:, QB[n], :], (lhs(m.wh, u, c), lhs(m.wl, u, c)),
                               (xh[:, 1, c, :], xl[:, 1, c, :]), c == 0, c == KC - 1)
            last.then_inc(m.unit_done, 1)

        def linear(b, par, l, chunks):
            bank = ps[:, LIN + l % 4, :]
            if chunks[0] == 0 and l < 4 and not first(b, 0):
                pe.wait_ge(v_ready, vals + 4 * b + l - 3)
            elif chunks[0] == 0 and l >= 4:
                pe.wait_ge(kt_ready, 4 * b + l - 3)
            for c in chunks:
                if l == 0:
                    pe.wait_ge(ctx_split, KC * b + c + 1)
                x_c = (xh[:, par, c, :], xl[:, par, c, :])
                if l < 4:
                    u = first_unit + 4 + l
                    pe.wait_ge(m.unit_ready, u + 1)
                    last = product(pe, bank, (lhs(m.wh, u, c), lhs(m.wl, u, c)), x_c, c == 0, c == KC - 1)
                else:
                    u = first_unit + 8 + c
                    pe.wait_ge(m.unit_ready, u + 1)
                    t = slice((l - 4) * P, (l - 3) * P)
                    last = product(pe, bank, (x_c[0][:, t], x_c[1][:, t]),
                                   (m.wh[:, u % RING_UNITS, :], m.wl[:, u % RING_UNITS, :]), c == 0, c == KC - 1)
            if chunks[-1] == KC - 1:
                last.then_inc(lin_done, 1)

        def attention_scores(b, par, hp):
            if hp == 0:
                pe.wait_ge(staged, stages + b + 1)
                pe.wait_ge(kt_ready, 4 * b + 4)
            if not (first(b, 0) and hp < 2):
                pe.wait_ge(exp_done, before + PAIRS * b + hp - 1)
            pe.matmul(ps[:, SC[hp % 2], :], q_pairs[:, par, hp // 2, hp % 2, :, :].rearrange("p e l -> p (e l)"),
                      kt[:, par, hp // 2, :], start=True, stop=True).then_inc(scores, 1)

        def probability_transposes(b, hp):
            pe.wait_ge(p_ready, before + PAIRS * b + hp + 1)
            if not (first(b, 0) and hp == 0):
                pe.wait_ge(pt_ready, before + PAIRS * b + hp)
            for t in range(TT):
                last = pe.transpose(ps[:, PTB, t * P:(t + 1) * P], p[:, hp % 2, t * P:(t + 1) * P], m.ident[:, :])
            last.then_inc(pt_done, 1)

        def values(b, par, hp):
            pe.wait_ge(pt_ready, before + PAIRS * b + hp + 1)
            pe.wait_ge(v_ready, vals + 4 * b + 4)
            if not (first(b, 0) and hp == 0):
                pe.wait_ge(o_ready, before + PAIRS * b + hp)
            for t in range(TT):
                last = pe.matmul(ps[:, PV, 0:P], v[:, par, t, (hp // 2) * P:(hp // 2 + 1) * P], pt[:, t, :],
                                 start=t == 0, stop=t == TT - 1)
            last.then_inc(pv_done, 1)

        def project(t, chunks):
            pe.wait_ge(o_split, halves + t + 1)
            for c in chunks:
                u = first_unit + 12 + c
                pe.wait_ge(m.unit_ready, u + 1)
                last = product(pe, ps[:, LIN + t, :], (oh[:, c, t * P:(t + 1) * P], ol[:, c, t * P:(t + 1) * P]),
                               (m.wh[:, u % RING_UNITS, :], m.wl[:, u % RING_UNITS, :]), c == 0, c == KC - 1)
                if t == TT - 1:
                    last.then_inc(m.unit_done, 1)
                elif c == KC - 1:
                    last.then_inc(out_done, 1)

        def step(b, par, lin=True, att=True, carry=True, release=False, out=False):
            for hp in range(PAIRS):
                behind = (b - 1, 1 - par, hp - 1) if hp else (b - 2, par, PAIRS - 1)
                follow = att and (hp or carry)
                if att:
                    attention_scores(b - 1, 1 - par, hp)
                if out and 1 <= hp < 7:
                    project((hp - 1) // 2, (range(0, 2), range(2, 4))[(hp - 1) % 2])
                if lin:
                    linear(b, par, hp, range(0, 2))
                if follow:
                    probability_transposes(behind[0], behind[2])
                if lin:
                    linear(b, par, hp, range(2, 4))
                if follow:
                    values(*behind)
                if release and hp == 4:
                    pe.wait_ge(lin_done, lins + 8 * b + 4)
                    pe.sem_inc(m.unit_done, 4)
        for l in range(KC):
            linear(0, 0, l, range(KC))
        latents.tensor(pe)
        for n in range(KC):
            queries(n)
        for l in range(KC, 2 * KC):
            linear(0, 0, l, range(KC))
        pe.wait_ge(q_ready, KC)
        step(1, 1, carry=False)
        with pe.Fori(1, B // 2 - 1) as i:
            step(2 * i, 0)
            step(2 * i + 1, 1)
        step(B - 2, 0)
        step(B - 1, 1, release=True)
        pe.wait_ge(lin_done, lins + 8 * B)
        pe.sem_inc(m.unit_done, 4)
        step(B, 0, lin=False, out=True)
        probability_transposes(B - 1, PAIRS - 1)
        values(B - 1, 1, PAIRS - 1)

        project(TT - 1, range(KC))

    def scalar(act):
        act.wait_ge(m.x_loaded, 16)
        for b in range(2):
            act.dma_start(ctx[:, b, :, :], m.d["ctx_columns"][b]).then_inc(ctx_loaded[b], 16)
        act.dma_start(bias[:, :], m.d["ca_bias"]).then_inc(bias_loaded, 16)

        def high(b, par, c):
            if c == 0:
                act.wait_ge(ctx_loaded[par], loads0 + 8 * (b - par) + 16)
                if not first(b, 0):
                    act.wait_ge(lin_done, lins + 8 * (b - 1))
            act.copy(xh[:, par, c, :], ctx[:, par, c, :]).then_inc(ctx_high, 1)

        def stage_queries(b, par):
            if first(b, 0):
                act.wait_ge(q_zero, zeros + 1)
                act.wait_ge(q_ready, KC)
            for h in range(4):
                part = slice(32 * h, 32 * h + 32)
                last = act.copy(q_pairs[part, par, :, h // 2, h % 2, :],
                                q[part, :, bass.ds(b, 1), :].rearrange("p c o l -> p c (o l)"))
            last.then_inc(staged, 1)

        def exponentials(b, hp):
            act.wait_ge(nmax_ready, before + PAIRS * b + hp + 1)
            act.activation(p[:, hp % 2, :], ps[:, SC[hp % 2], :], ACT.Exp, bias=nmax[:, hp % 2:hp % 2 + 1],
                           accum_out=rsum[:, hp % 2:hp % 2 + 1]).then_inc(exp_done, 1)

        def transposed(b, hp):
            act.wait_ge(pt_done, before + PAIRS * b + hp + 1)
            if not (first(b, 0) and hp == 0):
                act.wait_ge(pv_done, before + PAIRS * b + hp)
            act.copy(pt[:, :, :].rearrange("p t n -> p (t n)"), ps[:, PTB, :]).then_inc(pt_ready, 1)

        def output(b, hp):
            act.wait_ge(pv_done, before + PAIRS * b + hp + 1)
            for e in range(2):
                part = slice(64 * (hp % 2) + 32 * e, 64 * (hp % 2) + 32 * e + 32)
                last = act.copy(o[part, hp // 2, bass.ds(b * L, L)], ps[part, PV, 64 * e:64 * e + 64])
            last.then_inc(o_ready, 1)

        def output_high(t):
            act.copy(oh[:, :, t * P:(t + 1) * P], o[:, :, t * P:(t + 1) * P]).then_inc(o_high, 1)

        def step(b, par, lin=True, att=True, carry=True, nxt=True, out=False):
            for hp in range(PAIRS):
                behind = (b - 1, hp - 1) if hp else (b - 2, PAIRS - 1)
                follow = att and (hp or carry)
                if out and hp < TT - 1:
                    output_high(hp)
                if att:
                    exponentials(b - 1, hp)
                if follow:
                    transposed(*behind)
                if lin and hp >= 4:
                    t = hp - 4
                    act.wait_ge(lin_done, lins + 8 * b + 5 + t)
                    act.copy(v[:, par, t, :], ps[:, LIN + t, :]).then_inc(v_ready, 1)
                if follow:
                    output(*behind)
                if lin and hp == 2:
                    stage_queries(b, par)
                if nxt and hp % 2:
                    high(b + 1, 1 - par, hp // 2)

        for c in range(KC):
            high(0, 0, c)
        latents.scalar_guess(act)
        latents.scalar_high(act)
        for n in range(KC):
            act.wait_ge(m.unit_done, first_unit + n + 1)
            act.activation(q[:, n, :, :].rearrange("p b l -> p (b l)"), ps[:, QB[n], :], ACT.Copy, scale=SCALE)\
               .then_inc(q_ready, 1)
        step(0, 0, att=False)
        step(1, 1, carry=False)
        with act.Fori(1, B // 2 - 1) as i:
            step(2 * i, 0)
            step(2 * i + 1, 1)
        step(B - 2, 0)
        step(B - 1, 1, nxt=False)
        step(B, 0, lin=False, nxt=False, out=True)
        transposed(B - 1, PAIRS - 1)
        output(B - 1, PAIRS - 1)
        act.wait_ge(o_ready, before + PAIRS * B)
        output_high(TT - 1)

    def vector(dve):
        steps = m.dve_steps

        def low(b, par, c):
            dve.wait_ge(ctx_high, KC * b + c + 1)
            dve.tensor_tensor(xl[:, par, c, :], ctx[:, par, c, :], f32(xh[:, par, c, :]), ALU.subtract)\
               .then_inc(ctx_split, 1)

        def softmax(b, hp):
            slot = slice(hp % 2, hp % 2 + 1)
            dve.wait_ge(scores, before + PAIRS * b + hp + 1)
            dve.tensor_reduce(nmax[:, slot], ps[:, SC[hp % 2], :], AX.X, ALU.max, negate=True).then_inc(nmax_ready, 1)
            dve.wait_ge(exp_done, before + PAIRS * b + hp + 1)
            steps.done(dve.reciprocal(rinv[:, slot], rsum[:, slot]))
            dve.tensor_scalar(p[:, hp % 2, :], p[:, hp % 2, :], rinv[:, slot], None, ALU.mult).then_inc(p_ready, 1)

        def output_low(t):
            dve.wait_ge(o_high, halves + t + 1)
            tile = (slice(None), slice(None), slice(t * P, (t + 1) * P))
            dve.tensor_tensor(ol[tile], o[tile], f32(oh[tile]), ALU.subtract).then_inc(o_split, 1)

        def add_output(t):
            if t < TT - 1:
                dve.wait_ge(out_done, outs + t + 1)
            else:
                dve.wait_ge(m.unit_done, first_unit + 16)
            tile_added(dve, m, k, t, dve.tensor_tensor(m.x[:, t, :], m.x[:, t, :], ps[:, LIN + t, :], ALU.add))

        def step(b, par, lin=True, att=True, nxt=True, out=False):
            for hp in range(PAIRS):
                if out and hp < TT - 1:
                    output_low(hp)
                if att:
                    softmax(b - 1, hp)
                if out and hp in (3, 5, 7):
                    add_output((hp - 3) // 2)
                if lin and hp < 4:
                    keys(b, par, hp)
                if nxt and hp % 2:
                    low(b + 1, 1 - par, hp // 2)

        def keys(b, par, l):
            dve.wait_ge(lin_done, lins + 8 * b + l + 1)
            dve.tensor_copy(kt[:, par, l, :], ps[:, LIN + l, :]).then_inc(kt_ready, 1)

        for c in range(KC):
            low(0, 0, c)
        latents.vector_rows(dve, steps)
        dve.memset(q_pairs[:, :, :, :, :, :].rearrange("p s c r e l -> p (s c r e l)"), 0.0).then_inc(q_zero, 1)
        for l in range(KC):
            keys(0, 0, l)
        latents.vector_low(dve)
        dve.wait_ge(bias_loaded, 16)
        latents.wait_rows(dve)
        for t in range(TT):
            steps.mark(dve.tensor_tensor(m.x[:, t, :], m.x[:, t, :], bias[:, :], ALU.add))
        steps.wait()
        for c in range(KC):
            low(1, 1, c)
        step(1, 1)
        with dve.Fori(1, B // 2 - 1) as i:
            steps.enter(i - 1, 16)
            step(2 * i, 0)
            step(2 * i + 1, 1)
            steps.leave(B // 2 - 2)
        step(B - 2, 0)
        step(B - 1, 1, nxt=False)
        step(B, 0, lin=False, nxt=False, out=True)
        output_low(TT - 1)
        add_output(TT - 1)

    def loads(sp):
        with sp.Fori(1, B // 2) as i:
            for par in range(2):
                b = 2 * i + par
                sp.wait_ge(ctx_split, KC * (b - 1))
                sp.dma_start(ctx[:, par, :, :], m.d["ctx_columns"][bass.ds(b, 1)].rearrange("o p c n -> (o p) c n"))\
                  .then_inc(ctx_loaded[par], 16)

    return tensor, scalar, vector, loads


def linear_attention(nc, m, first_unit, k):
    HEADS, HD, FEATURES = 16, 32, 64
    PAIRS = HEADS // 2
    GROUP = 3
    GROUPS = (HEADS + GROUP - 1) // GROUP
    with ExitStack() as mem:
        sb = lambda name, shape, dt=F32: mem.enter_context(nc.sbuf_tensor("li_" + name, shape, dt))
        rows = sb("rows", [P, TT, D])
        xh, xl = sb("xh", [P, KC, T], F32R), sb("xl", [P, KC, T], F32R)
        qk_h, qk_l = sb("qk_h", [P, 2 * KC, T], F32R), sb("qk_l", [P, 2 * KC, T], F32R)
        feat = sb("feat", [P, 2, PAIRS, T])
        v = sb("v", [P, TT, HEADS, HD + 1])
        masked = sb("masked", [P, 2, TT, P])
        proj = sb("proj", [P, KC, 2, P])
        proj_h, proj_l = sb("proj_h", [P, KC, 2, P], F32R), sb("proj_l", [P, KC, 2, P], F32R)
        causal = sb("causal", [P, P])
        v_bias, out_bias = sb("v_bias", [P, D]), sb("out_bias", [P, D])
        small = sb("small", [P, 24])
    qk_bias = small[:, 0:8]
    inv = small[:, 8:8 + GROUP * TT].rearrange("p (h t) -> p h t", t=TT)
    latents = NormalizedColumns(m, k, rows, xh, xl, (0, 1, 2, 3))
    released = m.shared("out_split", 0)
    s = lambda name: m.sem("li_" + name)
    consts, loaded = m.shared("stage_consts", 4 * 16)
    proj_zero, proj_loaded, proj_split, ones_ready = s("proj_zero"), s("proj_loaded"), s("proj_split"), s("ones_ready")
    qk_high, qk_split, v_ready = s("qk_high"), s("qk_split"), s("v_ready")
    feat_done, fq_ready, fk_ready = s("feat_done"), s("fq_ready"), s("fk_ready")
    scores, mask_done, group_done, rows_out = s("scores"), s("mask_done"), s("group_done"), s("rows_out")
    o_turned = s("o_turned")
    (o_high, halves), (o_split, _) = m.shared("out_high", 4), m.shared("out_split", 4)
    out_done, outs = m.shared("out_done", TT - 1)
    QB, KB, VB, FB, SB, CB, OT, OB = 4, 0, 4, 0, 0, 2, 0, 4
    ps = m.ps

    def tensor(pe):
        latents.tensor(pe)
        for j, bank in enumerate((QB, KB)):
            for n in range(KC):
                u = first_unit + 4 * j + n
                pe.wait_ge(m.unit_ready, u + 1)
                at = u % RING_UNITS
                for c in range(KC):
                    latents.wait_split(pe, c + 1)
                    last = product(pe, ps[:, bank + n, :], (m.wh[:, at, c * P:(c + 1) * P], m.wl[:, at, c * P:(c + 1) * P]),
                                   (xh[:, c, :], xl[:, c, :]), c == 0, c == KC - 1)
                last.then_inc(m.unit_done, 1)
        for c in range(KC):
            u = first_unit + 8 + c
            pe.wait_ge(m.unit_ready, u + 1)
            for t in range(TT):
                if c == 0:
                    pe.wait_ge(qk_split, t + 1)
                last = product(pe, ps[:, VB + t, :], (xh[:, c, t * P:(t + 1) * P], xl[:, c, t * P:(t + 1) * P]),
                               (m.wh[:, u % RING_UNITS, :], m.wl[:, u % RING_UNITS, :]), c == 0, c == KC - 1)
            last.then_inc(m.unit_done, 1)
        pe.wait_ge(proj_split, 1)
        pe.wait_ge(qk_split, 2 * KC)
        for pair in range(PAIRS):
            if pair >= 2:
                pe.wait_ge(fq_ready, pair - 1)
                pe.wait_ge(fk_ready, pair - 1)
            for j in range(2):
                at = pair // 2
                product(pe, ps[:, FB + 2 * (pair % 2) + j, :], (proj_h[:, at, pair % 2, :], proj_l[:, at, pair % 2, :]),
                        (qk_h[:, KC * j + at, :], qk_l[:, KC * j + at, :]), True, True).then_inc(feat_done, 1)
        pe.wait_ge(fq_ready, PAIRS)
        pe.wait_ge(fk_ready, PAIRS)
        pe.wait_ge(v_ready, TT)
        pe.wait_ge(ones_ready, 1)

        def context(h):
            pe.wait_ge(mask_done, h + 1)
            for t in range(TT):
                at = ((h % GROUP) * TT + t) * (HD + 1)
                last = pe.matmul(ps[:, CB + h // GROUP, at:at + HD + 1], masked[:, h % 2, t, :], v[:, t, h, :],
                                 start=True, stop=True)
            last.then_inc(group_done, 1)

        for h in range(HEADS):
            part = slice(FEATURES * (h % 2), FEATURES * (h % 2) + FEATURES)
            if h >= 2:
                pe.wait_ge(mask_done, h - 1)
            for t in range(TT):
                tok = slice(t * P, (t + 1) * P)
                last = pe.matmul(ps[:, SB + h % 2, tok], feat[part, 1, h // 2, tok], feat[part, 0, h // 2, tok],
                                 start=True, stop=True)
            last.then_inc(scores, 1)
            if h:
                context(h - 1)
        context(HEADS - 1)
        pe.wait_ge(rows_out, GROUPS)
        for c in range(KC):
            for t in range(TT):
                last = pe.transpose(ps[:, OT + c, t * P:(t + 1) * P], rows[:, t, c * P:(c + 1) * P], m.ident[:, :])
            last.then_inc(o_turned, 1)
        for c in range(KC):
            u = first_unit + 12 + c
            pe.wait_ge(m.unit_ready, u + 1)
            pe.wait_ge(o_split, halves + c + 1)
            for t in range(TT):
                last = product(pe, ps[:, OB + t, :], (xh[:, c, t * P:(t + 1) * P], xl[:, c, t * P:(t + 1) * P]),
                               (m.wh[:, u % RING_UNITS, :], m.wl[:, u % RING_UNITS, :]), c == 0, c == KC - 1)
                if c == KC - 1 and t < TT - 1:
                    last.then_inc(out_done, 1)
            last.then_inc(m.unit_done, 1)

    def scalar(act):
        act.wait_ge(m.x_loaded, 16)
        if k:
            act.wait_ge(*released)
        for out, src in ((causal[:, :], m.d["causal"]), (v_bias[:, :], m.d["v_bias"]), (out_bias[:, :], m.d["li_bias"]),
                         (qk_bias, m.d["qk_bias"])):
            act.dma_start(out, src).then_inc(consts, 16)
        latents.scalar_guess(act)
        act.wait_ge(proj_zero, 1)
        for h in range(4):
            act.dma_start(proj[32 * h:32 * h + 32, :, h // 2, 64 * (h % 2):64 * (h % 2) + 64], m.d["proj"][h])\
               .then_inc(proj_loaded, 16)
        latents.scalar_high(act)
        act.wait_ge(consts, loaded + 4 * 16)
        for n in range(2 * KC):
            act.wait_ge(m.unit_done, first_unit + n + 1)
            act.activation(qk_h[:, n, :], ps[:, (QB, KB)[n // KC] + n % KC, :], ACT.Identity, bias=qk_bias[:, n:n + 1])\
               .then_inc(qk_high, 1)
        for pair in range(PAIRS):
            act.wait_ge(feat_done, 2 * pair + 1)
            act.activation(feat[:, 0, pair, :], ps[:, FB + 2 * (pair % 2), :], ACT.Relu).then_inc(fq_ready, 1)
        for c in range(KC):
            act.wait_ge(o_turned, c + 1)
            act.copy(xh[:, c, :], ps[:, OT + c, :]).then_inc(o_high, 1)

    def vector(dve):
        steps = m.dve_steps
        dve.wait_ge(m.x_loaded, 16)
        if k:
            dve.wait_ge(m.x_ready, TT * k)
        dve.memset(proj[:, :, :, :].rearrange("p c r n -> p (c r n)"), 0.0).then_inc(proj_zero, 1)
        latents.vector_rows(dve, steps)
        dve.memset(v[:, :, :, HD:HD + 1], 1.0).then_inc(ones_ready, 1)
        latents.vector_low(dve)
        dve.wait_ge(consts, loaded + 4 * 16)
        latents.wait_rows(dve)
        for t in range(TT):
            steps.mark(dve.tensor_tensor(m.x[:, t, :], m.x[:, t, :], out_bias[:, :], ALU.add))
        dve.wait_ge(proj_loaded, 4 * 16)
        steps.done(dve.tensor_copy(proj_h[:, :, :, :], proj[:, :, :, :]))
        dve.tensor_tensor(proj_l[:, :, :, :], proj[:, :, :, :], f32(proj_h[:, :, :, :]), ALU.subtract).then_inc(proj_split, 1)
        for n in range(2 * KC):
            dve.wait_ge(qk_high, n + 1)
            dve.scalar_tensor_tensor(qk_l[:, n, :], ps[:, (QB, KB)[n // KC] + n % KC, :], qk_bias[:, n:n + 1],
                                     f32(qk_h[:, n, :]), ALU.add, ALU.subtract).then_inc(qk_split, 1)
        dve.wait_ge(m.unit_done, first_unit + 12)
        by_head = lambda ap: ap.rearrange("p (h d) -> p h d", d=HD)
        for t in range(TT):
            dve.tensor_tensor(v[:, t, :, 0:HD], by_head(ps[:, VB + t, :]), by_head(v_bias[:, :]), ALU.add).then_inc(v_ready, 1)
        for pair in range(PAIRS):
            dve.wait_ge(feat_done, 2 * pair + 2)
            dve.tensor_scalar(feat[:, 1, pair, :], ps[:, FB + 2 * (pair % 2) + 1, :], 0.0, None, ALU.max).then_inc(fk_ready, 1)

        def divide(g):
            h0, h1 = g * GROUP, min((g + 1) * GROUP, HEADS)
            n = h1 - h0
            dve.wait_ge(group_done, h1)
            if g:
                dve.wait_ge(rows_out, g)
            out = ps[:, CB + g, 0:n * TT * (HD + 1)].rearrange("p (h t d) -> p h t d", h=n, t=TT)
            steps.done(dve.tensor_scalar(inv[:, 0:n, :], out[:, :, :, HD], 1e-6, None, ALU.add))
            steps.done(dve.reciprocal(inv[:, 0:n, :], inv[:, 0:n, :]))
            for t in range(TT):
                last = dve.tensor_tensor(by_head(rows[:, t, h0 * HD:h1 * HD]), out[:, :, t, 0:HD],
                                         inv[:, 0:n, t:t + 1].to_broadcast([P, n, HD]), ALU.mult)
            last.then_inc(rows_out, 1)

        for h in range(HEADS):
            dve.wait_ge(scores, h + 1)
            if h >= 2:
                dve.wait_ge(group_done, h - 1)
            dve.tensor_tensor(masked[:, h % 2, :, :], ps[:, SB + h % 2, :].rearrange("p (t n) -> p t n", t=TT),
                              causal[:, :].rearrange("p (o n) -> p o n", o=1).to_broadcast([P, TT, P]), ALU.mult)\
               .then_inc(mask_done, 1)
            if h % GROUP == 1 and h > GROUP:
                divide(h // GROUP - 1)
        for g in range((HEADS - 1) // GROUP - 1, GROUPS):
            divide(g)
        for c in range(KC):
            dve.wait_ge(o_high, halves + c + 1)
            dve.tensor_tensor(xl[:, c, :], ps[:, OT + c, :], f32(xh[:, c, :]), ALU.subtract).then_inc(o_split, 1)
        for t in range(TT):
            if t < TT - 1:
                dve.wait_ge(out_done, outs + t + 1)
            else:
                dve.wait_ge(m.unit_done, first_unit + 16)
            tile_added(dve, m, k, t, dve.tensor_tensor(m.x[:, t, :], m.x[:, t, :], ps[:, OB + t, :], ALU.add))

    return tensor, scalar, vector, None


def experts(nc, m, first_unit, k):
    E, F = 8, 1024
    NF = F // P
    LIMIT, ALPHA = 9.0, 1.702
    with ExitStack() as mem:
        sb = lambda name, shape, dt=F32: mem.enter_context(nc.sbuf_tensor("ex_" + name, shape, dt))
        xh, xl = sb("xh", [P, KC, T], F32R), sb("xl", [P, KC, T], F32R)
        hh, hl = sb("hh", [P, NF, T], F32R), sb("hl", [P, NF, T], F32R)
        rows = sb("rows", [P, TT, D])
        g, u, sg, h = sb("g", [P, 2, T]), sb("u", [P, 2, T]), sb("sg", [P, 2, T]), sb("h", [P, 2, T])
        b1 = sb("b1", [P, E, NF, 2])
        b2 = sb("b2", [E, D])
        gw_raw = sb("gw_raw", [P, KC, E])
        gwh, gwl = sb("gwh", [P, KC, E], F32R), sb("gwl", [P, KC, E], F32R)
        before = sb("before", [P, E, E])
        gates, rank, best, second, coef = (sb(n, [P, TT, E]) for n in ("gates", "rank", "best", "second", "coef"))
        greater, equal = sb("greater", [P, TT, E, E]), sb("equal", [P, TT, E, E])
        v1, v2, w1, w2 = (sb(n, [P, TT]) for n in ("v1", "v2", "w1", "w2"))
        coef_t = sb("coef_t", [E, T])
    UNITS = 3 * NF
    m.scalar_from = first_unit + RING_UNITS
    released = m.shared("out_split", 0)
    s = lambda name: m.sem("ex_" + name)
    consts, loaded = m.shared("stage_consts", 4 * 16)
    ln = NormalizedColumns(m, k, rows, xh, xl, (1, 2, 3, 4))
    gw_split, gates_done, gates_t_ready, gates_turned = (s(n) for n in ("gw_split", "gates_done", "gates_t_ready", "gates_turned"))
    diff_ready, diff_exp = s("diff_ready"), s("diff_exp")
    coef_ready, coef_turned, coef_t_ready, bias_done, bias_added = (
        s(n) for n in ("coef_ready", "coef_turned", "coef_t_ready", "bias_done", "bias_added"))
    g_ready, u_ready, sg_ready, h_ready, h_high, h_split = (
        s(n) for n in ("g_ready", "u_ready", "sg_ready", "h_ready", "h_high", "h_split"))
    tile_done, added = s("tile_done"), s("added")
    LIN, OUT, GATE = 1, (0, 5, 6, 7), 5
    ps = m.ps

    def tensor(pe):
        ln.tensor(pe)
        ln.wait_split(pe, KC)
        pe.wait_ge(gw_split, 1)
        for c in range(KC):
            last = product(pe, ps[0:E, GATE, :], (gwh[:, c, :], gwl[:, c, :]), (xh[:, c, :], xl[:, c, :]), c == 0, c == KC - 1)
        last.then_inc(gates_done, 1)

        def turn_gates():
            pe.wait_ge(gates_t_ready, 1)
            for t in range(TT):
                last = pe.transpose(ps[:, GATE, t * E:(t + 1) * E], coef_t[:, t * P:(t + 1) * P], m.ident[0:E, 0:E])
            last.then_inc(gates_turned, 1)

        def turn_weights():
            pe.wait_ge(coef_ready, 1)
            for t in range(TT):
                last = pe.transpose(ps[0:E, 6, t * P:(t + 1) * P], coef[:, t, :], m.ident[:, :])
            last.then_inc(coef_turned, 1)

        def output_biases():
            pe.wait_ge(coef_t_ready, 1)
            for t in range(TT):
                pe.matmul(ps[:, OUT[t], :], coef_t[:, t * P:(t + 1) * P], b2[:, :], start=True, stop=True).then_inc(bias_done, 1)

        def expert(e, is_first):
            for n in range(2 * NF):
                u0 = first_unit + n
                bank = LIN + n % 4
                pe.wait_ge(m.unit_ready, first_unit + 24 * e + (n + 1))
                if n >= 4 or not is_first:
                    pe.wait_ge((g_ready, u_ready)[n % 2], 8 * e + (n // 2 - 1))
                for c in range(KC):
                    w = (m.wh[:, u0 % RING_UNITS, c * P:(c + 1) * P], m.wl[:, u0 % RING_UNITS, c * P:(c + 1) * P])
                    last = product(pe, ps[:, bank, :], w, (xh[:, c, :], xl[:, c, :]), c == 0, c == KC - 1)
                last.then_inc(m.unit_done, 1)
                if is_first and n == 0:
                    turn_gates()
                if is_first and n == 5:
                    turn_weights()
                if is_first and n == 8:
                    output_biases()
            for n in range(NF):
                at = 2 * NF + n
                slot = (first_unit + at) % RING_UNITS
                pe.wait_ge(m.unit_ready, first_unit + 24 * e + (at + 1))
                pe.wait_ge(h_split, 8 * e + (n + 1))
                for t in range(TT):
                    if n == 0:
                        if is_first:
                            pe.wait_ge(bias_added, t + 1)
                        else:
                            pe.wait_ge(added, 4 * e + (t - 3))
                    cols = slice(t * P, (t + 1) * P)
                    last = product(pe, ps[:, OUT[t], :], (hh[:, n, cols], hl[:, n, cols]),
                                   (m.wh[:, slot, :], m.wl[:, slot, :]), n == 0, n == NF - 1)
                    if n == NF - 1 and t < TT - 1:
                        last.then_inc(tile_done, 1)
                last.then_inc(m.unit_done, 1)

        expert(0, True)
        with pe.Fori(1, E) as e:
            expert(e, False)

    def scalar(act):
        act.wait_ge(m.x_loaded, 16)
        if k:
            act.wait_ge(*released)
        for out, src in ((b1[:, :, :, :], m.d["expert_b1"]), (b2[:, :], m.d["expert_b2"]), (gw_raw[:, :, :], m.d["gate_w"]),
                         (before[:, :, :], m.d["before"])):
            act.dma_start(out, src).then_inc(consts, 16)
        ln.scalar_guess(act)
        ln.scalar_high(act)
        act.wait_ge(diff_ready, 1)
        act.activation(w2[:, :], v2[:, :], ACT.Exp).then_inc(diff_exp, 1)

        def high_part(e, n):
            m.high_part(act, (first_unit // 8) + 3 * e + (n // 8 + 1), n % 8)

        def expert(e, is_first=False, is_last=False):
            for n in range(NF + 1):
                if is_first and n == 3:
                    act.wait_ge(coef_turned, 1)
                    act.copy(coef_t[:, :], ps[0:E, 6, :]).then_inc(coef_t_ready, 1)
                if n < NF:
                    act.wait_ge(m.unit_done, first_unit + UNITS * e + (2 * n + 2))
                    if n >= 2 or not is_first:
                        act.wait_ge(h_ready, 8 * e + (n - 1))
                    act.activation(u[:, n % 2, :], ps[:, LIN + (2 * n + 1) % 4, :], ACT.Identity,
                                   bias=b1[:, bass.ds(e, 1), n, 1:2].rearrange("p o n -> p (o n)")).then_inc(u_ready, 1)
                    high_part(e, 2 * n)
                    high_part(e, 2 * n + 1)
                    act.wait_ge(g_ready, 8 * e + (n + 1))
                    act.activation(sg[:, n % 2, :], g[:, n % 2, :], ACT.Sigmoid, scale=ALPHA).then_inc(sg_ready, 1)
                if n:
                    act.wait_ge(h_ready, 8 * e + n)
                    act.copy(hh[:, n - 1, :], h[:, (n - 1) % 2, :]).then_inc(h_high, 1)
            if not is_last:
                for n in range(2 * NF, UNITS):
                    high_part(e, n)

        expert(0, is_first=True)
        with act.Fori(1, E - 1) as e:
            expert(e)
        expert(E - 1, is_last=True)

    def vector(dve):
        steps = m.dve_steps
        if k:
            dve.wait_ge(m.x_ready, TT * k)
        ln.vector_rows(dve, steps)
        dve.wait_ge(consts, loaded + 4 * 16)
        steps.done(dve.tensor_copy(gwh[:, :, :], gw_raw[:, :, :]))
        dve.tensor_tensor(gwl[:, :, :], gw_raw[:, :, :], f32(gwh[:, :, :]), ALU.subtract).then_inc(gw_split, 1)
        ln.vector_low(dve)
        dve.wait_ge(gates_done, 1)
        dve.tensor_copy(coef_t[:, :], ps[0:E, GATE, :]).then_inc(gates_t_ready, 1)
        dve.wait_ge(gates_turned, 1)
        steps.done(dve.tensor_copy(gates[:, :, :].rearrange("p t e -> p (t e)"), ps[:, GATE, 0:TT * E]))
        of_e = gates[:, :, :].unsqueeze(3).to_broadcast([P, TT, E, E])
        of_f = gates[:, :, :].unsqueeze(2).to_broadcast([P, TT, E, E])
        steps.mark(dve.tensor_tensor(greater[:, :, :, :], of_f, of_e, ALU.is_gt))
        steps.done(dve.tensor_tensor(equal[:, :, :, :], of_f, of_e, ALU.is_equal))
        flat = lambda ap: ap.rearrange("p t e f -> p t (e f)")
        steps.done(dve.tensor_tensor(flat(equal[:, :, :, :]), flat(equal[:, :, :, :]),
                                     before[:, :, :].rearrange("p e f -> p (e f)").unsqueeze(1).to_broadcast([P, TT, E * E]), ALU.mult))
        steps.done(dve.tensor_tensor(flat(greater[:, :, :, :]), flat(greater[:, :, :, :]), flat(equal[:, :, :, :]), ALU.add))
        steps.done(dve.tensor_reduce(rank[:, :, :], greater[:, :, :, :], AX.X, ALU.add))
        steps.mark(dve.tensor_scalar(best[:, :, :], rank[:, :, :], 0.0, None, ALU.is_equal))
        steps.mark(dve.tensor_scalar(second[:, :, :], rank[:, :, :], 1.0, None, ALU.is_equal))
        steps.mark(dve.tensor_reduce(v1[:, :], gates[:, :, :], AX.X, ALU.max))
        steps.wait()
        steps.done(dve.tensor_tensor(coef[:, :, :], gates[:, :, :], second[:, :, :], ALU.mult))
        steps.done(dve.tensor_reduce(v2[:, :], coef[:, :, :], AX.X, ALU.add))
        dve.tensor_tensor(v2[:, :], v2[:, :], v1[:, :], ALU.subtract).then_inc(diff_ready, 1)
        dve.wait_ge(diff_exp, 1)
        steps.done(dve.tensor_scalar(w1[:, :], w2[:, :], 1.0, None, ALU.add))
        steps.done(dve.reciprocal(w1[:, :], w1[:, :]))
        steps.mark(dve.tensor_tensor(w2[:, :], w2[:, :], w1[:, :], ALU.mult))
        spread = lambda ap: ap.unsqueeze(2).to_broadcast([P, TT, E])
        steps.done(dve.tensor_tensor(best[:, :, :], best[:, :, :], spread(w1[:, :]), ALU.mult))
        steps.done(dve.tensor_tensor(second[:, :, :], second[:, :, :], spread(w2[:, :]), ALU.mult))
        dve.tensor_tensor(coef[:, :, :], best[:, :, :], second[:, :, :], ALU.add).then_inc(coef_ready, 1)

        def expert(e, is_first):
            for n in range(NF + 1):
                if is_first and n == 5:
                    for t in range(TT):
                        dve.wait_ge(bias_done, t + 1)
                        dve.tensor_tensor(m.x[:, t, :], m.x[:, t, :], ps[:, OUT[t], :], ALU.add).then_inc(bias_added, 1)
                if n < NF:
                    s0 = n % 2
                    dve.wait_ge(m.unit_done, first_unit + 24 * e + (2 * n + 1))
                    if n or not is_first:
                        steps.wait()
                    dve.tensor_scalar(g[:, s0, :], ps[:, LIN + (2 * n) % 4, :], b1[:, bass.ds(e, 1), n, 0:1].rearrange("p o n -> p (o n)"),
                                      LIMIT, ALU.add, ALU.min).then_inc(g_ready, 1)
                    dve.wait_ge(u_ready, 8 * e + (n + 1))
                    steps.mark(dve.tensor_scalar(u[:, s0, :], u[:, s0, :], LIMIT, -LIMIT, ALU.min, ALU.max))
                    dve.wait_ge(sg_ready, 8 * e + (n + 1))
                    steps.done(dve.tensor_tensor(g[:, s0, :], g[:, s0, :], sg[:, s0, :], ALU.mult))
                    if n >= 2 or not is_first:
                        dve.wait_ge(h_split, 8 * e + (n - 1))
                    dve.scalar_tensor_tensor(h[:, s0, :], u[:, s0, :], 1.0, g[:, s0, :], ALU.add, ALU.mult).then_inc(h_ready, 1)
                if n:
                    dve.wait_ge(h_high, 8 * e + n)
                    dve.tensor_tensor(hl[:, n - 1, :], h[:, (n - 1) % 2, :], f32(hh[:, n - 1, :]), ALU.subtract).then_inc(h_split, 1)
            for t in range(TT):
                if t < TT - 1:
                    dve.wait_ge(tile_done, 3 * e + (t + 1))
                else:
                    dve.wait_ge(m.unit_done, first_unit + 24 * e + 24)
                dve.scalar_tensor_tensor(m.x[:, t, :], ps[:, OUT[t], :], coef[:, t, bass.ds(e, 1)], m.x[:, t, :], ALU.mult, ALU.add)\
                   .then_inc(added, 1)

        expert(0, True)
        with dve.Fori(1, E) as e:
            steps.enter(e - 1, 16)
            expert(e, False)
            steps.leave(E - 1)
        dve.wait_ge(added, TT * E)
        dve.sem_inc(m.x_ready, TT)

    return tensor, scalar, vector, None


class Memory:

    def __init__(self):
        self.sems = {}

    def shared(self, name, raised):
        if name not in self.sems:
            self.sems[name] = [self.sem(name), 0]
        sem, before = self.sems[name]
        self.sems[name][1] += raised
        return sem, before


def program(nc, d, out, stages):
    m = Memory()
    m.d = d
    n_blocks = sum(STAGE_BLOCKS[name] for name, _ in stages)
    with ExitStack() as whole:
        sb = lambda name, shape, dt=F32: whole.enter_context(nc.sbuf_tensor(name, shape, dt))
        m.sem = lambda name: whole.enter_context(nc.semaphore(name))
        m.x = sb("x_rows", [P, TT, D])
        m.ident = sb("ident", [P, P])
        m.norm = NormMemory(sb)
        m.wh, m.wl = sb("w_high", [P, RING_UNITS, 512], F32R), sb("w_low", [P, RING_UNITS, 512], F32R)
        w_raw = sb("w_raw", [P, 2, 4, 512])
        one, one_ready = sb("one", [P, 1]), m.sem("one_ready")
        m.ps = whole.enter_context(nc.psum_tensor("ps", [P, 8, 512], F32))
        m.consts, m.x_loaded, m.x_ready = m.sem("consts"), m.sem("x_loaded"), m.sem("x_ready")
        raw_loaded = [m.sem("raw_loaded0"), m.sem("raw_loaded1")]
        unit_high, m.unit_ready, m.unit_done = m.sem("unit_high"), m.sem("unit_ready"), m.sem("unit_done")
        stored = m.sem("stored")
        dve_steps = m.sem("dve_steps")
        scalar_high = m.sem("scalar_high")
        m.scalar_from = None

        def high_part(act, pair, at):
            n = 8 * pair + at
            act.wait_ge(raw_loaded[at // 4], 16 * (pair + 1))
            act.wait_ge(m.unit_done, n - 7)
            act.copy(m.wh[:, at, :], w_raw[:, at // 4, at % 4, :]).then_inc(scalar_high, 1)

        m.high_part = high_part
        first, made = 0, []
        for k, (name, stage) in enumerate(stages):
            made.append((first, STAGE_BLOCKS[name], stage(nc, m, 4 * first, k)))
            first += STAGE_BLOCKS[name]
        block = whole.enter_context(nc.Block())

        @block.sync
        def _(sp):
            def load_block(n, slot):
                if not isinstance(n, int) or n >= 2:
                    sp.wait_ge(m.unit_ready, 4 * (n - 1))
                sp.dma_start(w_raw[:, slot, :, :], d["weights"][bass.ds(n, 1)].rearrange("o p u n -> (o p) u n"))\
                  .then_inc(raw_loaded[slot], 16)

            sp.dma_start(m.x[:, :, :], d["x"]).then_inc(m.x_loaded, 16)
            sp.dma_start(m.ident[:, :], d["ident"]).then_inc(m.consts, 16)
            done = 0
            for first, count, (_, _, _, loads) in made:
                last = min(first + count + (1 if count else 0), n_blocks)
                while done < min(2, last):
                    load_block(done, done)
                    done += 1
                if last - done > 4:
                    if done % 2:
                        load_block(done, 1)
                        done += 1
                    with sp.Fori(done // 2, last // 2) as i:
                        load_block(2 * i, 0)
                        load_block(2 * i + 1, 1)
                    done = last // 2 * 2
                for n in range(done, last):
                    load_block(n, n % 2)
                done = max(done, last)
                if loads:
                    loads(sp)
            sp.wait_ge(m.x_ready, TT * len(stages))
            sp.dma_start(out, m.x[:, :, :]).then_inc(stored, 16)
            sp.wait_ge(stored, 16)

        @block.gpsimd
        def _(pool):
            def split(pair, first_pair=False, high=True):
                for slot in range(2):
                    if high:
                        pool.wait_ge(raw_loaded[slot], 16 * (pair + 1))
                    for u in range(4):
                        n, at = 8 * pair + 4 * slot + u, 4 * slot + u
                        if high:
                            if not first_pair:
                                pool.wait_ge(m.unit_done, n - 7)
                            pool.tensor_tensor(m.wh[:, at, :], w_raw[:, slot, u, :], one[:, :].to_broadcast([P, 512]), ALU.mult)\
                                .then_inc(unit_high, 1)
                            pool.wait_ge(unit_high, n + 1)
                        else:
                            pool.wait_ge(scalar_high, n + 1 - m.scalar_from)
                        pool.tensor_tensor(m.wl[:, at, :], w_raw[:, slot, u, :], f32(m.wh[:, at, :]), ALU.subtract)\
                            .then_inc(m.unit_ready, 1)

            pool.memset(one[:, :], 1.0).then_inc(one_ready, 1)
            pool.wait_ge(one_ready, 1)
            pairs = n_blocks // 2
            own = pairs if m.scalar_from is None else m.scalar_from // 8
            if own:
                split(0, first_pair=True)
            if own > 1:
                with pool.Fori(1, own) as i:
                    split(i)
            if pairs > own:
                with pool.Fori(own, pairs) as i:
                    split(i, high=False)

        @block.scalar
        def _(act):
            for _, _, (_, scalar, _, _) in made:
                scalar(act)

        @block.vector
        def _(dve):
            m.dve_steps = Steps(dve, dve_steps)
            for _, _, (_, _, vector, _) in made:
                vector(dve)

        @block.tensor
        def _(pe):
            for _, _, (tensor, _, _, _) in made:
                tensor(pe)


STAGES = (("latent_attention", latent_attention), ("oscillator", oscillator), ("bit_ffn", bit_ffn),
          ("context_attention", context_attention), ("linear_attention", linear_attention), ("experts", experts))


def columns_unit(w):
    k, n = w.shape
    return w.reshape(k // 128, 128, n // 512, 4, 128).transpose(2, 1, 3, 0, 4).reshape(n // 512, 128, 4, k)


def rows_unit(w):
    return w.reshape(-1, 4, 128, 512).transpose(0, 2, 1, 3)


def per_partition(v):
    return np.ascontiguousarray(v.reshape(-1, 128).T)


def lay_out(i):
    i = {k: np.asarray(v) for k, v in i.items()}
    d = {"x": i["x"].reshape(4, 128, 512).transpose(1, 0, 2), "ident": np.eye(128, dtype=np.float32)}
    blocks = []
    at = np.arange(128)
    halves = np.arange(512).reshape(2, 4, 2, 32).transpose(2, 0, 1, 3).reshape(512)
    wkv = i["L0_xattn_Wkv"]
    blocks += [columns_unit(i["L0_xattn_Wq"]), columns_unit(wkv[:, :512][:, halves]),
               rows_unit(wkv[:, 512:]), rows_unit(i["L0_xattn_Wo"])]
    d["ctx_rows"] = i["ctx_1024"].reshape(8, 4, 128, 512).transpose(0, 2, 1, 3)
    for name in ("gamma_x", "beta_x", "gamma_l", "beta_l"):
        d[name] = per_partition(i["L0_xattn_" + name])
    freq = (1.0 / np.float32(10000.0) ** (np.arange(0, 64, 2, dtype=np.float32) / np.float32(64))).astype(np.float32)
    angle = np.tile(freq[:, None] * np.arange(512, dtype=np.float32)[None, :], (4, 1))
    d["rope_cos"], d["rope_sin"] = np.cos(angle), np.sin(angle)
    w_in, w_bc = i["L0_attn_W_in"], i["L0_attn_W_bc"]
    bc = w_bc.reshape(8, 4, 4, 32, 8, 128).transpose(0, 5, 2, 4, 1, 3).reshape(8, 128, 2, 4, 512)
    blocks += [columns_unit(w_in[1024:2048].T), columns_unit(w_in[:1024].T),
               bc.transpose(0, 2, 1, 3, 4).reshape(16, 128, 4, 512), rows_unit(i["L0_attn_W_out"].T)]
    params = w_in[2048:].reshape(32, 2, 512).transpose(1, 0, 2).reshape(64, 512)
    d["w_params"] = np.concatenate([params, params]).T.reshape(4, 128, 128).transpose(1, 0, 2)
    d["conv_w"] = i["L0_attn_dw_weight"].reshape(8, 128, 4).transpose(1, 0, 2)
    d["conv_b"], d["skip"] = per_partition(i["L0_attn_dw_bias"]), per_partition(i["L0_attn_skip"])
    d["a_log"] = i["L0_attn_A_log"].reshape(8, 4, 32).transpose(1, 2, 0).reshape(128, 8)
    d["dt_bias"] = i["L0_attn_dt_bias"][:, None]
    select = np.zeros((128, 16, 128), np.float32)
    for n in range(16):
        for p in range(128):
            select[32 * (n // 8) + 4 * (n % 8) + p // 32, n, p] = 1
    d["select"] = select
    d["causal"] = ((at[:, None] // 64 == at[None, :] // 64) & (at[:, None] <= at[None, :])).astype(np.float32)
    pick = (at[:, None] // 32 == np.arange(32)[None, :]).astype(np.float32)
    d["pick"], d["spread"] = pick, (at[None, :] // 32 == at[:, None] % 32).astype(np.float32)
    d["ffn_w1"] = i["L0_ffn_w1"].T.reshape(4, 128, 2048).transpose(1, 0, 2).reshape(128, 8192)
    d["ffn_w2"] = i["L0_ffn_w2"].T.reshape(16, 128, 512).transpose(1, 0, 2).reshape(128, 8192)
    d["ffn_conv_w"] = i["L0_ffn_conv_w"].reshape(16, 128, 3).transpose(1, 0, 2)
    d["ffn_conv_b"] = per_partition(i["L0_ffn_conv_b"])
    d["ones"] = np.ones((128, 128), np.float32)
    wkv = i["L1_xattn_Wkv"]
    blocks += [columns_unit(i["L1_xattn_Wq"].T), columns_unit(wkv[:512].T), rows_unit(wkv[512:].T),
               rows_unit(i["L1_xattn_Wout"].T)]
    d["ctx_columns"] = i["ctx_1024"].reshape(8, 512, 4, 128).transpose(0, 3, 2, 1)
    d["ca_bias"] = np.broadcast_to(i["L1_xattn_bout"], (128, 512))
    w, b = i["L1_attn_qkv_w"], i["L1_attn_qkv_b"]
    blocks += [columns_unit(w[:, :512]), columns_unit(w[:, 512:1024]), rows_unit(w[:, 1024:]), rows_unit(i["L1_attn_out_w"])]
    d["qk_bias"] = per_partition(b[:1024])
    d["v_bias"], d["li_bias"] = np.broadcast_to(b[1024:], (128, 512)), np.broadcast_to(i["L1_attn_out_b"], (128, 512))
    d["proj"] = i["L1_attn_proj"].reshape(4, 4, 32, 64).transpose(1, 2, 0, 3)
    w1 = i["L1_ffn_dense_1_w"].reshape(8, 4, 2, 128, 2, 4, 128).transpose(0, 1, 6, 2, 4, 5, 3).reshape(8, 4, 128, 4, 512)
    w2 = i["L1_ffn_dense_2_w"].transpose(0, 2, 1).reshape(8, 2, 4, 128, 512).transpose(0, 1, 3, 2, 4)
    blocks.append(np.concatenate([w1, w2], axis=1).reshape(48, 128, 4, 512))
    d["expert_b1"] = i["L1_ffn_dense_1_b"].reshape(8, 8, 128, 2).transpose(2, 0, 1, 3)
    d["expert_b2"] = i["L1_ffn_dense_2_b"]
    d["gate_w"] = i["L1_ffn_gate_w"].reshape(4, 128, 8).transpose(1, 0, 2)
    e = np.arange(8)
    d["before"] = np.broadcast_to((e[None, :] < e[:, None]).astype(np.float32), (128, 8, 8))
    d["weights"] = np.concatenate(blocks)
    return {k: np.ascontiguousarray(v) for k, v in d.items()}


def kernel(**inputs):
    import concourse.bacc as _bacc
    from concourse.bass_utils import run_bass_kernel_spmd as _run

    nc = _bacc.Bacc("TRN2", target_bir_lowering=False, num_devices=1)
    arrays = lay_out(inputs)
    d = {name: nc.dram_tensor("in_" + name, a.shape, mybir.dt.from_np(a.dtype), kind="ExternalInput").ap()
         for name, a in arrays.items()}
    out = nc.dram_tensor("out_x", (P, TT, D), F32, kind="ExternalOutput").ap()
    program(nc, d, out, STAGES)
    r = _run(nc, [{"in_" + name: a for name, a in arrays.items()}], core_ids=[0])
    return np.ascontiguousarray(r.results[0]["out_x"].transpose(1, 0, 2).reshape(B, L, D))
```
